# Optimizing a Trainium2 kernel written in Bass

```python
import numpy as np
import jax
import jax.numpy as jnp

def _softmax(x, axis=-1):
    return jax.nn.softmax(x, axis=axis)

def _gelu(x):
    return jax.nn.gelu(x, approximate=True)

def _silu(x):
    return jax.nn.silu(x)

def _sigmoid(x):
    return jax.nn.sigmoid(x)

def _layernorm(x, axis=-1, eps=1e-05):
    m = jnp.mean(x, axis=axis, keepdims=True)
    v = jnp.var(x, axis=axis, keepdims=True)
    return (x - m) / jnp.sqrt(v + eps)

def _scatter_add(tgt, idx, src, axis=0):
    return tgt.at[idx].add(src)

def _segment_sum(src, seg, n):
    return jax.ops.segment_sum(src, seg, n)
kernel_name = 'mk_flamingo_gated_d4_seqx_r4_3f967d'

def setup_inputs(seed: int=0):
    np.random.seed(seed)
    _w = jnp.asarray

    def _rec_inputs():
        import jax
        import jax.numpy as jnp
        _rk = jax.random.key(seed)
        x = 7.22e-05 + 1 * jax.random.normal(jax.random.fold_in(_rk, 1), (32, 112, 256), jnp.float32)
        _lenS = 112 - jax.random.randint(jax.random.fold_in(_rk, 7), (32,), 0, max(1, 112 // 4) + 1, jnp.int32)
        _lenS2 = 375 - jax.random.randint(jax.random.fold_in(_rk, 8), (32,), 0, max(1, 375 // 4) + 1, jnp.int32)
        _ctx_1024P = jax.random.normal(jax.random.fold_in(_rk, 11), (32, 16, 256), jnp.float32)
        _ctx_1024c = jax.random.dirichlet(jax.random.fold_in(_rk, 511), 0.3 * jnp.ones((16,), jnp.float32), (32, 375))
        _ctx_1024t = jnp.einsum('bsk,bkd->bsd', _ctx_1024c, _ctx_1024P)
        _ctx_1024t = _ctx_1024t * jax.lax.rsqrt(jnp.mean(jnp.square(_ctx_1024t)) + 1e-12) * 0.953939
        ctx_1024 = 4.13588e-05 + 0.999923 * (_ctx_1024t + 0.3 * jax.random.normal(jax.random.fold_in(_rk, 611), (32, 375, 256), jnp.float32))
        _validS = jnp.arange(112)[None, :] < _lenS[:, None]
        _validS2 = jnp.arange(375)[None, :] < _lenS2[:, None]
        _causal = jnp.tril(jnp.ones((112, 112), dtype=bool))
        mask_Bx1xS2_ik0 = jnp.where(jnp.broadcast_to(_validS2[:, None, :], (32, 1, 375)), 0, 1).astype(jnp.int32)
        mask_BxS2_ik1 = jnp.where(jnp.broadcast_to(_validS2[:, :], (32, 375)), 1, 0).astype(jnp.int32)
        _g = jax.random.normal(jax.random.fold_in(_rk, 9001), (2, 4), jnp.float32)
        _g = jnp.sign(_g) * jnp.maximum(jnp.abs(_g), 1.0) + (_g == 0) * 1.0
        g_xattn = _g[0]
        g_ffn = _g[1]
        return (x, ctx_1024, mask_Bx1xS2_ik0, mask_BxS2_ik1, g_xattn, g_ffn)
    x, ctx_1024, mask_Bx1xS2_ik0, mask_BxS2_ik1, g_xattn, g_ffn = _rec_inputs()

    def _L0_xattn_setup():
        import jax, jax.numpy as jnp
        import numpy as np
        D_MODEL = 256
        NEG_BIG = -1000000000.0
        key = jax.random.key(seed)
        kq, kk, kv, km = jax.random.split(key, 4)
        B, S, D = (4, 512, D_MODEL)
        q = jax.random.normal(kq, (B, S, D), dtype=jnp.float32)
        k = jax.random.normal(kk, (B, S, D), dtype=jnp.float32)
        v = jax.random.normal(kv, (B, S, D), dtype=jnp.float32)
        mask = jax.random.randint(km, (B, 1, S), 0, 2, dtype=jnp.int32)
        return {'q': q, 'k': k, 'v': v, 'mask': mask}
    _L0_xattn_all = _L0_xattn_setup()
    _L0_xattn_in = {k: v for k, v in _L0_xattn_all.items() if k in ()}
    del _L0_xattn_all

    def _L0_ffn_setup():
        import jax, jax.numpy as jnp
        import numpy as np
        DIM = 256
        HIDDEN = 768
        SCALE = 1.0 / 127.0

        def _dequant(w_int, dtype):
            return w_int.astype(dtype) * jnp.asarray(SCALE, dtype)
        key = jax.random.key(seed)
        k_x, k_g, k_u, k_d = jax.random.split(key, 4)
        x = jax.random.normal(k_x, (4, 512, DIM), dtype=jnp.float32)
        w_gate = jax.random.randint(k_g, (HIDDEN, DIM), -127, 128, dtype=jnp.int32)
        w_up = jax.random.randint(k_u, (HIDDEN, DIM), -127, 128, dtype=jnp.int32)
        w_down = jax.random.randint(k_d, (DIM, HIDDEN), -127, 128, dtype=jnp.int32)
        return {'x': x, 'w_gate': w_gate, 'w_up': w_up, 'w_down': w_down}
    _L0_ffn_all = _L0_ffn_setup()
    _L0_ffn_in = {k: v for k, v in _L0_ffn_all.items() if k in ('w_gate', 'w_up', 'w_down')}
    del _L0_ffn_all

    def _L1_xattn_setup():
        import jax, jax.numpy as jnp
        import numpy as np
        D_MODEL = 256
        B, S = (4, 512)
        key = jax.random.key(seed)
        ks = jax.random.split(key, 8)
        scale = 0.02
        return {'q': jax.random.normal(ks[0], (B, S, D_MODEL), jnp.float32), 'k': jax.random.normal(ks[1], (B, S, D_MODEL), jnp.float32), 'v': jax.random.normal(ks[2], (B, S, D_MODEL), jnp.float32), 'Wq': jax.random.normal(ks[3], (D_MODEL, D_MODEL), jnp.float32) * scale, 'bq': jnp.zeros((D_MODEL,), jnp.float32), 'Wk': jax.random.normal(ks[4], (D_MODEL, D_MODEL), jnp.float32) * scale, 'bk': jnp.zeros((D_MODEL,), jnp.float32), 'Wv': jax.random.normal(ks[5], (D_MODEL, D_MODEL), jnp.float32) * scale, 'bv': jnp.zeros((D_MODEL,), jnp.float32), 'Wo': jax.random.normal(ks[6], (D_MODEL, D_MODEL), jnp.float32) * scale, 'bo': jnp.zeros((D_MODEL,), jnp.float32)}
    _L1_xattn_all = _L1_xattn_setup()
    _L1_xattn_in = {k: v for k, v in _L1_xattn_all.items() if k in ('Wq', 'bq', 'Wk', 'bk', 'Wv', 'bv', 'Wo', 'bo')}
    del _L1_xattn_all

    def _L1_ffn_setup():
        import jax, jax.numpy as jnp
        import numpy as np
        LN_EPS = 1e-05

        def layernorm(x, g, b):
            mu = jnp.mean(x, axis=-1, keepdims=True)
            var = jnp.mean((x - mu) ** 2, axis=-1, keepdims=True)
            return (x - mu) * jax.lax.rsqrt(var + LN_EPS) * g + b

        def act_quant_fake(x):
            scale = 127.0 / jnp.clip(jnp.max(jnp.abs(x), axis=-1, keepdims=True), 1e-05)
            return jnp.clip(jnp.round(x * scale), -128.0, 127.0) / scale

        def weight_quant_fake(w):
            scale = 1.0 / jnp.clip(jnp.mean(jnp.abs(w)), 1e-05)
            return jnp.clip(jnp.round(w * scale), -1.0, 1.0) / scale

        def bitlinear(x, w, b):
            dqx = act_quant_fake(x)
            dqw = weight_quant_fake(w)
            return jnp.einsum('btd,hd->bth', dqx, dqw) + b
        key = jax.random.key(seed)
        ks = jax.random.split(key, 5)
        B, T, D, H = (8, 1024, 256, 1024)
        return {'x': jax.random.normal(ks[0], (B, T, D), dtype=jnp.float32), 'ln1_g': jnp.ones((D,), jnp.float32), 'ln1_b': jnp.zeros((D,), jnp.float32), 'w1': jax.random.normal(ks[1], (H, D), dtype=jnp.float32) * (1.0 / np.sqrt(D)), 'b1': jax.random.normal(ks[2], (H,), dtype=jnp.float32) * 0.02, 'ln2_g': jnp.ones((H,), jnp.float32), 'ln2_b': jnp.zeros((H,), jnp.float32), 'w2': jax.random.normal(ks[3], (D, H), dtype=jnp.float32) * (1.0 / np.sqrt(H)), 'b2': jax.random.normal(ks[4], (D,), jnp.float32) * 0.02}
    _L1_ffn_all = _L1_ffn_setup()
    _L1_ffn_in = {k: v for k, v in _L1_ffn_all.items() if k in ('ln1_g', 'ln1_b', 'w1', 'b1', 'ln2_g', 'ln2_b', 'w2', 'b2')}
    del _L1_ffn_all

    def _L2_xattn_setup():
        import jax, jax.numpy as jnp
        import numpy as np
        N, L, S, D = (8, 512, 512, 256)
        key = jax.random.key(seed)
        k1, k2, k3, k4, k5 = jax.random.split(key, 5)
        return {'key': jax.random.normal(k1, (N, S, D), dtype=jnp.float32), 'query': jax.random.normal(k2, (N, L, D), dtype=jnp.float32), 'value': jax.random.normal(k3, (N, S, D), dtype=jnp.float32), 'W': jax.random.normal(k4, (D, D), dtype=jnp.float32) / np.sqrt(D), 'b': jax.random.normal(k5, (D,), dtype=jnp.float32)}
    _L2_xattn_all = _L2_xattn_setup()
    _L2_xattn_in = {k: v for k, v in _L2_xattn_all.items() if k in ('W', 'b')}
    del _L2_xattn_all

    def _L2_ffn_setup():
        import jax, jax.numpy as jnp
        import numpy as np
        B, T, N = (2, 512, 256)
        H = 16
        E = 8
        K = 2
        FF = 4 * N
        EPS = 1e-05
        SCALE = 1.0

        def _layernorm(x, scale, bias):
            mu = x.mean(-1, keepdims=True)
            var = ((x - mu) ** 2).mean(-1, keepdims=True)
            return (x - mu) * jax.lax.rsqrt(var + EPS) * scale + bias

        def _attention(x, w_qkv, b_qkv, w_proj, b_proj):
            b, t, n = x.shape
            qkv = x @ w_qkv + b_qkv
            q, k, v = jnp.split(qkv, 3, axis=2)
            hd = n // H
            q = q.reshape(b, t, H, hd).transpose(0, 2, 1, 3)
            k = k.reshape(b, t, H, hd).transpose(0, 2, 1, 3)
            v = v.reshape(b, t, H, hd).transpose(0, 2, 1, 3)
            att = jnp.einsum('bhqd,bhkd->bhqk', q, k) / hd ** 0.5
            mask = jnp.tril(jnp.ones((1, 1, t, t), bool))
            att = jnp.where(mask, att, jnp.finfo(jnp.float32).min)
            att = jax.nn.softmax(att, axis=-1)
            y = jnp.einsum('bhqk,bhkd->bhqd', att, v)
            y = y.transpose(0, 2, 1, 3).reshape(b, t, n)
            return y @ w_proj + b_proj

        def _moe(x, w_gate, b_gate, w_fc, b_fc, w_fcproj, b_fcproj):
            b, t, n = x.shape
            xf = x.reshape(-1, n)
            bt = xf.shape[0]
            logits = xf @ w_gate + b_gate
            probs = jax.nn.softmax(logits, axis=-1)
            top_p, top_i = jax.lax.top_k(probs, K)
            out = jnp.zeros((bt, n), xf.dtype)
            expert_mask = jnp.transpose(jax.nn.one_hot(top_i, E), (2, 1, 0))
            rows = jnp.arange(bt)
            for e in range(E):
                active = expert_mask[e]
                mask = active.any(axis=0)
                cumsum = jnp.cumsum(mask) - 1
                indices = jnp.where(mask, cumsum, -1)
                sel = jnp.where(mask[:, None], xf, 0.0)
                h = jax.nn.gelu(sel @ w_fc[e] + b_fc[e], approximate=True)
                eo = h @ w_fcproj[e] + b_fcproj[e]
                rp = jnp.where(mask[:, None], top_p[rows, jnp.argmax(active, axis=0)][:, None], 0.0)
                out = out.at[indices].add(eo * rp)
            return out.reshape(b, t, n)
        key = jax.random.key(seed)
        ks = jax.random.split(key, 12)
        s = lambda fan_in: 1.0 / np.sqrt(fan_in)
        return {'x': jax.random.normal(ks[0], (B, T, N), jnp.float32), 'ln1_scale': jnp.ones((N,), jnp.float32), 'ln1_bias': jnp.zeros((N,), jnp.float32), 'w_qkv': jax.random.normal(ks[1], (N, 3 * N), jnp.float32) * s(N), 'b_qkv': jnp.zeros((3 * N,), jnp.float32), 'w_attnproj': jax.random.normal(ks[2], (N, N), jnp.float32) * s(N), 'b_attnproj': jnp.zeros((N,), jnp.float32), 'ln2_scale': jnp.ones((N,), jnp.float32), 'ln2_bias': jnp.zeros((N,), jnp.float32), 'w_gate': jax.random.normal(ks[3], (N, E), jnp.float32) * s(N), 'b_gate': jnp.zeros((E,), jnp.float32), 'w_fc': jax.random.normal(ks[4], (E, N, FF), jnp.float32) * s(N), 'b_fc': jnp.zeros((E, FF), jnp.float32), 'w_fcproj': jax.random.normal(ks[5], (E, FF, N), jnp.float32) * s(FF), 'b_fcproj': jnp.zeros((E, N), jnp.float32)}
    _L2_ffn_all = _L2_ffn_setup()
    _L2_ffn_in = {k: v for k, v in _L2_ffn_all.items() if k in ('ln1_scale', 'ln1_bias', 'w_qkv', 'b_qkv', 'w_attnproj', 'b_attnproj', 'ln2_scale', 'ln2_bias', 'w_gate', 'b_gate', 'w_fc', 'b_fc', 'w_fcproj', 'b_fcproj')}
    del _L2_ffn_all

    def _L3_xattn_setup():
        import jax, jax.numpy as jnp
        import numpy as np
        B, S, D = (8, 512, 256)
        key = jax.random.key(seed)
        ks = jax.random.split(key, 10)
        scale = 1.0 / np.sqrt(D)
        return {'query': jax.random.normal(ks[0], (B, S, D), jnp.float32), 'key': jax.random.normal(ks[1], (B, S, D), jnp.float32), 'value': jax.random.normal(ks[2], (B, S, D), jnp.float32), 'mask': jax.random.randint(ks[3], (B, S), 0, 2, jnp.int32), 'Wq': jax.random.uniform(ks[4], (D, D), jnp.float32, -scale, scale), 'bq': jax.random.uniform(ks[5], (D,), jnp.float32, -scale, scale), 'Wk': jax.random.uniform(ks[6], (D, D), jnp.float32, -scale, scale), 'bk': jax.random.uniform(ks[7], (D,), jnp.float32, -scale, scale), 'Wv': jax.random.uniform(ks[8], (D, D), jnp.float32, -scale, scale), 'bv': jax.random.uniform(ks[9], (D,), jnp.float32, -scale, scale)}
    _L3_xattn_all = _L3_xattn_setup()
    _L3_xattn_in = {k: v for k, v in _L3_xattn_all.items() if k in ('Wq', 'bq', 'Wk', 'bk', 'Wv', 'bv')}
    del _L3_xattn_all

    def _L3_ffn_setup():
        import jax, jax.numpy as jnp
        import numpy as np
        N_EXPERTS = 8
        CAP_FACTOR = 1.25
        BATCH, SEQ, DMODEL, DFF = (4, 512, 256, 1024)
        key = jax.random.key(seed)
        k0, k1, k2, k3 = jax.random.split(key, 4)
        x = jax.random.normal(k0, (BATCH, SEQ, DMODEL), dtype=jnp.float32)
        Wr = jax.random.normal(k1, (DMODEL, N_EXPERTS), dtype=jnp.float32) * 0.02
        W1 = jax.random.normal(k2, (N_EXPERTS, DMODEL, DFF), dtype=jnp.float32) * 0.02
        W2 = jax.random.normal(k3, (N_EXPERTS, DFF, DMODEL), dtype=jnp.float32) * 0.02
        return {'x': x, 'Wr': Wr, 'W1': W1, 'W2': W2}
    _L3_ffn_all = _L3_ffn_setup()
    _L3_ffn_in = {k: v for k, v in _L3_ffn_all.items() if k in ('Wr', 'W1', 'W2')}
    del _L3_ffn_all
    return {'x': x, 'ctx_1024': ctx_1024, 'mask_Bx1xS2_ik0': mask_Bx1xS2_ik0, 'mask_BxS2_ik1': mask_BxS2_ik1, 'g_xattn': g_xattn, 'g_ffn': g_ffn, 'L0_ffn_w_gate': _L0_ffn_in['w_gate'], 'L0_ffn_w_up': _L0_ffn_in['w_up'], 'L0_ffn_w_down': _L0_ffn_in['w_down'], 'L1_xattn_Wq': _L1_xattn_in['Wq'], 'L1_xattn_bq': _L1_xattn_in['bq'], 'L1_xattn_Wk': _L1_xattn_in['Wk'], 'L1_xattn_bk': _L1_xattn_in['bk'], 'L1_xattn_Wv': _L1_xattn_in['Wv'], 'L1_xattn_bv': _L1_xattn_in['bv'], 'L1_xattn_Wo': _L1_xattn_in['Wo'], 'L1_xattn_bo': _L1_xattn_in['bo'], 'L1_ffn_ln1_g': _L1_ffn_in['ln1_g'], 'L1_ffn_ln1_b': _L1_ffn_in['ln1_b'], 'L1_ffn_w1': _L1_ffn_in['w1'], 'L1_ffn_b1': _L1_ffn_in['b1'], 'L1_ffn_ln2_g': _L1_ffn_in['ln2_g'], 'L1_ffn_ln2_b': _L1_ffn_in['ln2_b'], 'L1_ffn_w2': _L1_ffn_in['w2'], 'L1_ffn_b2': _L1_ffn_in['b2'], 'L2_xattn_W': _L2_xattn_in['W'], 'L2_xattn_b': _L2_xattn_in['b'], 'L2_ffn_ln1_scale': _L2_ffn_in['ln1_scale'], 'L2_ffn_ln1_bias': _L2_ffn_in['ln1_bias'], 'L2_ffn_w_qkv': _L2_ffn_in['w_qkv'], 'L2_ffn_b_qkv': _L2_ffn_in['b_qkv'], 'L2_ffn_w_attnproj': _L2_ffn_in['w_attnproj'], 'L2_ffn_b_attnproj': _L2_ffn_in['b_attnproj'], 'L2_ffn_ln2_scale': _L2_ffn_in['ln2_scale'], 'L2_ffn_ln2_bias': _L2_ffn_in['ln2_bias'], 'L2_ffn_w_gate': _L2_ffn_in['w_gate'], 'L2_ffn_b_gate': _L2_ffn_in['b_gate'], 'L2_ffn_w_fc': _L2_ffn_in['w_fc'], 'L2_ffn_b_fc': _L2_ffn_in['b_fc'], 'L2_ffn_w_fcproj': _L2_ffn_in['w_fcproj'], 'L2_ffn_b_fcproj': _L2_ffn_in['b_fcproj'], 'L3_xattn_Wq': _L3_xattn_in['Wq'], 'L3_xattn_bq': _L3_xattn_in['bq'], 'L3_xattn_Wk': _L3_xattn_in['Wk'], 'L3_xattn_bk': _L3_xattn_in['bk'], 'L3_xattn_Wv': _L3_xattn_in['Wv'], 'L3_xattn_bv': _L3_xattn_in['bv'], 'L3_ffn_Wr': _L3_ffn_in['Wr'], 'L3_ffn_W1': _L3_ffn_in['W1'], 'L3_ffn_W2': _L3_ffn_in['W2']}

def reference(x, ctx_1024, mask_Bx1xS2_ik0, mask_BxS2_ik1, g_xattn, g_ffn, L0_ffn_w_gate, L0_ffn_w_up, L0_ffn_w_down, L1_xattn_Wq, L1_xattn_bq, L1_xattn_Wk, L1_xattn_bk, L1_xattn_Wv, L1_xattn_bv, L1_xattn_Wo, L1_xattn_bo, L1_ffn_ln1_g, L1_ffn_ln1_b, L1_ffn_w1, L1_ffn_b1, L1_ffn_ln2_g, L1_ffn_ln2_b, L1_ffn_w2, L1_ffn_b2, L2_xattn_W, L2_xattn_b, L2_ffn_ln1_scale, L2_ffn_ln1_bias, L2_ffn_w_qkv, L2_ffn_b_qkv, L2_ffn_w_attnproj, L2_ffn_b_attnproj, L2_ffn_ln2_scale, L2_ffn_ln2_bias, L2_ffn_w_gate, L2_ffn_b_gate, L2_ffn_w_fc, L2_ffn_b_fc, L2_ffn_w_fcproj, L2_ffn_b_fcproj, L3_xattn_Wq, L3_xattn_bq, L3_xattn_Wk, L3_xattn_bk, L3_xattn_Wv, L3_xattn_bv, L3_ffn_Wr, L3_ffn_W1, L3_ffn_W2):
    import jax
    import jax.numpy as jnp

    def _L0_xattn_ref(q, k, v, mask):
        import jax, jax.numpy as jnp
        import numpy as np
        D_MODEL = 256
        NEG_BIG = -1000000000.0
        scale = jnp.asarray(D_MODEL, q.dtype) ** (-0.5)
        logits = jnp.einsum('bqd,bkd->bqk', q, k) * scale
        logits = logits + mask.astype(q.dtype) * NEG_BIG
        weights = jax.nn.softmax(logits, axis=-1)
        return jnp.einsum('bqk,bkd->bqd', weights, v)

    def _L0_ffn_ref(x, w_gate, w_up, w_down):
        import jax, jax.numpy as jnp
        import numpy as np
        DIM = 256
        HIDDEN = 768
        SCALE = 1.0 / 127.0

        def _dequant(w_int, dtype):
            return w_int.astype(dtype) * jnp.asarray(SCALE, dtype)
        wg = _dequant(w_gate, x.dtype)
        wu = _dequant(w_up, x.dtype)
        wd = _dequant(w_down, x.dtype)
        gate = jnp.einsum('bsd,hd->bsh', x, wg)
        up = jnp.einsum('bsd,hd->bsh', x, wu)
        h = jax.nn.silu(gate) * up
        return jnp.einsum('bsh,dh->bsd', h, wd)

    def _L1_xattn_ref(q, k, v, Wq, bq, Wk, bk, Wv, bv, Wo, bo):
        import jax, jax.numpy as jnp
        import numpy as np
        D_MODEL = 256
        B, S = (4, 512)
        qp = q @ Wq + bq
        kp = k @ Wk + bk
        vp = v @ Wv + bv
        d_k = qp.shape[-1]
        scores = jnp.einsum('bqd,bkd->bqk', qp, kp) / jnp.sqrt(jnp.asarray(d_k, qp.dtype))
        attn = jax.nn.softmax(scores, axis=-1)
        attn_out = jnp.einsum('bqk,bkd->bqd', attn, vp)
        b = attn_out.shape[0]
        atten_out = attn_out.transpose(0, 2, 1).reshape(b, -1, D_MODEL)
        out = atten_out @ Wo + bo
        return out

    def _L1_ffn_ref(x, ln1_g, ln1_b, w1, b1, ln2_g, ln2_b, w2, b2):
        import jax, jax.numpy as jnp
        import numpy as np
        LN_EPS = 1e-05

        def layernorm(x, g, b):
            mu = jnp.mean(x, axis=-1, keepdims=True)
            var = jnp.mean((x - mu) ** 2, axis=-1, keepdims=True)
            return (x - mu) * jax.lax.rsqrt(var + LN_EPS) * g + b

        def act_quant_fake(x):
            scale = 127.0 / jnp.clip(jnp.max(jnp.abs(x), axis=-1, keepdims=True), 1e-05)
            return jnp.clip(jnp.round(x * scale), -128.0, 127.0) / scale

        def weight_quant_fake(w):
            scale = 1.0 / jnp.clip(jnp.mean(jnp.abs(w)), 1e-05)
            return jnp.clip(jnp.round(w * scale), -1.0, 1.0) / scale

        def bitlinear(x, w, b):
            dqx = act_quant_fake(x)
            dqw = weight_quant_fake(w)
            return jnp.einsum('btd,hd->bth', dqx, dqw) + b
        h = layernorm(x, ln1_g, ln1_b)
        h = bitlinear(h, w1, b1)
        h = jax.nn.gelu(h, approximate=False)
        h = layernorm(h, ln2_g, ln2_b)
        h = bitlinear(h, w2, b2)
        return h

    def _L2_xattn_ref(key, query, value, W, b):
        import jax, jax.numpy as jnp
        import numpy as np
        N, L, S, D = (8, 512, 512, 256)
        q_proj = jnp.einsum('nlq,kq->nlk', query, W) + b
        score = jnp.einsum('nlk,nsk->nls', q_proj, key)
        score = jax.nn.softmax(score, axis=2)
        out = jnp.einsum('nls,nsd->nld', score, value)
        return out

    def _L2_ffn_ref(x, ln1_scale, ln1_bias, w_qkv, b_qkv, w_attnproj, b_attnproj, ln2_scale, ln2_bias, w_gate, b_gate, w_fc, b_fc, w_fcproj, b_fcproj):
        import jax, jax.numpy as jnp
        import numpy as np
        B, T, N = (2, 512, 256)
        H = 16
        E = 8
        K = 2
        FF = 4 * N
        EPS = 1e-05
        SCALE = 1.0

        def _layernorm(x, scale, bias):
            mu = x.mean(-1, keepdims=True)
            var = ((x - mu) ** 2).mean(-1, keepdims=True)
            return (x - mu) * jax.lax.rsqrt(var + EPS) * scale + bias

        def _attention(x, w_qkv, b_qkv, w_proj, b_proj):
            b, t, n = x.shape
            qkv = x @ w_qkv + b_qkv
            q, k, v = jnp.split(qkv, 3, axis=2)
            hd = n // H
            q = q.reshape(b, t, H, hd).transpose(0, 2, 1, 3)
            k = k.reshape(b, t, H, hd).transpose(0, 2, 1, 3)
            v = v.reshape(b, t, H, hd).transpose(0, 2, 1, 3)
            att = jnp.einsum('bhqd,bhkd->bhqk', q, k) / hd ** 0.5
            mask = jnp.tril(jnp.ones((1, 1, t, t), bool))
            att = jnp.where(mask, att, jnp.finfo(jnp.float32).min)
            att = jax.nn.softmax(att, axis=-1)
            y = jnp.einsum('bhqk,bhkd->bhqd', att, v)
            y = y.transpose(0, 2, 1, 3).reshape(b, t, n)
            return y @ w_proj + b_proj

        def _moe(x, w_gate, b_gate, w_fc, b_fc, w_fcproj, b_fcproj):
            b, t, n = x.shape
            xf = x.reshape(-1, n)
            bt = xf.shape[0]
            logits = xf @ w_gate + b_gate
            probs = jax.nn.softmax(logits, axis=-1)
            top_p, top_i = jax.lax.top_k(probs, K)
            out = jnp.zeros((bt, n), xf.dtype)
            expert_mask = jnp.transpose(jax.nn.one_hot(top_i, E), (2, 1, 0))
            rows = jnp.arange(bt)
            for e in range(E):
                active = expert_mask[e]
                mask = active.any(axis=0)
                cumsum = jnp.cumsum(mask) - 1
                indices = jnp.where(mask, cumsum, -1)
                sel = jnp.where(mask[:, None], xf, 0.0)
                h = jax.nn.gelu(sel @ w_fc[e] + b_fc[e], approximate=True)
                eo = h @ w_fcproj[e] + b_fcproj[e]
                rp = jnp.where(mask[:, None], top_p[rows, jnp.argmax(active, axis=0)][:, None], 0.0)
                out = out.at[indices].add(eo * rp)
            return out.reshape(b, t, n)
        x = x + SCALE * _attention(_layernorm(x, ln1_scale, ln1_bias), w_qkv, b_qkv, w_attnproj, b_attnproj)
        x = x + SCALE * _moe(_layernorm(x, ln2_scale, ln2_bias), w_gate, b_gate, w_fc, b_fc, w_fcproj, b_fcproj)
        return x

    def _L3_xattn_ref(query, key, value, mask, Wq, bq, Wk, bk, Wv, bv):
        import jax, jax.numpy as jnp
        import numpy as np
        B, S, D = (8, 512, 256)
        Q = jnp.einsum('bsd,od->bso', query, Wq) + bq
        K = jnp.einsum('bsd,od->bso', key, Wk) + bk
        V = jnp.einsum('bsd,od->bso', value, Wv) + bv
        d_k = K.shape[-1]
        scores = jnp.einsum('bqd,bkd->bqk', Q, K) / jnp.sqrt(jnp.float32(d_k))
        m = (mask != 0)[:, None, :]
        scores = jnp.where(m, scores, -jnp.inf)
        weights = jax.nn.softmax(scores, axis=-1)
        out = jnp.einsum('bqk,bkv->bqv', weights, V)
        return out

    def _L3_ffn_ref(x, Wr, W1, W2):
        import jax, jax.numpy as jnp
        import numpy as np
        N_EXPERTS = 8
        CAP_FACTOR = 1.25
        BATCH, SEQ, DMODEL, DFF = (4, 512, 256, 1024)
        B, S, D = x.shape
        E = W1.shape[0]
        cap = int(CAP_FACTOR * B * S / E)
        t = x.reshape(-1, D)
        probs = jax.nn.softmax(t @ Wr, axis=-1)
        idx = jnp.argmax(probs, axis=-1)
        pmax = jnp.max(probs, axis=-1)
        onehot = jax.nn.one_hot(idx, E, dtype=jnp.int32)
        pos = jnp.sum(jnp.cumsum(onehot, axis=0) * onehot, axis=-1) - 1
        kept = pos < cap
        flat = idx * cap + jnp.minimum(pos, cap - 1)
        disp = jnp.zeros((E * cap, D), t.dtype).at[flat].add(t * kept[:, None].astype(t.dtype))
        ein = disp.reshape(E, cap, D)
        h = jax.nn.relu(jnp.einsum('ecd,edf->ecf', ein, W1))
        eout = jnp.einsum('ecf,efd->ecd', h, W2).reshape(E * cap, D)
        comb = jnp.where(kept[:, None], eout[flat], t)
        factor = jnp.where(kept, pmax, jnp.ones_like(pmax))
        out = (comb * factor[:, None]).reshape(B, S, D)
        return out
    x = x + jnp.tanh(g_xattn[0]) * _L0_xattn_ref(_layernorm(x, axis=-1), ctx_1024, ctx_1024, mask_Bx1xS2_ik0)
    x = x + jnp.tanh(g_ffn[0]) * _L0_ffn_ref(_layernorm(x, axis=-1), L0_ffn_w_gate, L0_ffn_w_up, L0_ffn_w_down)
    x = x + jnp.tanh(g_xattn[1]) * _L1_xattn_ref(_layernorm(x, axis=-1), ctx_1024, ctx_1024, L1_xattn_Wq, L1_xattn_bq, L1_xattn_Wk, L1_xattn_bk, L1_xattn_Wv, L1_xattn_bv, L1_xattn_Wo, L1_xattn_bo)
    x = x + jnp.tanh(g_ffn[1]) * _L1_ffn_ref(_layernorm(x, axis=-1), L1_ffn_ln1_g, L1_ffn_ln1_b, L1_ffn_w1, L1_ffn_b1, L1_ffn_ln2_g, L1_ffn_ln2_b, L1_ffn_w2, L1_ffn_b2)
    x = x + jnp.tanh(g_xattn[2]) * _L2_xattn_ref(ctx_1024, _layernorm(x, axis=-1), ctx_1024, L2_xattn_W, L2_xattn_b)
    x = x + jnp.tanh(g_ffn[2]) * _L2_ffn_ref(_layernorm(x, axis=-1), L2_ffn_ln1_scale, L2_ffn_ln1_bias, L2_ffn_w_qkv, L2_ffn_b_qkv, L2_ffn_w_attnproj, L2_ffn_b_attnproj, L2_ffn_ln2_scale, L2_ffn_ln2_bias, L2_ffn_w_gate, L2_ffn_b_gate, L2_ffn_w_fc, L2_ffn_b_fc, L2_ffn_w_fcproj, L2_ffn_b_fcproj)
    x = x + jnp.tanh(g_xattn[3]) * _L3_xattn_ref(_layernorm(x, axis=-1), ctx_1024, ctx_1024, mask_BxS2_ik1, L3_xattn_Wq, L3_xattn_bq, L3_xattn_Wk, L3_xattn_bk, L3_xattn_Wv, L3_xattn_bv)
    x = x + jnp.tanh(g_ffn[3]) * _L3_ffn_ref(_layernorm(x, axis=-1), L3_ffn_Wr, L3_ffn_W1, L3_ffn_W2)
    return x

_drawn_inputs = setup_inputs


def setup_inputs(seed=0):
    import zlib

    import numpy as np

    out = dict(_drawn_inputs(seed))
    spreads = {'L1_xattn_bq': (0.0, 0.8),
     'L1_xattn_bk': (0.0, 2.0),
     'L1_xattn_bv': (0.0, 0.8),
     'L1_xattn_bo': (0.0, 0.8),
     'L1_ffn_ln1_g': (1.0, 0.6),
     'L1_ffn_ln1_b': (0.0, 0.8),
     'L1_ffn_ln2_g': (1.0, 0.6),
     'L1_ffn_ln2_b': (0.0, 0.8),
     'L2_ffn_ln1_scale': (1.0, 0.6),
     'L2_ffn_ln1_bias': (0.0, 0.8),
     'L2_ffn_b_qkv': (0.0, 0.8),
     'L2_ffn_b_attnproj': (0.0, 0.8),
     'L2_ffn_ln2_scale': (1.0, 0.6),
     'L2_ffn_ln2_bias': (0.0, 0.8),
     'L2_ffn_b_gate': (0.0, 0.8),
     'L2_ffn_b_fc': (0.0, 2.0),
     'L2_ffn_b_fcproj': (0.0, 2.0)}
    factors = {'g_ffn': 8.0,
     'L1_xattn_Wq': 8.0,
     'L1_xattn_Wk': 8.0,
     'L1_xattn_Wv': 8.0,
     'L1_xattn_Wo': 8.0,
     'L1_ffn_w1': 8.0,
     'L1_ffn_b1': 23.852,
     'L1_ffn_w2': 8.0,
     'L1_ffn_b2': 64.0,
     'L2_xattn_W': 8.0,
     'L2_xattn_b': 8.0,
     'L2_ffn_w_qkv': 8.0,
     'L2_ffn_w_attnproj': 8.0,
     'L2_ffn_w_gate': 8.0,
     'L2_ffn_w_fc': 8.0,
     'L2_ffn_w_fcproj': 8.0,
     'L3_xattn_Wq': 64.0,
     'L3_xattn_bq': 64.0,
     'L3_xattn_Wk': 64.0,
     'L3_xattn_bk': 200.0,
     'L3_xattn_Wv': 64.0,
     'L3_xattn_bv': 200.0,
     'L3_ffn_Wr': 64.0,
     'L3_ffn_W1': 64.0,
     'L3_ffn_W2': 64.0}
    for name, (base, spread) in spreads.items():
        noise = np.random.default_rng([zlib.crc32(name.encode()), seed]).standard_normal(out[name].shape)
        drawn = base * np.exp(spread * noise) if base else spread * noise
        out[name] = jnp.asarray(drawn.astype(out[name].dtype))
    for name, factor in factors.items():
        out[name] = (out[name] * factor).astype(out[name].dtype)
    return out
```

```python
from contextlib import ExitStack

import concourse.bass as bass
from concourse import mybir

ALU = mybir.AluOpType
ACT = mybir.ActivationFunctionType
F32 = mybir.dt.float32
BF16 = mybir.dt.bfloat16
I32 = mybir.dt.int32
U32 = mybir.dt.uint32
AX = mybir.AxisListType

P = 128
B, T, D, S_CTX = 32, 112, 256, 375
TOKENS = B * T
KD = D // P
SC, NSC = 125, 3
H0 = 768
F1 = 1024
KF = F1 // P
HEADS, HD = 16, 16
CH = P // HD
E = 8
LANES = 4
GROUPS = B // LANES
BANK = 512
EPS = 1e-5
INT8_SCALE = 1.0 / 127.0
MAGIC = 12582912.0
NEG = -1e9
MINUS_BIG = -3.0e38
CAP = int(1.25 * TOKENS / E)
BLK = 128
NBLK = (2 * TOKENS) // BLK + E - 1


def n(i, lane):
    return LANES * i + lane + 1


class Machine:

    def __init__(self, nc, stack, phase):
        self.nc, self.stack, self.phase, self.sems = nc, stack, phase, {}

    def sb(self, name, shape, dt=F32):
        return self.stack.enter_context(self.nc.sbuf_tensor(f'{self.phase}_{name}', shape, dt))

    def ps(self, name, shape, dt=F32):
        return self.stack.enter_context(self.nc.psum_tensor(f'{self.phase}_{name}', shape, dt))

    def sem(self, name):
        if name not in self.sems:
            self.sems[name] = self.stack.enter_context(self.nc.semaphore(f'{self.phase}_{name}'))
        return self.sems[name]

    def clear_all(self):
        sems = list(self.sems.values())
        with self.nc.Block() as block:
            @block.sync
            def _(sync):
                for s in sems:
                    sync.sem_clear(s)



def make_constants(nc, m, k):
    with nc.Block() as block:
        @block.gpsimd
        def _(g):
            g.memset(k['ones'][:, :], 1.0).then_inc(m.sem('ones_set'), 1)
            g.memset(k['minus_half'][:, :], -0.5)
            g.wait_ge(m.sem('ones_set'), 1)
            g.affine_select(k['ident'][:, :], k['ones'][:, :], [[-1, P]], ALU.is_equal, 0.0,
                            base=0, channel_multiplier=1).then_inc(m.sem('ident_set'), 1)
            g.affine_select(k['tri'][:, :], k['ones'][:, :], [[1, P]], ALU.is_ge, 0.0,
                            base=0, channel_multiplier=-1).then_inc(m.sem('ident_set'), 1)

        @block.vector
        def _(v):
            v.wait_ge(m.sem('ident_set'), 2)
            v.tensor_copy(k['ident16'][:, :], k['ident'][:, :]).then_inc(m.sem('ident_set'), 1)

        @block.sync
        def _(sync):
            sync.dma_start(k['gate'][:, 0:4], k['g_xattn'].partition_broadcast(P)).then_inc(m.sem('gates'), 16)
            sync.dma_start(k['gate'][:, 4:8], k['g_ffn'].partition_broadcast(P)).then_inc(m.sem('gates'), 16)

        @block.scalar
        def _(s):
            s.wait_ge(m.sem('gates'), 32)
            s.activation(k['gate'][:, :], k['gate'][:, :], ACT.Tanh).then_inc(m.sem('gates_tanh'), 1)
    m.clear_all()



def norm_stats(v, m, L, i, src_of, ready_of):
    for lane in range(LANES):
        src = src_of(lane)
        if ready_of is not None:
            v.wait_ge(*ready_of(lane))
        width = src.shape[1]
        parts = max(1, width // BANK)
        for j in range(parts):
            w = width // parts
            stats = v.bn_stats(L['stats'][:, lane, 6 * j:6 * j + 6], src[:, j * w:(j + 1) * w])
        stats.then_inc(m.sem('norm_stats'), 1)
    for lane in range(LANES):
        width = src_of(lane).shape[1]
        parts = max(1, width // BANK)
        v.wait_ge(m.sem('norm_stats'), n(i, lane))
        v.bn_aggr(L['mv'][:, lane, :], L['stats'][:, lane, 0:6 * parts]).then_inc(m.sem('norm_aggr'), 1)


def norm_apply(v, m, L, i, src_of, dst_of):
    for lane in range(LANES):
        v.wait_ge(m.sem('norm_rstd'), n(i, lane))
        v.tensor_scalar(dst_of(lane), src_of(lane), L['mv'][:, lane, 0:1], L['rstd'][:, lane, 0:1],
                        ALU.subtract, ALU.mult).then_inc(m.sem('norm_out'), 1)


def norm_rstd(g, m, L, i, minus_half):
    for lane in range(LANES):
        g.wait_ge(m.sem('norm_aggr'), n(i, lane))
        g.tensor_scalar(L['var'][:, lane, 0:1], L['mv'][:, lane, 1:2], EPS, None,
                        ALU.add).then_inc(m.sem('norm_var'), 1)
        g.wait_ge(m.sem('norm_var'), n(i, lane))
        g.tensor_tensor(L['rstd'][:, lane, 0:1], L['var'][:, lane, 0:1], minus_half,
                        ALU.pow).then_inc(m.sem('norm_rstd'), 1)


def turn_rows(pe, m, k, L, i, src_of, ready_of):
    for lane in range(LANES):
        pe.wait_ge(*ready_of(lane))
        src = src_of(lane)
        for c in range(KD):
            t = pe.transpose(L['ps'][lane][:, c * T:(c + 1) * T], src[:, c * P:(c + 1) * P],
                             k['ident'][0:T, 0:T])
        t.then_inc(m.sem('turned'), 1)


def project_t(pe, m, L, w, src_of, ready_of, bank, done):
    for lane in range(LANES):
        pe.wait_ge(*ready_of(lane))
        for o in range(KD):
            for c in range(KD):
                mm = pe.matmul(L['ps'][lane][:, bank * BANK + o * T:bank * BANK + (o + 1) * T],
                               w[:, c, o * P:(o + 1) * P], src_of(lane)[:, c * T:(c + 1) * T],
                               start=(c == 0), stop=(c == KD - 1))
        mm.then_inc(m.sem(done), 1)


def rows_out(pe, L, lane, w, lhs, chunks, bank, width, bias=None, ones=None, stop=True):
    out = L['ps'][lane][0:T, bank * BANK:bank * BANK + width]
    for c in range(chunks):
        mm = pe.matmul(out, lhs[:, c * T:(c + 1) * T], w[:, c, :], start=(c == 0),
                       stop=(c == chunks - 1 and bias is None))
    if bias is not None:
        mm = pe.matmul(out, ones[0:1, 0:T], bias, start=False, stop=True)
    return mm


def attention_scores(pe, m, L, i, q_of, ready_of):
    for lane in range(LANES):
        pe.wait_ge(*ready_of(lane))
        for c in range(KD):
            mm = pe.matmul(L['ps'][lane][0:T, BANK:BANK + S_CTX], q_of(lane)[:, c * T:(c + 1) * T],
                           L['ctxT'][:, lane, c, :], start=(c == 0), stop=(c == KD - 1))
        mm.then_inc(m.sem('scores'), 1)


def attention_logits(v, m, L, i, scale, mask_of=None, mask_ready=None, row_of=None):
    for lane in range(LANES):
        v.wait_ge(m.sem('scores'), n(i, lane))
        ps = L['ps'][lane][0:T, BANK:BANK + S_CTX]
        out = L['wide'][0:T, lane, 0:S_CTX]
        if mask_of is not None:
            v.wait_ge(*mask_ready(lane))
            v.scalar_tensor_tensor(out, ps, scale, mask_of(lane), ALU.mult,
                                   ALU.add).then_inc(m.sem('logits'), 1)
        elif row_of is not None:
            v.tensor_scalar(out, ps, row_of(lane), scale, ALU.add, ALU.mult).then_inc(m.sem('logits'), 1)
        else:
            v.tensor_copy(out, ps).then_inc(m.sem('logits'), 1)
    for lane in range(LANES):
        v.wait_ge(m.sem('logits'), n(i, lane))
        v.tensor_reduce(L['nmax'][:, lane, 0:1], L['wide'][0:T, lane, 0:S_CTX], AX.X, ALU.max,
                        negate=True).then_inc(m.sem('row_max'), 1)


def attention_exp(s, m, L, i):
    for lane in range(LANES):
        s.wait_ge(m.sem('row_max'), n(i, lane))
        s.activation(L['wide'][0:T, lane, 384:384 + S_CTX], L['wide'][0:T, lane, 0:S_CTX], ACT.Exp,
                     bias=L['nmax'][:, lane, 0:1], scale=1.0,
                     accum_out=L['sum'][:, lane, 0:1]).then_inc(m.sem('probs'), 1)


def attention_norm(v, m, L, i, j, gate=None):
    for lane in range(LANES):
        v.wait_ge(m.sem('probs'), n(i, lane))
        v.reciprocal(L['rsum'][:, lane, 0:1], L['sum'][:, lane, 0:1]).then_inc(m.sem('rsum'), 1)
    for lane in range(LANES):
        v.wait_ge(m.sem('rsum'), n(i, lane))
        if gate is not None:
            v.tensor_scalar(L['factor'][:, lane, 0:1], L['rsum'][:, lane, 0:1], gate, None,
                            ALU.mult).then_inc(m.sem('factor'), 1)
        else:
            p = L['wide'][0:T, lane, 384:384 + S_CTX]
            v.tensor_scalar(p, p, L['rsum'][:, lane, 0:1], None, ALU.mult).then_inc(m.sem('probs_normed'), 1)


def turn_probs(pe, m, k, L, i, ready_of):
    for lane in range(LANES):
        pe.wait_ge(*ready_of(lane))
        for c in range(NSC):
            t = pe.transpose(L['ps'][lane][0:SC, c * T:(c + 1) * T],
                             L['wide'][0:T, lane, 384 + c * SC:384 + (c + 1) * SC], k['ident'][0:T, 0:T])
        t.then_inc(m.sem('probs_turned'), 1)


def copy_probs(s, m, L, i):
    for lane in range(LANES):
        s.wait_ge(m.sem('probs_turned'), n(i, lane))
        s.activation(L['mid'][0:SC, lane, 0:NSC * T], L['ps'][lane][0:SC, 0:NSC * T],
                     ACT.Copy).then_inc(m.sem('probs_copied'), 1)


def attend_rows(pe, m, L, i):
    for lane in range(LANES):
        pe.wait_ge(m.sem('probs_copied'), n(i, lane))
        for c in range(NSC):
            mm = pe.matmul(L['ps'][lane][0:T, BANK:BANK + D], L['mid'][0:SC, lane, c * T:(c + 1) * T],
                           L['ctx'][:, lane, c, :], start=(c == 0), stop=(c == NSC - 1))
        mm.then_inc(m.sem('attended'), 1)


def attend_t(pe, m, L, i):
    for lane in range(LANES):
        pe.wait_ge(m.sem('probs_copied'), n(i, lane))
        for o in range(KD):
            for c in range(NSC):
                mm = pe.matmul(L['ps'][lane][:, BANK + o * T:BANK + (o + 1) * T],
                               L['ctx'][:, lane, c, o * P:(o + 1) * P],
                               L['mid'][0:SC, lane, c * T:(c + 1) * T],
                               start=(c == 0), stop=(c == NSC - 1))
        mm.then_inc(m.sem('attended'), 1)


def copy_t(s, m, L, src_bank, dst_of, ready_of, done, scale=None, bias=None):
    for lane in range(LANES):
        s.wait_ge(*ready_of(lane))
        src = L['ps'][lane][:, src_bank * BANK:src_bank * BANK + KD * T]
        if bias is None:
            s.activation(dst_of(lane), src, ACT.Copy).then_inc(m.sem(done), 1)
            continue
        for c in range(KD):
            last = s.activation(dst_of(lane)[:, c * T:(c + 1) * T], src[:, c * T:(c + 1) * T], ACT.Identity,
                                bias=bias[:, c:c + 1], scale=1.0 if scale is None else scale[:, c:c + 1])
        last.then_inc(m.sem(done), 1)


def turn_context(pe, m, k, L):
    for lane in range(LANES):
        for c in range(KD):
            for j in range(NSC):
                t = pe.transpose(L['ps'][lane][:, c * BANK + j * SC:c * BANK + (j + 1) * SC],
                                 L['ctx'][:, lane, j, c * P:(c + 1) * P], k['ident'][0:SC, 0:SC])
        t.then_inc(m.sem('ctx_turned'), 1)


def copy_context(s, m, L):
    for lane in range(LANES):
        s.wait_ge(m.sem('ctx_turned'), n(0, lane))
        for c in range(KD):
            last = s.activation(L['ctxT'][:, lane, c, :], L['ps'][lane][:, c * BANK:c * BANK + S_CTX], ACT.Copy)
        last.then_inc(m.sem('ctx_copied'), 1)


def load_context(sync, m, L, ctx_in, first, sems):
    for lane in range(LANES):
        sync.dma_start(L['ctx'][:, lane, :, :],
                       ctx_in[bass.ds(first + lane, 1), :, :].rearrange("o (c p) d -> p (o c) d", p=SC)
                       ).then_inc(m.sem(f'{sems}{lane}'), 16)


def lane_buffers(m, names_widths):
    L = {name: m.sb('lane_' + name, [rows, LANES, *width], F32) for name, rows, width in names_widths}
    L['ps'] = [m.ps(f'lane_ps{lane}', [P, 2 * BANK]) for lane in range(LANES)]
    return L



NORMS = ['x0', 'f0', 'x1', 'f1', 'f1_in', 'f1_hidden', 'x2', 'f2', 'f2_in', 'f2_moe']
UPDATES = ['x0', 'f0', 'x1', 'f1', 'x2']
ATTENTIONS = ['x0', 'x1', 'x2']


def phase_one(nc, a, k, scratch):
    with ExitStack() as stack:
        m = Machine(nc, stack, 'one')
        W = {}
        for name, rows, cols in [('w_gateT', D, H0), ('w_upT', D, H0), ('w_downT', H0, D), ('Wq1', D, D),
                                 ('WkT1', D, D), ('Wv1', D, D), ('Wo1', D, D), ('WT2', D, D),
                                 ('w_qkv', D, 3 * D), ('w_proj', D, D), ('w_route', D, E)]:
            W[name] = m.sb(name, [P, rows // P, cols])
        for name in ['bq1', 'bk1', 'bv1', 'b2x', 'ln1_scale', 'ln1_bias', 'bq2', 'bk2']:
            W[name] = m.sb(name, [P, KD])
        for name, cols in [('bo1', D), ('bv2', D), ('b_proj', D), ('b_route', E)]:
            W[name] = m.sb(name, [1, cols])
        for name, cols in [('ln1_g', D), ('ln1_b', D), ('b1', F1), ('ln2_g', F1), ('ln2_b', F1), ('b2', D),
                           ('ln2_scale', D), ('ln2_bias', D)]:
            W[name] = m.sb(name, [T, cols])
        W['w1q'] = m.sb('w1q', [P, KD, F1], BF16)
        W['w2q'] = m.sb('w2q', [P, KF, D], BF16)
        W['wscale'] = m.sb('wscale', [P, 2])
        W['headmask'] = m.sb('headmask', [P, CH])
        W['causal'] = m.sb('causal', [T, 4 * T])
        W['gate_int8'] = m.sb('gate_int8', [P, 1])
        load_weights(nc, a, k, W, scratch)

        L = lane_buffers(m, [('x', T, [D]), ('xh', T, [D]), ('u', T, [D]), ('hT', P, [KD * T]),
                             ('qT', P, [KD * T]), ('kT', P, [KD * T]), ('ctx', SC, [NSC, D]),
                             ('ctxT', P, [KD, S_CTX]), ('mask', T, [S_CTX]), ('block', P, [CH * T]),
                             ('wide', P, [HEADS * T]), ('mid', P, [CH * T]),
                             ('stats', T, [12]), ('mv', T, [2]), ('var', T, [1]), ('rstd', T, [1]),
                             ('nmax', T, [1]), ('sum', T, [1]), ('rsum', T, [1]), ('factor', T, [1]),
                             ('row', T, [1]), ('absmax', T, [1]), ('step', T, [1]), ('inv', T, [1]),
                             ('dq', T, [1]), ('hmax', T, [HEADS]), ('hsum', T, [HEADS]),
                             ('logit', T, [E])])
        flat = lambda name: (lambda lane: L[name][:, lane, :])

        with nc.Block() as block:
            @block.sync
            def _(sync):
                load_context(sync, m, L, a['ctx_1024'], 0, 'ctx')
                for lane in range(LANES):
                    sync.wait_ge(m.sem(f'ctx{lane}'), 16)
        m.clear_all()

        with nc.Fori(0, GROUPS) as g:
            with nc.Block() as block:
                phase_one_body(block, nc, m, a, k, W, L, flat, scratch, g)
            m.clear_all()


def phase_one_body(block, nc, m, a, k, W, L, flat, scratch, g):
    gate = k['gate']
    upd = lambda i: (lambda lane: (m.sem('x_updated'), n(i, lane)))
    normed = lambda i: (lambda lane: (m.sem('norm_out'), n(i, lane)))
    after = lambda name, i=0: (lambda lane: (m.sem(name), n(i, lane)))

    @block.sync
    def _(sync):
        for lane in range(LANES):
            b = g * LANES + lane
            sync.dma_start(L['x'][:, lane, :], a['x'][bass.ds(b, 1), :, :].rearrange("o t d -> (o t) d")
                           ).then_inc(m.sem(f'x_in{lane}'), 16)
            sync.dma_start(L['mid'][0:T, lane, 0:S_CTX].bitcast(I32),
                           a['mask_Bx1xS2_ik0'][bass.ds(b, 1), :, :].rearrange("o u s -> (o u) s")
                           .broadcast_to([T, S_CTX])).then_inc(m.sem(f'mask_in{lane}'), 16)
        for lane in range(LANES):
            b = g * LANES + lane
            sync.wait_ge(m.sem('v1'), n(0, lane))
            sync.dma_start(scratch['turned'][bass.ds(b, 1), :, :].rearrange("o (c p) t -> p (o c) t", p=P),
                           L['hT'][:, lane, :].rearrange("p (c t) -> p c t", c=KD)
                           ).then_inc(m.sem(f'turned_out{lane}'), 16)
        for lane in range(LANES):
            b = g * LANES + lane
            sync.wait_ge(m.sem(f'turned_out{lane}'), 16)
            sync.dma_start(L['u'][:, lane, :],
                           scratch['turned'][bass.ds(b, 1), :, :].rearrange("o p t -> (o p t)")
                           .rearrange("(i j) -> i j", j=D)).then_inc(m.sem(f'turned_in{lane}'), 16)
        for lane in range(LANES):
            b = g * LANES + lane
            sync.wait_ge(m.sem('x_updated'), n(4, lane))
            sync.dma_start(scratch['x2'][bass.ds(b * T, T), :], L['x'][:, lane, :]
                           ).then_inc(m.sem(f'x_out{lane}'), 16)
            sync.dma_start(L['ctx'][:, lane, :, :],
                           a['ctx_1024'][bass.ds((b + LANES) % B, 1), :, :]
                           .rearrange("o (c p) d -> p (o c) d", p=SC)).then_inc(m.sem(f'ctx{lane}'), 16)
        for lane in range(LANES):
            b = g * LANES + lane
            sync.wait_ge(m.sem('res2'), n(0, lane))
            sync.dma_start(scratch['res2'][bass.ds(b * T, T), :], L['xh'][:, lane, :]
                           ).then_inc(m.sem(f'res_out{lane}'), 16)
        for lane in range(LANES):
            b = g * LANES + lane
            sync.wait_ge(m.sem('moe_bias'), n(0, lane))
            sync.dma_start(scratch['moe_in'][bass.ds(b * T, T), :], L['u'][:, lane, :]
                           ).then_inc(m.sem(f'moe_out{lane}'), 16)
        for lane in range(LANES):
            b = g * LANES + lane
            sync.wait_ge(m.sem('route_copied'), n(0, lane))
            sync.dma_start(scratch['route2'][bass.ds(b * T, T), :], L['logit'][:, lane, :]
                           ).then_inc(m.sem(f'route_out{lane}'), 16)
        for lane in range(LANES):
            for name in ['x_out', 'ctx', 'res_out', 'moe_out', 'route_out']:
                sync.wait_ge(m.sem(f'{name}{lane}'), 16)

    @block.tensor
    def _(pe):
        turn_context(pe, m, k, L)
        for lane in range(LANES):
            pe.wait_ge(m.sem('ctx_copied'), n(0, lane))
        turn_rows(pe, m, k, L, 0, flat('xh'), normed(0))
        attention_scores(pe, m, L, 0, flat('hT'), after('turned_copied', 0))
        turn_probs(pe, m, k, L, 0, after('probs', 0))
        attend_rows(pe, m, L, 0)
        turn_rows(pe, m, k, L, 1, flat('xh'), normed(1))
        for r in range(2):
            for lane in range(LANES):
                pe.wait_ge(m.sem('turned_copied'), n(1, lane))
                if r:
                    pe.wait_ge(m.sem('hidden0'), n(0, lane))
                for bank, w in enumerate((W['w_gateT'], W['w_upT'])):
                    for j in range(3):
                        for c in range(KD):
                            o = (3 * r + j) * P
                            mm = pe.matmul(L['ps'][lane][:, bank * BANK + j * T:bank * BANK + (j + 1) * T],
                                           w[:, c, o:o + P], L['hT'][:, lane, c * T:(c + 1) * T],
                                           start=(c == 0), stop=(c == KD - 1))
                mm.then_inc(m.sem('gate_up'), 1)
        for lane in range(LANES):
            pe.wait_ge(m.sem('hidden0'), n(1, lane))
            rows_out(pe, L, lane, W['w_downT'], L['block'][:, lane, :], H0 // P, 0, D).then_inc(m.sem('down0'), 1)
        turn_rows(pe, m, k, L, 2, flat('xh'), normed(2))
        project_t(pe, m, L, W['Wq1'], flat('hT'), after('turned_copied', 2), 0, 'q1_raw')
        for lane in range(LANES):
            pe.wait_ge(m.sem('q1'), n(0, lane))
            for o in range(KD):
                for c in range(KD):
                    pe.matmul(L['ps'][lane][:, BANK + o * T:BANK + (o + 1) * T], W['WkT1'][:, c, o * P:(o + 1) * P],
                              L['qT'][:, lane, c * T:(c + 1) * T], start=(c == 0), stop=(c == KD - 1))
            for c in range(KD):
                mm = pe.matmul(L['ps'][lane][0:T, BANK + KD * T:BANK + KD * T + 1],
                               L['qT'][:, lane, c * T:(c + 1) * T], W['bk1'][:, c:c + 1],
                               start=(c == 0), stop=(c == KD - 1))
            mm.then_inc(m.sem('key_q1'), 1)
        attention_scores(pe, m, L, 1, flat('hT'), after('key_q1_copied'))
        turn_probs(pe, m, k, L, 1, after('probs_normed', 0))
        attend_t(pe, m, L, 1)
        project_t(pe, m, L, W['Wv1'], flat('qT'), after('attended_copied'), 0, 'v1_raw')
        turn_rows(pe, m, k, L, 3, flat('u'), lambda lane: (m.sem(f'turned_in{lane}'), 16))
        for lane in range(LANES):
            pe.wait_ge(m.sem('turned_copied'), n(3, lane))
            rows_out(pe, L, lane, W['Wo1'], L['qT'][:, lane, :], KD, 1, D, W['bo1'][:, :],
                     k['ones']).then_inc(m.sem('o1'), 1)
        for lane in range(LANES):
            pe.wait_ge(m.sem('quant'), n(0, lane))
            q = L['block'][0:T, lane, 0:D // 2].bitcast(BF16)
            out = L['ps'][lane][:, 0:KD * T // 2].bitcast(BF16)
            for c in range(KD):
                t = pe.transpose(out[:, c * T:(c + 1) * T], q[:, c * P:(c + 1) * P], k['ident16'][0:T, 0:T])
            t.then_inc(m.sem('quant_turned'), 1)
        for lane in range(LANES):
            pe.wait_ge(m.sem('quant_copied'), n(0, lane))
            qT = L['mid'][:, lane, 0:KD * T // 2].bitcast(BF16)
            for o in range(2):
                for c in range(KD):
                    mm = pe.matmul(L['ps'][lane][0:T, o * BANK:(o + 1) * BANK], qT[:, c * T:(c + 1) * T],
                                   W['w1q'][:, c, o * BANK:(o + 1) * BANK], start=(c == 0), stop=(c == KD - 1))
            mm.then_inc(m.sem('hidden1_raw'), 1)
        for lane in range(LANES):
            pe.wait_ge(m.sem('quant'), n(1, lane))
            q = L['block'][0:T, lane, 0:F1 // 2].bitcast(BF16)
            out = L['ps'][lane][:, 0:KF * T // 2].bitcast(BF16)
            for c in range(KF):
                t = pe.transpose(out[:, c * T:(c + 1) * T], q[:, c * P:(c + 1) * P], k['ident16'][0:T, 0:T])
            t.then_inc(m.sem('quant_turned'), 1)
        for lane in range(LANES):
            pe.wait_ge(m.sem('quant_copied'), n(1, lane))
            rows_out(pe, L, lane, W['w2q'], L['mid'][:, lane, 0:KF * T // 2].bitcast(BF16), KF, 1, D
                     ).then_inc(m.sem('ffn1_raw'), 1)
        turn_rows(pe, m, k, L, 4, flat('xh'), normed(6))
        project_t(pe, m, L, W['WT2'], flat('hT'), after('turned_copied', 4), 0, 'q2_raw')
        attention_scores(pe, m, L, 2, flat('qT'), after('q2'))
        turn_probs(pe, m, k, L, 2, after('probs', 2))
        attend_rows(pe, m, L, 2)
        turn_rows(pe, m, k, L, 5, flat('u'), normed(8))
        for lane in range(LANES):
            pe.wait_ge(m.sem('turned_copied'), n(5, lane))
            h = L['hT'][:, lane, :]
            for bank in range(2):
                for o in range(KD):
                    for c in range(KD):
                        pe.matmul(L['ps'][lane][:, bank * BANK + o * T:bank * BANK + (o + 1) * T],
                                  W['w_qkv'][:, c, bank * D + o * P:bank * D + (o + 1) * P],
                                  h[:, c * T:(c + 1) * T], start=(c == 0), stop=(c == KD - 1))
            v_out = L['ps'][lane][0:T, D:2 * D]
            for c in range(KD):
                pe.matmul(v_out, h[:, c * T:(c + 1) * T], W['w_qkv'][:, c, 2 * D:3 * D], start=(c == 0), stop=False)
            pe.matmul(v_out, k['ones'][0:1, 0:T], W['bv2'][:, :], start=False, stop=True
                      ).then_inc(m.sem('qkv'), 1)
        for c in range(KD):
            for lane in range(LANES):
                pe.wait_ge(m.sem('key_blocks'), n(c, lane))
                if c:
                    pe.wait_ge(m.sem('self_logits'), n(0, lane))
                for bank in range(2):
                    mm = pe.matmul(L['ps'][lane][0:T, bank * BANK:bank * BANK + 4 * T],
                                   L['qT'][:, lane, c * T:(c + 1) * T],
                                   L['block'][:, lane, bank * 4 * T:(bank + 1) * 4 * T], start=True, stop=True)
                mm.then_inc(m.sem('self_scores'), 1)
        for r in range(HEADS // 4):
            for lane in range(LANES):
                pe.wait_ge(m.sem('self_probs'), n(r // 2, lane))
                if r:
                    pe.wait_ge(m.sem('self_copied'), n(r - 1, lane))
                else:
                    pe.wait_ge(m.sem('self_logits'), n(1, lane))
                for h in range(4):
                    t = pe.transpose(L['ps'][lane][0:T, h * T:(h + 1) * T],
                                     L['wide'][0:T, lane, (4 * r + h) * T:(4 * r + h + 1) * T], k['ident'][0:T, 0:T])
                t.then_inc(m.sem('self_turned'), 1)
            for lane in range(LANES):
                pe.wait_ge(m.sem('self_copied'), n(r, lane))
                for h in range(4 * r, 4 * r + 4):
                    mm = pe.matmul(L['ps'][lane][0:T, BANK + h * HD:BANK + (h + 1) * HD],
                                   L['mid'][0:T, lane, (h % 8) * T:(h % 8 + 1) * T],
                                   L['mask'][:, lane, h * HD:(h + 1) * HD], start=True, stop=True)
                mm.then_inc(m.sem('self_out'), 1)
        turn_rows(pe, m, k, L, 6, flat('u'), after('self_normed'))
        for lane in range(LANES):
            pe.wait_ge(m.sem('turned_copied'), n(6, lane))
            rows_out(pe, L, lane, W['w_proj'], L['hT'][:, lane, :], KD, 1, D, W['b_proj'][:, :],
                     k['ones']).then_inc(m.sem('self_proj'), 1)
        turn_rows(pe, m, k, L, 7, flat('u'), after('moe_bias'))
        for lane in range(LANES):
            pe.wait_ge(m.sem('turned_copied'), n(7, lane))
            rows_out(pe, L, lane, W['w_route'], L['hT'][:, lane, :], KD, 1, E, W['b_route'][:, :],
                     k['ones']).then_inc(m.sem('route'), 1)

    @block.scalar
    def _(s):
        copy_context(s, m, L)
        copy_t(s, m, L, 0, flat('hT'), after('turned', 0), 'turned_copied')
        attention_exp(s, m, L, 0)
        copy_probs(s, m, L, 0)
        copy_t(s, m, L, 0, flat('hT'), after('turned', 1), 'turned_copied')
        for r in range(2):
            for lane in range(LANES):
                s.wait_ge(m.sem('gate_up'), n(r, lane))
                s.activation(L['mid'][:, lane, 0:3 * T], L['ps'][lane][:, 0:3 * T], ACT.Tanh,
                             scale=INT8_SCALE / 2).then_inc(m.sem('gate_tanh'), 1)
        copy_t(s, m, L, 0, flat('hT'), after('turned', 2), 'turned_copied')
        copy_t(s, m, L, 0, flat('qT'), after('q1_raw'), 'q1', bias=W['bq1'])
        for lane in range(LANES):
            s.wait_ge(m.sem('key_q1'), n(0, lane))
            s.activation(L['hT'][:, lane, :], L['ps'][lane][:, BANK:BANK + KD * T], ACT.Copy)
            s.activation(L['row'][:, lane, :], L['ps'][lane][0:T, BANK + KD * T:BANK + KD * T + 1],
                         ACT.Copy).then_inc(m.sem('key_q1_copied'), 1)
        attention_exp(s, m, L, 1)
        copy_probs(s, m, L, 1)
        copy_t(s, m, L, 1, flat('qT'), after('attended', 1), 'attended_copied')
        copy_t(s, m, L, 0, flat('hT'), after('v1_raw'), 'v1', bias=W['bv1'])
        copy_t(s, m, L, 0, flat('qT'), after('turned', 3), 'turned_copied')
        for lane in range(LANES):
            s.wait_ge(m.sem('quant_turned'), n(0, lane))
            s.activation(L['mid'][:, lane, 0:KD * T // 2].bitcast(BF16),
                         L['ps'][lane][:, 0:KD * T // 2].bitcast(BF16), ACT.Copy
                         ).then_inc(m.sem('quant_copied'), 1)
        for lane in range(LANES):
            s.wait_ge(m.sem('hidden1'), n(0, lane))
            s.activation(L['wide'][0:T, lane, 0:F1], L['wide'][0:T, lane, 0:F1], ACT.Gelu).then_inc(m.sem('gelu1'), 1)
        for lane in range(LANES):
            s.wait_ge(m.sem('quant_turned'), n(1, lane))
            s.activation(L['mid'][:, lane, 0:KF * T // 2].bitcast(BF16),
                         L['ps'][lane][:, 0:KF * T // 2].bitcast(BF16), ACT.Copy
                         ).then_inc(m.sem('quant_copied'), 1)
        copy_t(s, m, L, 0, flat('hT'), after('turned', 4), 'turned_copied')
        copy_t(s, m, L, 0, flat('qT'), after('q2_raw'), 'q2', bias=W['b2x'])
        attention_exp(s, m, L, 2)
        copy_probs(s, m, L, 2)
        copy_t(s, m, L, 0, flat('hT'), after('turned', 5), 'turned_copied', scale=W['ln1_scale'],
               bias=W['ln1_bias'])
        for lane in range(LANES):
            s.wait_ge(m.sem('qkv'), n(0, lane))
            for c in range(KD):
                for bank, name, bias in ((0, 'qT', 'bq2'), (1, 'kT', 'bk2')):
                    s.activation(L[name][:, lane, c * T:(c + 1) * T],
                                 L['ps'][lane][:, bank * BANK + c * T:bank * BANK + (c + 1) * T], ACT.Identity,
                                 bias=W[bias][:, c:c + 1], scale=1.0)
            s.activation(L['mask'][:, lane, 0:D], L['ps'][lane][0:T, D:2 * D], ACT.Copy
                         ).then_inc(m.sem('qkv_copied'), 1)
        for c in range(KD):
            for lane in range(LANES):
                s.wait_ge(m.sem('self_shifted'), n(c, lane))
                w = L['wide'][0:T, lane, c * CH * T:(c + 1) * CH * T]
                s.activation(w, w, ACT.Exp).then_inc(m.sem('self_probs'), 1)
        for r in range(HEADS // 4):
            for lane in range(LANES):
                s.wait_ge(m.sem('self_turned'), n(r, lane))
                s.activation(L['mid'][0:T, lane, (r % 2) * 4 * T:(r % 2 + 1) * 4 * T],
                             L['ps'][lane][0:T, 0:4 * T], ACT.Copy).then_inc(m.sem('self_copied'), 1)
        copy_t(s, m, L, 0, flat('hT'), after('turned', 6), 'turned_copied')
        copy_t(s, m, L, 0, flat('hT'), after('turned', 7), 'turned_copied')

    @block.gpsimd
    def _(gp):
        for lane in range(LANES):
            gp.wait_ge(m.sem(f'mask_in{lane}'), 16)
            gp.tensor_scalar(L['mask'][:, lane, :], L['mid'][0:T, lane, 0:S_CTX].bitcast(I32), NEG, None,
                             ALU.mult).then_inc(m.sem('mask_ready'), 1)
        for i in range(len(NORMS)):
            norm_rstd(gp, m, L, i, k['minus_half'][0:T, 0:1])

    @block.vector
    def _(v):
        def update(name, i, bank, factor_of, done_sem, count):
            for lane in range(LANES):
                v.wait_ge(m.sem(done_sem), n(count, lane))
                v.scalar_tensor_tensor(L['x'][:, lane, :], L['ps'][lane][0:T, bank * BANK:bank * BANK + D],
                                       factor_of(lane), L['x'][:, lane, :], ALU.mult,
                                       ALU.add).then_inc(m.sem('x_updated'), 1)

        def quantise(i, src_of, width):
            q_of = lambda lane: L['block'][0:T, lane, 0:width // 2].bitcast(BF16)
            for lane in range(LANES):
                v.wait_ge(m.sem('quant_in'), n(i, lane))
                v.tensor_reduce(L['absmax'][:, lane, :], src_of(lane), AX.X, ALU.max,
                                apply_absolute_value=True).then_inc(m.sem('quant_max'), 1)
            for lane in range(LANES):
                v.wait_ge(m.sem('quant_max'), n(i, lane))
                v.tensor_scalar(L['step'][:, lane, :], L['absmax'][:, lane, :], EPS, INT8_SCALE, ALU.max,
                                ALU.mult).then_inc(m.sem('quant_step'), 1)
            for lane in range(LANES):
                v.wait_ge(m.sem('quant_step'), n(i, lane))
                v.reciprocal(L['inv'][:, lane, :], L['step'][:, lane, :])
                v.tensor_scalar(L['dq'][:, lane, :], L['step'][:, lane, :], W['wscale'][0:T, i:i + 1], None,
                                ALU.mult).then_inc(m.sem('quant_inv'), 1)
            for lane in range(LANES):
                v.wait_ge(m.sem('quant_inv'), n(i, lane))
                v.tensor_scalar(src_of(lane), src_of(lane), L['inv'][:, lane, :], 127.0, ALU.mult,
                                ALU.min).then_inc(m.sem('quant_scaled'), 1)
            for lane in range(LANES):
                v.wait_ge(m.sem('quant_scaled'), n(i, lane))
                v.tensor_scalar(src_of(lane), src_of(lane), -128.0, MAGIC, ALU.max,
                                ALU.add).then_inc(m.sem('quant_rounded'), 1)
            for lane in range(LANES):
                v.wait_ge(m.sem('quant_rounded'), n(i, lane))
                v.tensor_scalar(q_of(lane), src_of(lane), -MAGIC, None, ALU.add).then_inc(m.sem('quant'), 1)

        norm_stats(v, m, L, 0, flat('x'), lambda lane: (m.sem(f'x_in{lane}'), 16))
        norm_apply(v, m, L, 0, flat('x'), flat('xh'))
        attention_logits(v, m, L, 0, D ** -0.5, flat('mask'), after('mask_ready'))
        attention_norm(v, m, L, 0, 0, gate[0:T, 0:1])
        for lane in range(LANES):
            v.wait_ge(m.sem('factor'), n(0, lane))
        update('x0', 0, 1, lambda lane: L['factor'][:, lane, 0:1], 'attended', 0)
        norm_stats(v, m, L, 1, flat('x'), upd(0))
        norm_apply(v, m, L, 1, flat('x'), flat('xh'))
        for r in range(2):
            for lane in range(LANES):
                v.wait_ge(m.sem('gate_tanh'), n(r, lane))
                v.scalar_tensor_tensor(L['wide'][:, lane, 0:3 * T], L['mid'][:, lane, 0:3 * T], 1.0,
                                       L['ps'][lane][:, 0:3 * T], ALU.add, ALU.mult
                                       ).then_inc(m.sem('gate_silu'), 1)
            for lane in range(LANES):
                v.wait_ge(m.sem('gate_silu'), n(r, lane))
                v.scalar_tensor_tensor(L['block'][:, lane, r * 3 * T:(r + 1) * 3 * T],
                                       L['ps'][lane][:, BANK:BANK + 3 * T], INT8_SCALE * INT8_SCALE / 2,
                                       L['wide'][:, lane, 0:3 * T], ALU.mult, ALU.mult).then_inc(m.sem('hidden0'), 1)
        update('f0', 1, 0, lambda lane: W['gate_int8'][0:T, 0:1], 'down0', 0)
        norm_stats(v, m, L, 2, flat('x'), upd(1))
        norm_apply(v, m, L, 2, flat('x'), flat('xh'))
        for lane in range(LANES):
            v.wait_ge(m.sem('key_q1_copied'), n(0, lane))
        attention_logits(v, m, L, 1, D ** -0.5, row_of=lambda lane: L['row'][:, lane, 0:1])
        attention_norm(v, m, L, 1, 0)
        update('x1', 2, 1, lambda lane: gate[0:T, 1:2], 'o1', 0)
        norm_stats(v, m, L, 3, flat('x'), upd(2))
        norm_apply(v, m, L, 3, flat('x'), flat('xh'))
        norm_stats(v, m, L, 4, flat('xh'), normed(3))
        norm_apply(v, m, L, 4, flat('xh'), flat('u'))
        for lane in range(LANES):
            v.wait_ge(m.sem('norm_out'), n(4, lane))
            v.tensor_tensor(L['u'][:, lane, :], L['u'][:, lane, :], W['ln1_g'][:, :], ALU.mult
                            ).then_inc(m.sem('quant_gain'), 1)
        for lane in range(LANES):
            v.wait_ge(m.sem('quant_gain'), n(0, lane))
            v.tensor_tensor(L['u'][:, lane, :], L['u'][:, lane, :], W['ln1_b'][:, :], ALU.add
                            ).then_inc(m.sem('quant_in'), 1)
        quantise(0, flat('u'), D)
        hidden = lambda lane: L['wide'][0:T, lane, 0:F1]
        for lane in range(LANES):
            v.wait_ge(m.sem('hidden1_raw'), n(0, lane))
            v.scalar_tensor_tensor(hidden(lane), L['ps'][lane][0:T, 0:F1], L['dq'][:, lane, 0:1],
                                   W['b1'][:, :], ALU.mult, ALU.add).then_inc(m.sem('hidden1'), 1)
        norm_stats(v, m, L, 5, hidden, after('gelu1'))
        norm_apply(v, m, L, 5, hidden, hidden)
        for lane in range(LANES):
            v.wait_ge(m.sem('norm_out'), n(5, lane))
            v.tensor_tensor(hidden(lane), hidden(lane), W['ln2_g'][:, :], ALU.mult
                            ).then_inc(m.sem('quant_gain'), 1)
        for lane in range(LANES):
            v.wait_ge(m.sem('quant_gain'), n(1, lane))
            v.tensor_tensor(hidden(lane), hidden(lane), W['ln2_b'][:, :], ALU.add
                            ).then_inc(m.sem('quant_in'), 1)
        quantise(1, hidden, F1)
        for lane in range(LANES):
            v.wait_ge(m.sem('ffn1_raw'), n(0, lane))
            v.scalar_tensor_tensor(L['u'][:, lane, :], L['ps'][lane][0:T, BANK:BANK + D], L['dq'][:, lane, 0:1],
                                   W['b2'][:, :], ALU.mult, ALU.add).then_inc(m.sem('ffn1'), 1)
        for lane in range(LANES):
            v.wait_ge(m.sem('ffn1'), n(0, lane))
            v.scalar_tensor_tensor(L['x'][:, lane, :], L['u'][:, lane, :], gate[0:T, 5:6], L['x'][:, lane, :],
                                   ALU.mult, ALU.add).then_inc(m.sem('x_updated'), 1)
        norm_stats(v, m, L, 6, flat('x'), upd(3))
        norm_apply(v, m, L, 6, flat('x'), flat('xh'))
        attention_logits(v, m, L, 2, 1.0)
        attention_norm(v, m, L, 2, 1, gate[0:T, 2:3])
        for lane in range(LANES):
            v.wait_ge(m.sem('factor'), n(1, lane))
        update('x2', 4, 1, lambda lane: L['factor'][:, lane, 0:1], 'attended', 2)
        norm_stats(v, m, L, 7, flat('x'), upd(4))
        norm_apply(v, m, L, 7, flat('x'), flat('xh'))
        norm_stats(v, m, L, 8, flat('xh'), normed(7))
        norm_apply(v, m, L, 8, flat('xh'), flat('u'))
        for c in range(KD):
            for lane in range(LANES):
                if c:
                    v.wait_ge(m.sem('self_scores'), n(0, lane))
                else:
                    v.wait_ge(m.sem('qkv_copied'), n(0, lane))
                v.tensor_tensor(L['block'][:, lane, :].rearrange("p (j t) -> p j t", j=CH),
                                L['kT'][:, lane, c * T:(c + 1) * T].unsqueeze(1).broadcast_to([P, CH, T]),
                                W['headmask'][:, :].unsqueeze(2).broadcast_to([P, CH, T]), ALU.mult
                                ).then_inc(m.sem('key_blocks'), 1)
            for lane in range(LANES):
                wide = L['wide'][0:T, lane, c * CH * T:(c + 1) * CH * T]
                v.wait_ge(m.sem('self_scores'), n(c, lane))
                for bank in range(2):
                    last = v.scalar_tensor_tensor(wide[:, bank * 4 * T:(bank + 1) * 4 * T],
                                                  L['ps'][lane][0:T, bank * BANK:bank * BANK + 4 * T],
                                                  HD ** -0.5, W['causal'][:, :], ALU.mult, ALU.add)
                last.then_inc(m.sem('self_logits'), 1)
            for lane in range(LANES):
                heads = L['wide'][0:T, lane, c * CH * T:(c + 1) * CH * T].rearrange("p (j t) -> p j t", j=CH)
                v.wait_ge(m.sem('self_logits'), n(c, lane))
                v.tensor_reduce(L['hmax'][:, lane, c * CH:(c + 1) * CH], heads, AX.X, ALU.max
                                ).then_inc(m.sem('self_max'), 1)
            for lane in range(LANES):
                heads = L['wide'][0:T, lane, c * CH * T:(c + 1) * CH * T].rearrange("p (j t) -> p j t", j=CH)
                v.wait_ge(m.sem('self_max'), n(c, lane))
                v.tensor_tensor(heads, heads, L['hmax'][:, lane, c * CH:(c + 1) * CH].unsqueeze(2)
                                .broadcast_to([T, CH, T]), ALU.subtract).then_inc(m.sem('self_shifted'), 1)
        for lane in range(LANES):
            for c in range(KD):
                heads = L['wide'][0:T, lane, c * CH * T:(c + 1) * CH * T].rearrange("p (j t) -> p j t", j=CH)
                v.wait_ge(m.sem('self_probs'), n(c, lane))
                last = v.tensor_reduce(L['hsum'][:, lane, c * CH:(c + 1) * CH], heads, AX.X, ALU.add)
            last.then_inc(m.sem('self_sum'), 1)
        for lane in range(LANES):
            v.wait_ge(m.sem('self_sum'), n(0, lane))
            v.reciprocal(L['hsum'][:, lane, :], L['hsum'][:, lane, :]).then_inc(m.sem('self_rsum'), 1)
        for lane in range(LANES):
            v.wait_ge(m.sem('self_rsum'), n(0, lane))
            v.wait_ge(m.sem('self_out'), n(3, lane))
            v.tensor_tensor(L['u'][:, lane, :].rearrange("p (h j) -> p h j", h=HEADS),
                            L['ps'][lane][0:T, BANK:BANK + D].rearrange("p (h j) -> p h j", h=HEADS),
                            L['hsum'][:, lane, :].unsqueeze(2).broadcast_to([T, HEADS, HD]), ALU.mult
                            ).then_inc(m.sem('self_normed'), 1)
        for lane in range(LANES):
            v.wait_ge(m.sem('self_proj'), n(0, lane))
            v.tensor_tensor(L['xh'][:, lane, :], L['ps'][lane][0:T, BANK:BANK + D], L['xh'][:, lane, :],
                            ALU.add).then_inc(m.sem('res2'), 1)
        norm_stats(v, m, L, 9, flat('xh'), after('res2'))
        norm_apply(v, m, L, 9, flat('xh'), flat('u'))
        for lane in range(LANES):
            v.wait_ge(m.sem('norm_out'), n(9, lane))
            v.tensor_tensor(L['u'][:, lane, :], L['u'][:, lane, :], W['ln2_scale'][:, :], ALU.mult
                            ).then_inc(m.sem('moe_gain'), 1)
        for lane in range(LANES):
            v.wait_ge(m.sem('moe_gain'), n(0, lane))
            v.tensor_tensor(L['u'][:, lane, :], L['u'][:, lane, :], W['ln2_bias'][:, :], ALU.add
                            ).then_inc(m.sem('moe_bias'), 1)
        for lane in range(LANES):
            v.wait_ge(m.sem('route'), n(0, lane))
            v.tensor_copy(L['logit'][:, lane, :], L['ps'][lane][0:T, BANK:BANK + E]
                          ).then_inc(m.sem('route_copied'), 1)


def load_weights(nc, a, k, W, scratch):
    with ExitStack() as stack:
        m = Machine(nc, stack, 'load')
        w1, w2 = m.sb('w1_raw', [P, KD, F1]), m.sb('w2_raw', [P, KF, D])
        total = m.sb('abs_total', [P, 2])
        inv = m.sb('w_inv', [P, 2])
        k['zeros'] = m.sb('zeros', [P, 2320])
        mean_ps = m.ps('mean_ps', [P, 2])

        with nc.Block() as block:
            @block.vector
            def _(v):
                v.memset(k['zeros'][:, :], 0.0)

        with nc.Block() as block:
            @block.sync
            def _(sync):
                loads = 0
                for tile, name in ((w1, 'w1T'), (w2, 'w2T')):
                    sync.dma_start(tile[:, :, :], a[name].rearrange("(c p) n -> p c n", p=P)
                                   ).then_inc(m.sem('w12_in'), 16)
                for name in ('w_gateT', 'w_upT', 'w_downT'):
                    sync.dma_start(W[name][:, :, :].bitcast(I32), a[name].rearrange("(c p) n -> p c n", p=P)
                                   ).then_inc(m.sem('ints_in'), 16)
                for name, src in (('Wq1', 'L1_xattn_Wq'), ('WkT1', 'WkT1'), ('Wv1', 'L1_xattn_Wv'),
                                  ('Wo1', 'L1_xattn_Wo'), ('WT2', 'WT2'), ('w_qkv', 'L2_ffn_w_qkv'),
                                  ('w_proj', 'L2_ffn_w_attnproj'), ('w_route', 'L2_ffn_w_gate')):
                    sync.dma_start(W[name][:, :, :], a[src].rearrange("(c p) n -> p c n", p=P)
                                   ).then_inc(m.sem('rest_in'), 16)
                    loads += 1
                bq = a['L2_ffn_b_qkv']
                with nc.allow_non_contiguous_dma(reason="a few hundred bias values, once"):
                    for name, src in (('bq1', a['L1_xattn_bq']), ('bk1', a['L1_xattn_bk']),
                                      ('bv1', a['L1_xattn_bv']), ('b2x', a['L2_xattn_b']),
                                      ('ln1_scale', a['L2_ffn_ln1_scale']), ('ln1_bias', a['L2_ffn_ln1_bias']),
                                      ('bq2', bq[0:D]), ('bk2', bq[D:2 * D])):
                        sync.dma_start(W[name][:, :], src.rearrange("(c p) -> p c", p=P)
                                       ).then_inc(m.sem('rest_in'), 16)
                        loads += 1
                for name, src in (('bo1', a['L1_xattn_bo']), ('bv2', bq[2 * D:3 * D]),
                                  ('b_proj', a['L2_ffn_b_attnproj']), ('b_route', a['L2_ffn_b_gate'])):
                    sync.dma_start(W[name][:, :], src.partition_broadcast(1)).then_inc(m.sem('rest_in'), 16)
                    loads += 1
                for name, src in (('ln1_g', 'L1_ffn_ln1_g'), ('ln1_b', 'L1_ffn_ln1_b'), ('b1', 'L1_ffn_b1'),
                                  ('ln2_g', 'L1_ffn_ln2_g'), ('ln2_b', 'L1_ffn_ln2_b'), ('b2', 'L1_ffn_b2'),
                                  ('ln2_scale', 'L2_ffn_ln2_scale'), ('ln2_bias', 'L2_ffn_ln2_bias')):
                    sync.dma_start(W[name][:, :], a[src].partition_broadcast(T)).then_inc(m.sem('rest_in'), 16)
                    loads += 1
                sync.wait_ge(m.sem('rest_in'), 16 * loads)

            @block.scalar
            def _(s):
                zero_fill(s, m, k, scratch)

            @block.gpsimd
            def _(g):
                g.affine_select(W['headmask'][:, :], k['ones'][:, 0:CH], [[-HD, CH]], ALU.is_ge, 0.0,
                                base=0, channel_multiplier=1).then_inc(m.sem('masks'), 1)
                g.wait_ge(m.sem('masks'), 1)
                g.affine_select(W['headmask'][:, :], W['headmask'][:, :], [[HD, CH]], ALU.is_ge, 0.0,
                                base=HD - 1, channel_multiplier=-1)
                g.memset(W['causal'][:, :], 0.0).then_inc(m.sem('masks'), 1)
                g.wait_ge(m.sem('masks'), 2)
                g.affine_select(W['causal'][:, :], W['causal'][:, :], [[0, 4], [-1, T]], ALU.is_ge, -1e30,
                                base=0, channel_multiplier=1)

            @block.tensor
            def _(pe):
                pe.wait_ge(m.sem('abs_sums'), 2)
                pe.matmul(mean_ps[:, :], k['ones'][:, :], total[:, :], start=True, stop=True
                          ).then_inc(m.sem('abs_totals'), 1)

            @block.vector
            def _(v):
                v.wait_ge(m.sem('w12_in'), 32)
                for i, w in enumerate((w1, w2)):
                    v.tensor_reduce(total[:, i:i + 1], w[:, :, :], AX.XY, ALU.add, apply_absolute_value=True
                                    ).then_inc(m.sem('abs_sums'), 1)
                v.wait_ge(m.sem('ints_in'), 48)
                for name in ('w_gateT', 'w_upT', 'w_downT'):
                    v.tensor_copy(W[name][:, :, :], W[name][:, :, :].bitcast(I32))
                v.tensor_scalar(W['gate_int8'][:, :], k['gate'][:, 4:5], INT8_SCALE, None, ALU.mult)
                v.wait_ge(m.sem('abs_totals'), 1)
                v.tensor_scalar(W['wscale'][:, :], mean_ps[:, :], 1.0 / (D * F1), EPS, ALU.mult, ALU.max
                                ).then_inc(m.sem('w_mean'), 1)
                v.wait_ge(m.sem('w_mean'), 1)
                v.reciprocal(inv[:, :], W['wscale'][:, :]).then_inc(m.sem('w_mean'), 1)
                v.wait_ge(m.sem('w_mean'), 2)
                for i, w in enumerate((w1, w2)):
                    v.tensor_scalar(w[:, :, :], w[:, :, :], inv[:, i:i + 1], 1.0, ALU.mult, ALU.min
                                    ).then_inc(m.sem('w_step'), 1)
                for i, w in enumerate((w1, w2)):
                    v.wait_ge(m.sem('w_step'), 2)
                    v.tensor_scalar(w[:, :, :], w[:, :, :], -1.0, MAGIC, ALU.max, ALU.add
                                    ).then_inc(m.sem('w_step2'), 1)
                v.wait_ge(m.sem('w_step2'), 2)
                for w, q in ((w1, 'w1q'), (w2, 'w2q')):
                    v.tensor_scalar(W[q][:, :, :], w[:, :, :], -MAGIC, None, ALU.add)
        m.clear_all()



def zero_fill(queue, m, k, scratch):
    flat2 = scratch['moe_x2'].rearrange("r w -> (r w)").rearrange("(p f) -> p f", p=P)
    step = flat2.shape[1] // 7
    for j in range(7):
        queue.dma_start(flat2[:, j * step:(j + 1) * step], k['zeros'][:, 0:step]).then_inc(m.sem('zeroed'), 16)
    flat3 = scratch['moe_x3'][0:E * CAP, :].rearrange("r w -> (r w)").rearrange("(p f) -> p f", p=P)
    step = flat3.shape[1] // 4
    for j in range(4):
        queue.dma_start(flat3[:, j * step:(j + 1) * step], k['zeros'][:, 0:step]).then_inc(m.sem('zeroed'), 16)
    queue.wait_ge(m.sem('zeroed'), 16 * 11)


def spread(ap, shape):
    return ap.unsqueeze(2).broadcast_to(shape)


def route_block(nc, a, k, scratch, name, top_k, finish, extra):
    with ExitStack() as stack:
        m = Machine(nc, stack, name)
        R = {t: m.sb('route_' + t, [T, B, E]) for t in
             ('p', 'eq', 'prio', 'oh0', 'oh1', 'taken', 'slot', 'tmp')}
        for t in ('max', 'sum', 'pm0', 'pm1', 'prio_max', 'slot0', 'slot1'):
            R[t] = m.sb('route_' + t, [T, B])
        for t in ('total', 'before'):
            R[t] = m.sb('route_' + t, [T, E, B])
        for t in ('count', 'blocks', 'blocks_to', 'blocks_before', 'base', 'rank', 'ones8'):
            R[t] = m.sb('route_' + t, [T, E])
        R['iota_i'] = m.sb('route_iota_i', [T, 128], I32)
        R['iota'] = m.sb('route_iota', [T, 128])
        R['ones32'] = m.sb('route_ones32', [T, B])
        R['part_i'] = m.sb('route_part_i', [T, 1], I32)
        R['part'] = m.sb('route_part', [T, 1])
        R['ranks'] = m.ps('route_ranks', [P, BANK])
        R['totals'] = m.ps('route_totals', [P, BANK])
        full = [T, B, E]
        extra(m, R)

        with nc.Block() as block:
            @block.sync
            def _(sync):
                sync.dma_start(R['p'][:, :, :], scratch[name].rearrange("(b t) e -> t b e", t=T)
                               ).then_inc(m.sem('logits_in'), 16)

            @block.gpsimd
            def _(g):
                g.iota(R['iota_i'][:, :], [[1, 128]], base=0, channel_multiplier=0)
                g.iota(R['part_i'][:, :], [[0, 1]], base=0, channel_multiplier=1).then_inc(m.sem('iota'), 1)

            @block.scalar
            def _(s):
                s.wait_ge(m.sem('shifted'), 1)
                s.activation(R['p'][:, :, :], R['p'][:, :, :], ACT.Exp).then_inc(m.sem('exp'), 1)

            @block.tensor
            def _(pe):
                pe.wait_ge(m.sem('taken'), 1)
                pe.matmul(R['ranks'][0:T, 0:B * E], k['tri'][0:T, 0:T],
                          R['taken'][:, :, :].rearrange("p b e -> p (b e)"), start=True, stop=True)
                pe.matmul(R['totals'][0:T, 0:B * E], k['ones'][0:T, 0:T],
                          R['taken'][:, :, :].rearrange("p b e -> p (b e)"), start=True, stop=True
                          ).then_inc(m.sem('ranked'), 1)

            @block.vector
            def _(v):
                v.memset(R['ones32'][:, :], 1.0)
                v.memset(R['ones8'][:, :], 1.0)
                v.wait_ge(m.sem('iota'), 1)
                v.tensor_copy(R['iota'][:, :], R['iota_i'][:, :]).then_inc(m.sem('iota_f'), 1)
                v.tensor_copy(R['part'][:, :], R['part_i'][:, :])
                v.wait_ge(m.sem('iota_f'), 1)
                v.tensor_scalar(R['rank'][:, :], R['iota'][:, 0:E], -1.0, float(E), ALU.mult, ALU.add)
                v.wait_ge(m.sem('logits_in'), 16)
                v.tensor_reduce(R['max'][:, :], R['p'][:, :, :], AX.X, ALU.max).then_inc(m.sem('max'), 1)
                v.wait_ge(m.sem('max'), 1)
                v.tensor_tensor(R['p'][:, :, :], R['p'][:, :, :], spread(R['max'][:, :], full), ALU.subtract
                                ).then_inc(m.sem('shifted'), 1)
                v.wait_ge(m.sem('exp'), 1)
                v.tensor_reduce(R['sum'][:, :], R['p'][:, :, :], AX.X, ALU.add).then_inc(m.sem('sum'), 1)
                v.wait_ge(m.sem('sum'), 1)
                v.reciprocal(R['sum'][:, :], R['sum'][:, :]).then_inc(m.sem('sum'), 1)
                v.wait_ge(m.sem('sum'), 2)
                v.tensor_tensor(R['p'][:, :, :], R['p'][:, :, :], spread(R['sum'][:, :], full), ALU.mult
                                ).then_inc(m.sem('probs'), 1)
                for c in range(top_k):
                    pm, oh = R[f'pm{c}'], R[f'oh{c}']
                    v.wait_ge(m.sem('probs'), c + 1)
                    v.tensor_reduce(pm[:, :], R['p'][:, :, :], AX.X, ALU.max).then_inc(m.sem('pm'), 1)
                    v.wait_ge(m.sem('pm'), c + 1)
                    v.tensor_tensor(R['eq'][:, :, :], R['p'][:, :, :], spread(pm[:, :], full), ALU.is_equal
                                    ).then_inc(m.sem('equal'), 1)
                    v.wait_ge(m.sem('equal'), c + 1)
                    v.tensor_tensor(R['prio'][:, :, :], R['eq'][:, :, :],
                                    R['rank'][:, :].unsqueeze(1).broadcast_to(full), ALU.mult
                                    ).then_inc(m.sem('prio'), 1)
                    v.wait_ge(m.sem('prio'), c + 1)
                    v.tensor_reduce(R['prio_max'][:, :], R['prio'][:, :, :], AX.X, ALU.max
                                    ).then_inc(m.sem('prio_max'), 1)
                    v.wait_ge(m.sem('prio_max'), c + 1)
                    v.tensor_tensor(oh[:, :, :], R['prio'][:, :, :], spread(R['prio_max'][:, :], full),
                                    ALU.is_equal).then_inc(m.sem('one_hot'), 1)
                    v.wait_ge(m.sem('one_hot'), c + 1)
                    if c + 1 < top_k:
                        v.scalar_tensor_tensor(R['p'][:, :, :], oh[:, :, :], -2.0, R['p'][:, :, :], ALU.mult,
                                               ALU.add).then_inc(m.sem('probs'), 1)
                if top_k == 2:
                    v.tensor_tensor(R['taken'][:, :, :], R['oh0'][:, :, :], R['oh1'][:, :, :], ALU.add
                                    ).then_inc(m.sem('taken'), 1)
                else:
                    v.tensor_copy(R['taken'][:, :, :], R['oh0'][:, :, :]).then_inc(m.sem('taken'), 1)
                v.wait_ge(m.sem('ranked'), 1)
                v.tensor_copy(R['total'][:, :, :], R['totals'][0:T, 0:B * E].rearrange("p (b e) -> p e b", e=E)
                              ).then_inc(m.sem('total'), 1)
                v.wait_ge(m.sem('total'), 1)
                for e in range(E):
                    last = v.tensor_tensor_scan(R['before'][:, e, :], R['ones32'][:, :], R['total'][:, e, :],
                                                0.0, ALU.mult, ALU.add)
                last.then_inc(m.sem('running'), 1)
                v.wait_ge(m.sem('running'), 1)
                v.tensor_copy(R['count'][:, :], R['before'][:, :, B - 1]).then_inc(m.sem('count'), 1)
                v.wait_ge(m.sem('count'), 1)
                v.tensor_tensor(R['before'][:, :, :], R['before'][:, :, :], R['total'][:, :, :], ALU.subtract
                                ).then_inc(m.sem('before'), 1)
                v.wait_ge(m.sem('before'), 1)
                finish(v, m, R)
        m.clear_all()


def slots_of(v, m, R, k, c, count):
    v.tensor_tensor(R['tmp'][:, :, :], R[f'oh{c}'][:, :, :], R['slot'][:, :, :], ALU.mult
                    ).then_inc(m.sem('slot_pick'), 1)
    v.wait_ge(m.sem('slot_pick'), count)
    v.tensor_reduce(R[f'slot{c}'][:, :], R['tmp'][:, :, :], AX.X, ALU.add).then_inc(m.sem('slot_sum'), 1)
    v.wait_ge(m.sem('slot_sum'), count)


def phase_route_two(nc, a, k, scratch, K2):
    NJ = TOKENS // BLK

    def finish(v, m, R):
        with_blocks = R['cmp']
        v.tensor_scalar(R['mult'][:, :], R['iota'][:, 0:NJ], float(BLK), None, ALU.mult
                        ).then_inc(m.sem('steps'), 1)
        v.wait_ge(m.sem('steps'), 1)
        v.tensor_tensor(with_blocks[:, :, 0:NJ], R['count'][:, :].unsqueeze(2).broadcast_to([T, E, NJ]),
                        R['mult'][:, :].unsqueeze(1).broadcast_to([T, E, NJ]), ALU.is_gt
                        ).then_inc(m.sem('steps'), 1)
        v.wait_ge(m.sem('steps'), 2)
        v.tensor_reduce(R['blocks'][:, :], with_blocks[:, :, 0:NJ], AX.X, ALU.add).then_inc(m.sem('steps'), 1)
        v.wait_ge(m.sem('steps'), 3)
        v.tensor_tensor_scan(R['blocks_to'][:, :], R['ones8'][:, :], R['blocks'][:, :], 0.0, ALU.mult, ALU.add
                             ).then_inc(m.sem('steps'), 1)
        v.wait_ge(m.sem('steps'), 4)
        v.tensor_tensor(R['blocks_before'][:, :], R['blocks_to'][:, :], R['blocks'][:, :], ALU.subtract
                        ).then_inc(m.sem('steps'), 1)
        v.wait_ge(m.sem('steps'), 5)
        v.tensor_scalar(R['base'][:, :], R['blocks_before'][:, :], float(BLK), -1.0, ALU.mult, ALU.add
                        ).then_inc(m.sem('steps'), 1)
        v.wait_ge(m.sem('steps'), 6)
        v.tensor_tensor(R['before'][:, :, :], R['before'][:, :, :],
                        R['base'][:, :].unsqueeze(2).broadcast_to([T, E, B]), ALU.add).then_inc(m.sem('steps'), 1)
        v.wait_ge(m.sem('steps'), 7)
        v.tensor_tensor(R['slot'][:, :, :], R['ranks'][0:T, 0:B * E].rearrange("p (b e) -> p b e", e=E),
                        R['before'][:, :, :].rearrange("p e b -> p b e"), ALU.add).then_inc(m.sem('steps'), 1)
        v.wait_ge(m.sem('steps'), 8)
        for c in range(2):
            slots_of(v, m, R, k, c, c + 1)
            v.tensor_copy(K2['slot'][:, c, :], R[f'slot{c}'][:, :])
            v.tensor_copy(K2['weight'][:, c, :], R[f'pm{c}'][:, :])
        v.tensor_tensor(R['passed'][:, :, :], R['iota'][:, 0:NBLK].unsqueeze(2).broadcast_to([T, NBLK, E]),
                        R['blocks_to'][:, :].unsqueeze(1).broadcast_to([T, NBLK, E]), ALU.is_ge
                        ).then_inc(m.sem('steps'), 1)
        v.wait_ge(m.sem('steps'), 9)
        v.tensor_reduce(R['expert'][:, :], R['passed'][:, :, :], AX.X, ALU.add).then_inc(m.sem('steps'), 1)
        v.wait_ge(m.sem('steps'), 10)
        v.tensor_tensor(R['passed'][:, :, :], R['passed'][:, :, :],
                        R['blocks'][:, :].unsqueeze(1).broadcast_to([T, NBLK, E]), ALU.mult
                        ).then_inc(m.sem('steps'), 1)
        v.wait_ge(m.sem('steps'), 11)
        v.tensor_scalar(R['expert'][:, :], R['expert'][:, :], float(E - 1), None, ALU.min
                        ).then_inc(m.sem('steps'), 1)
        v.tensor_reduce(R['row'][:, :], R['passed'][:, :, :], AX.X, ALU.add).then_inc(m.sem('steps'), 1)
        v.wait_ge(m.sem('steps'), 13)
        v.tensor_copy(K2['expert'][:, :], R['expert'][0:1, :])
        v.tensor_scalar(K2['one_hot'][:, :], R['expert'][0:E, :], R['part'][0:E, 0:1], None, ALU.is_equal)
        v.tensor_tensor(R['row'][:, :], R['iota'][:, 0:NBLK], R['row'][:, :], ALU.subtract
                        ).then_inc(m.sem('steps'), 1)
        v.wait_ge(m.sem('steps'), 14)
        v.tensor_scalar(K2['row'][:, :], R['row'][0:1, :], float(NJ - 1), None, ALU.min)

    extra = lambda m, R: R.update(cmp=m.sb('route_cmp', [T, E, 28]), mult=m.sb('route_mult', [T, 28]),
                                  passed=m.sb('route_passed', [T, NBLK, E]),
                                  expert=m.sb('route_expert', [T, NBLK]), row=m.sb('route_row', [T, NBLK]))
    route_block(nc, a, k, scratch, 'route2', 2, finish, extra)


def phase_scatter(nc, k, scratch, src, dst, slot, weight, copies):
    width = D + (1 if weight is not None else 0)
    with ExitStack() as stack:
        m = Machine(nc, stack, f'scatter{copies}')
        rows = m.sb('scatter_rows', [T, LANES, copies, width])
        index = m.sb('scatter_index', [T, LANES, copies], U32)
        scattered = k['pool_dma'][f'scattered{copies}']
        with nc.Fori(0, GROUPS) as g:
            with nc.Block() as block:
                @block.sync
                def _(sync):
                    for lane in range(LANES):
                        for c in range(copies):
                            sync.dma_start(rows[:, lane, c, 0:D], src[bass.ds((g * LANES + lane) * T, T), :]
                                           ).then_inc(m.sem(f'rows_in{lane}'), 16)

                @block.vector
                def _(v):
                    for lane in range(LANES):
                        b = g * LANES + lane
                        for c in range(copies):
                            if weight is not None:
                                v.tensor_copy(rows[:, lane, c, D:D + 1], weight[:, c, bass.ds(b, 1)])
                            last = v.tensor_copy(index[:, lane, c:c + 1], slot[:, c, bass.ds(b, 1)])
                        last.then_inc(m.sem('indexed'), 1)

                @block.gpsimd
                def _(gp):
                    for lane in range(LANES):
                        gp.wait_ge(m.sem(f'rows_in{lane}'), 16 * copies)
                        gp.wait_ge(m.sem('indexed'), lane + 1)
                        for c in range(copies):
                            gp.indirect_dma_start(dst, bass.IndirectOffsetOnAxis(ap=index[:, lane, c:c + 1], axis=0),
                                                  rows[:, lane, c, :], None).then_inc(scattered, 16)
                    gp.wait_ge(scattered, (g + 1) * (16 * LANES * copies))
            m.clear_all()



STEP = 7
assert NBLK % STEP == 0


def phase_experts_two(nc, a, k, scratch, K2):
    NJ = TOKENS // BLK
    with ExitStack() as outer:
        mo = Machine(nc, outer, 'acc')
        acc = mo.sb('moe_acc', [P, NJ, D])
        with ExitStack() as stack:
            m = Machine(nc, stack, 'experts2')
            w_fc = m.sb('w_fc', [P, E, KD, F1])
            w_out = m.sb('w_out', [P, E, KF, D])
            b_fc, b_out = m.sb('b_fc', [E, F1]), m.sb('b_out', [E, D])
            rows = m.sb('moe_rows', [P, 2, D + 1])
            xT = m.sb('moe_xT', [P, 2, KD * P])
            hid = m.sb('moe_hidden', [P, 2, F1])
            hT = m.sb('moe_hiddenT', [P, KF * P])
            pick = m.sb('moe_pick', [E, 2, P])
            x_ps = m.ps('moe_x_ps', [P, BANK])
            h_ps = [m.ps(f'moe_h_ps{i}', [P, 2 * BANK]) for i in range(2)]
            t_ps = m.ps('moe_t_ps', [P, 2 * BANK])
            o_ps = m.ps('moe_o_ps', [P, BANK])

            with nc.Block() as block:
                @block.sync
                def _(sync):
                    for e in range(E):
                        sync.dma_start(w_fc[:, e, :, :], a['L2_ffn_w_fc'][e].rearrange("(c p) n -> p c n", p=P)
                                       ).then_inc(m.sem('weights_in'), 16)
                    sync.dma_start(b_fc[:, :], a['L2_ffn_b_fc']).then_inc(m.sem('weights_in'), 16)
                    sync.wait_ge(m.sem('weights_in'), 16 * (E + 1))

                @block.scalar
                def _(s):
                    for e in range(E):
                        s.dma_start(w_out[:, e, :, :], a['L2_ffn_w_fcproj'][e].rearrange("(c p) n -> p c n", p=P)
                                    ).then_inc(m.sem('weights_in2'), 16)
                    s.dma_start(b_out[:, :], a['L2_ffn_b_fcproj']).then_inc(m.sem('weights_in2'), 16)
                    s.wait_ge(m.sem('weights_in2'), 16 * (E + 1))

                @block.vector
                def _(v):
                    v.memset(acc[:, :, :], 0.0)
            m.clear_all()

            with nc.Fori(0, NBLK // STEP) as g:
                with nc.Block() as block:
                    @block.sync
                    def _(sync):
                        for j in range(STEP):
                            if j >= 2:
                                sync.wait_ge(m.sem('x_turned'), j - 1)
                                sync.wait_ge(m.sem('added'), j - 1)
                            sync.dma_start(rows[:, j % 2, :],
                                           scratch['moe_x2'][bass.ds((g * STEP + j) * BLK, BLK), :]
                                           ).then_inc(m.sem(f'rows_in{j % 2}'), 16)

                    @block.tensor
                    def _(pe):
                        def turn_x(j):
                            pe.wait_ge(m.sem(f'rows_in{j % 2}'), 16 * (j // 2 + 1))
                            if j:
                                pe.wait_ge(m.sem('x_copied'), j)
                            for c in range(KD):
                                t = pe.transpose(x_ps[:, c * P:(c + 1) * P], rows[:, j % 2, c * P:(c + 1) * P],
                                                 k['ident'][:, :])
                            t.then_inc(m.sem('x_turned'), 1)

                        def hidden(j):
                            e = pe.value_load(K2['expert'][0:1, bass.ds(g * STEP + j, 1)], min_val=0, max_val=E - 1)
                            pe.wait_ge(m.sem('x_copied'), j + 1)
                            pe.wait_ge(m.sem('picked'), j + 1)
                            if j >= 2:
                                pe.wait_ge(m.sem('activated'), j - 1)
                            for o in range(2):
                                out = h_ps[j % 2][:, o * BANK:(o + 1) * BANK]
                                for c in range(KD):
                                    pe.matmul(out, xT[:, j % 2, c * P:(c + 1) * P],
                                              w_fc[:, bass.ds(e, 1), c, o * BANK:(o + 1) * BANK]
                                              .rearrange("p o n -> p (o n)"), start=(c == 0), stop=False)
                                mm = pe.matmul(out, pick[:, j % 2, :], b_fc[:, o * BANK:(o + 1) * BANK],
                                               start=False, stop=True)
                            mm.then_inc(m.sem('hidden'), 1)
                            return e

                        def output(j, e):
                            pe.wait_ge(m.sem('activated'), j + 1)
                            if j:
                                pe.wait_ge(m.sem('h_copied'), 2 * j)
                            for o in range(2):
                                for c in range(4 * o, 4 * o + 4):
                                    t = pe.transpose(t_ps[:, c * P:(c + 1) * P], hid[:, j % 2, c * P:(c + 1) * P],
                                                     k['ident'][:, :])
                                t.then_inc(m.sem('h_turned'), 1)
                            if j:
                                pe.wait_ge(m.sem('added'), j)
                            pe.matmul(o_ps[:, 0:D], pick[:, j % 2, :], b_out[:, :], start=True, stop=False)
                            for c in range(KF):
                                if c % 4 == 0:
                                    pe.wait_ge(m.sem('h_copied'), 2 * j + 1 + c // 4)
                                mm = pe.matmul(o_ps[:, 0:D], hT[:, c * P:(c + 1) * P],
                                               w_out[:, bass.ds(e, 1), c, :].rearrange("p o n -> p (o n)"),
                                               start=False, stop=(c == KF - 1))
                            mm.then_inc(m.sem('out'), 1)

                        turn_x(0)
                        experts = [hidden(0)]
                        for j in range(STEP):
                            if j + 1 < STEP:
                                turn_x(j + 1)
                                experts.append(hidden(j + 1))
                            output(j, experts[j])

                    @block.scalar
                    def _(s):
                        for j in range(STEP):
                            s.wait_ge(m.sem('hidden'), j + 1)
                            if j >= 2:
                                s.wait_ge(m.sem('h_turned'), 2 * (j - 1))
                            s.activation(hid[:, j % 2, :], h_ps[j % 2][:, :], ACT.Gelu_apprx_tanh
                                         ).then_inc(m.sem('activated'), 1)

                    @block.vector
                    def _(v):
                        def copy_x(j):
                            if j >= 2:
                                v.wait_ge(m.sem('out'), j - 1)
                            v.tensor_copy(pick[:, j % 2, :],
                                          K2['one_hot'][:, bass.ds(g * STEP + j, 1)].broadcast_to([E, P])
                                          ).then_inc(m.sem('picked'), 1)
                            v.wait_ge(m.sem('x_turned'), j + 1)
                            v.tensor_copy(xT[:, j % 2, :], x_ps[:, 0:KD * P]).then_inc(m.sem('x_copied'), 1)

                        copy_x(0)
                        for j in range(STEP):
                            if j + 1 < STEP:
                                copy_x(j + 1)
                            row = v.value_load(K2['row'][0:1, bass.ds(g * STEP + j, 1)], min_val=0,
                                               max_val=NJ - 1)
                            for o in range(2):
                                v.wait_ge(m.sem('h_turned'), 2 * j + 1 + o)
                                if j:
                                    v.wait_ge(m.sem('out'), j)
                                v.tensor_copy(hT[:, o * BANK:(o + 1) * BANK], t_ps[:, o * BANK:(o + 1) * BANK]
                                              ).then_inc(m.sem('h_copied'), 1)
                            v.wait_ge(m.sem('out'), j + 1)
                            if j:
                                v.wait_ge(m.sem('added'), j)
                            place = acc[:, bass.ds(row, 1), :].rearrange("p o n -> p (o n)")
                            v.scalar_tensor_tensor(place, o_ps[:, 0:D], rows[:, j % 2, D:D + 1], place,
                                                   ALU.mult, ALU.add).then_inc(m.sem('added'), 1)
                m.clear_all()

        with ExitStack() as stack:
            m = Machine(nc, stack, 'combine2')
            x2, res = m.sb('x2_rows', [P, NJ, D]), m.sb('res_rows', [P, NJ, D])
            parts, w = 4, NJ // 4
            by_rows = lambda ap, j: ap[j * w * P:(j + 1) * w * P, :].rearrange("(j p) d -> p j d", p=P)
            with nc.Block() as block:
                @block.sync
                def _(sync):
                    for j in range(parts):
                        sync.dma_start(res[:, j * w:(j + 1) * w, :], by_rows(scratch['res2'], j)
                                       ).then_inc(m.sem(f'in{j}'), 16)
                        sync.dma_start(x2[:, j * w:(j + 1) * w, :], by_rows(scratch['x2'], j)
                                       ).then_inc(m.sem(f'in{j}'), 16)
                    for j in range(parts):
                        sync.wait_ge(m.sem('combined'), j + 1)
                        sync.dma_start(by_rows(scratch['x3'], j), x2[:, j * w:(j + 1) * w, :]
                                       ).then_inc(m.sem('x3_out'), 16)
                    sync.wait_ge(m.sem('x3_out'), 16 * parts)

                @block.vector
                def _(v):
                    for j in range(parts):
                        s = slice(j * w, (j + 1) * w)
                        v.wait_ge(m.sem(f'in{j}'), 32)
                        v.tensor_tensor(res[:, s, :], res[:, s, :], acc[:, s, :], ALU.add).then_inc(m.sem('summed'), 1)
                        v.wait_ge(m.sem('summed'), j + 1)
                        v.scalar_tensor_tensor(x2[:, s, :], res[:, s, :], k['gate'][:, 6:7], x2[:, s, :], ALU.mult,
                                               ALU.add).then_inc(m.sem('combined'), 1)
            m.clear_all()



def phase_four(nc, a, k, scratch):
    with ExitStack() as stack:
        m = Machine(nc, stack, 'four')
        W = {}
        for name, cols in [('WqT3', D), ('Wk3', D), ('WvT3', D), ('Wr', E)]:
            W[name] = m.sb(name, [P, KD, cols])
        for name in ('bq3', 'bq3s', 'bk3', 'qscale'):
            W[name] = m.sb(name, [P, KD])
        W['bv3'] = m.sb('bv3', [1, D])
        L = lane_buffers(m, [('x', T, [D]), ('xh', T, [D]), ('u', T, [D]), ('hT', P, [KD * T]),
                             ('qT', P, [KD * T]), ('ctx', SC, [NSC, D]), ('ctxT', P, [KD, S_CTX]),
                             ('mask', T, [S_CTX]), ('wide', P, [2 * 384]), ('mid', P, [384]),
                             ('stats', T, [12]), ('mv', T, [2]), ('var', T, [1]), ('rstd', T, [1]),
                             ('nmax', T, [1]), ('sum', T, [1]), ('rsum', T, [1]), ('factor', T, [1]),
                             ('row', T, [1]), ('logit', T, [E])])
        flat = lambda name: (lambda lane: L[name][:, lane, :])
        after = lambda name, i=0: (lambda lane: (m.sem(name), n(i, lane)))
        rows3 = scratch['moe_y3']

        with nc.Block() as block:
            @block.sync
            def _(sync):
                load_context(sync, m, L, a['ctx_1024'], 0, 'ctx')
                for name, src in (('WqT3', 'WqT3'), ('Wk3', 'L3_xattn_Wk'), ('WvT3', 'WvT3'), ('Wr', 'L3_ffn_Wr')):
                    sync.dma_start(W[name][:, :, :], a[src].rearrange("(c p) n -> p c n", p=P)
                                   ).then_inc(m.sem('w_in'), 16)
                with nc.allow_non_contiguous_dma(reason="a few hundred bias values, once"):
                    for name, src in (('bq3', 'L3_xattn_bq'), ('bk3', 'L3_xattn_bk')):
                        sync.dma_start(W[name][:, :], a[src].rearrange("(c p) -> p c", p=P)
                                       ).then_inc(m.sem('w_in'), 16)
                sync.dma_start(W['bv3'][:, :], a['L3_xattn_bv'].partition_broadcast(1)).then_inc(m.sem('w_in'), 16)
                sync.wait_ge(m.sem('w_in'), 16 * 7)
                for lane in range(LANES):
                    sync.wait_ge(m.sem(f'ctx{lane}'), 16)

            @block.vector
            def _(v):
                v.memset(W['qscale'][:, :], D ** -0.5)
                v.wait_ge(m.sem('w_in'), 16 * 7)
                v.tensor_scalar(W['bq3s'][:, :], W['bq3'][:, :], D ** -0.5, None, ALU.mult)
        m.clear_all()

        with nc.Fori(0, GROUPS) as g:
            with nc.Block() as block:
                @block.sync
                def _(sync):
                    for lane in range(LANES):
                        b = g * LANES + lane
                        sync.dma_start(L['x'][:, lane, :], scratch['x3'][bass.ds(b * T, T), :]
                                       ).then_inc(m.sem(f'x_in{lane}'), 16)
                        sync.dma_start(L['mid'][0:T, lane, 0:S_CTX].bitcast(I32),
                                       a['mask_BxS2_ik1'][bass.ds(b, 1), :].broadcast_to([T, S_CTX])
                                       ).then_inc(m.sem(f'mask_in{lane}'), 16)
                    for lane in range(LANES):
                        sync.wait_ge(m.sem('attended'), n(0, lane))
                        sync.dma_start(L['ctx'][:, lane, :, :],
                                       a['ctx_1024'][bass.ds((g * LANES + lane + LANES) % B, 1), :, :]
                                       .rearrange("o (c p) d -> p (o c) d", p=SC)).then_inc(m.sem(f'ctx{lane}'), 16)
                    for lane in range(LANES):
                        b = g * LANES + lane
                        sync.wait_ge(m.sem('x_updated'), n(0, lane))
                        sync.dma_start(scratch['x4'][bass.ds(b * T, T), :], L['x'][:, lane, :]
                                       ).then_inc(m.sem(f'x_out{lane}'), 16)
                    for lane in range(LANES):
                        b = g * LANES + lane
                        sync.wait_ge(m.sem('norm_out'), n(1, lane))
                        sync.dma_start(rows3[bass.ds(b * T + E * CAP, T), :], L['u'][:, lane, :]
                                       ).then_inc(m.sem(f'h_out{lane}'), 16)
                    for lane in range(LANES):
                        b = g * LANES + lane
                        sync.wait_ge(m.sem('route_copied'), n(0, lane))
                        sync.dma_start(scratch['route3'][bass.ds(b * T, T), :], L['logit'][:, lane, :]
                                       ).then_inc(m.sem(f'route_out{lane}'), 16)
                    for lane in range(LANES):
                        for name in ('x_out', 'h_out', 'route_out', 'ctx'):
                            sync.wait_ge(m.sem(f'{name}{lane}'), 16)

                @block.tensor
                def _(pe):
                    turn_context(pe, m, k, L)
                    for lane in range(LANES):
                        pe.wait_ge(m.sem('ctx_copied'), n(0, lane))
                    turn_rows(pe, m, k, L, 0, flat('xh'), after('norm_out', 0))
                    project_t(pe, m, L, W['WqT3'], flat('hT'), after('turned_copied', 0), 0, 'q3_raw')
                    for lane in range(LANES):
                        pe.wait_ge(m.sem('q3'), n(0, lane))
                        for o in range(KD):
                            for c in range(KD):
                                pe.matmul(L['ps'][lane][:, BANK + o * T:BANK + (o + 1) * T],
                                          W['Wk3'][:, c, o * P:(o + 1) * P], L['qT'][:, lane, c * T:(c + 1) * T],
                                          start=(c == 0), stop=(c == KD - 1))
                        for c in range(KD):
                            mm = pe.matmul(L['ps'][lane][0:T, BANK + KD * T:BANK + KD * T + 1],
                                           L['qT'][:, lane, c * T:(c + 1) * T], W['bk3'][:, c:c + 1],
                                           start=(c == 0), stop=(c == KD - 1))
                        mm.then_inc(m.sem('key_q3'), 1)
                    attention_scores(pe, m, L, 0, flat('hT'), after('key_q3_copied'))
                    turn_probs(pe, m, k, L, 0, after('probs_normed', 0))
                    attend_t(pe, m, L, 0)
                    for lane in range(LANES):
                        pe.wait_ge(m.sem('attended_copied'), n(0, lane))
                        rows_out(pe, L, lane, W['WvT3'], L['qT'][:, lane, :], KD, 0, D, W['bv3'][:, :], k['ones']
                                 ).then_inc(m.sem('v3'), 1)
                    turn_rows(pe, m, k, L, 1, flat('u'), after('norm_out', 1))
                    for lane in range(LANES):
                        pe.wait_ge(m.sem('turned_copied'), n(1, lane))
                        rows_out(pe, L, lane, W['Wr'], L['hT'][:, lane, :], KD, 1, E).then_inc(m.sem('route'), 1)

                @block.scalar
                def _(s):
                    copy_context(s, m, L)
                    copy_t(s, m, L, 0, flat('hT'), after('turned', 0), 'turned_copied')
                    copy_t(s, m, L, 0, flat('qT'), after('q3_raw'), 'q3', scale=W['qscale'], bias=W['bq3s'])
                    for lane in range(LANES):
                        s.wait_ge(m.sem('key_q3'), n(0, lane))
                        s.activation(L['hT'][:, lane, :], L['ps'][lane][:, BANK:BANK + KD * T], ACT.Copy)
                        s.activation(L['row'][:, lane, :], L['ps'][lane][0:T, BANK + KD * T:BANK + KD * T + 1],
                                     ACT.Copy).then_inc(m.sem('key_q3_copied'), 1)
                    attention_exp(s, m, L, 0)
                    copy_probs(s, m, L, 0)
                    copy_t(s, m, L, 1, flat('qT'), after('attended', 0), 'attended_copied')
                    copy_t(s, m, L, 0, flat('hT'), after('turned', 1), 'turned_copied')

                @block.gpsimd
                def _(gp):
                    for lane in range(LANES):
                        gp.wait_ge(m.sem(f'mask_in{lane}'), 16)
                        gp.tensor_scalar(L['mask'][:, lane, :], L['mid'][0:T, lane, 0:S_CTX].bitcast(I32), 0.0,
                                         MINUS_BIG, ALU.is_equal, ALU.mult).then_inc(m.sem('mask_ready'), 1)
                    for i in range(2):
                        norm_rstd(gp, m, L, i, k['minus_half'][0:T, 0:1])

                @block.vector
                def _(v):
                    norm_stats(v, m, L, 0, flat('x'), lambda lane: (m.sem(f'x_in{lane}'), 16))
                    norm_apply(v, m, L, 0, flat('x'), flat('xh'))
                    for lane in range(LANES):
                        v.wait_ge(m.sem('key_q3_copied'), n(0, lane))
                        v.wait_ge(m.sem('mask_ready'), n(0, lane))
                        v.wait_ge(m.sem('scores'), n(0, lane))
                        v.scalar_tensor_tensor(L['wide'][0:T, lane, 0:S_CTX], L['ps'][lane][0:T, BANK:BANK + S_CTX],
                                               L['row'][:, lane, 0:1], L['mask'][:, lane, :], ALU.add,
                                               ALU.add).then_inc(m.sem('logits'), 1)
                    for lane in range(LANES):
                        v.wait_ge(m.sem('logits'), n(0, lane))
                        v.tensor_reduce(L['nmax'][:, lane, 0:1], L['wide'][0:T, lane, 0:S_CTX], AX.X, ALU.max,
                                        negate=True).then_inc(m.sem('row_max'), 1)
                    attention_norm(v, m, L, 0, 0)
                    for lane in range(LANES):
                        v.wait_ge(m.sem('v3'), n(0, lane))
                        v.scalar_tensor_tensor(L['x'][:, lane, :], L['ps'][lane][0:T, 0:D], k['gate'][0:T, 3:4],
                                               L['x'][:, lane, :], ALU.mult, ALU.add
                                               ).then_inc(m.sem('x_updated'), 1)
                    norm_stats(v, m, L, 1, flat('x'), after('x_updated', 0))
                    norm_apply(v, m, L, 1, flat('x'), flat('u'))
                    for lane in range(LANES):
                        v.wait_ge(m.sem('route'), n(0, lane))
                        v.tensor_copy(L['logit'][:, lane, :], L['ps'][lane][0:T, BANK:BANK + E]
                                      ).then_inc(m.sem('route_copied'), 1)
            m.clear_all()



def phase_route_three(nc, a, k, scratch, K3):
    def finish(v, m, R):
        step = [0]

        def done(ins):
            step[0] += 1
            ins.then_inc(m.sem('steps'), 1)
            v.wait_ge(m.sem('steps'), step[0])
        done(v.tensor_tensor(R['slot'][:, :, :], R['ranks'][0:T, 0:B * E].rearrange("p (b e) -> p b e", e=E),
                             R['before'][:, :, :].rearrange("p e b -> p b e"), ALU.add))
        slots_of(v, m, R, k, 0, 1)
        done(v.tensor_scalar(R['slot0'][:, :], R['slot0'][:, :], -1.0, None, ALU.add))
        done(v.tensor_scalar(R['kept'][:, :], R['slot0'][:, :], float(CAP), None, ALU.is_lt))
        done(v.tensor_scalar(R['slot1'][:, :], R['prio_max'][:, :], -float(CAP), float(E * CAP), ALU.mult, ALU.add))
        done(v.tensor_tensor(R['slot0'][:, :], R['slot0'][:, :], R['slot1'][:, :], ALU.add))
        done(v.tensor_scalar(R['own'][:, :], R['iota'][:, 0:B], float(T), float(E * CAP), ALU.mult, ALU.add))
        done(v.tensor_scalar(R['own'][:, :], R['own'][:, :], R['part'][:, 0:1], None, ALU.add))
        done(v.tensor_tensor(R['slot0'][:, :], R['slot0'][:, :], R['own'][:, :], ALU.subtract))
        done(v.tensor_tensor(R['slot0'][:, :], R['slot0'][:, :], R['kept'][:, :], ALU.mult))
        done(v.tensor_tensor(R['slot0'][:, :], R['slot0'][:, :], R['own'][:, :], ALU.add))
        v.tensor_copy(K3['slot'][:, 0, :], R['slot0'][:, :])
        done(v.tensor_tensor(R['pm0'][:, :], R['pm0'][:, :], R['kept'][:, :], ALU.mult))
        done(v.tensor_scalar(R['kept'][:, :], R['kept'][:, :], -1.0, 1.0, ALU.mult, ALU.add))
        done(v.tensor_tensor(R['pm0'][:, :], R['pm0'][:, :], R['kept'][:, :], ALU.add))
        v.tensor_scalar(K3['factor'][:, :], R['pm0'][:, :], k['gate'][0:T, 7:8], None, ALU.mult)

    extra = lambda m, R: R.update(kept=m.sb('route_kept', [T, B]), own=m.sb('route_own', [T, B]))
    route_block(nc, a, k, scratch, 'route3', 1, finish, extra)


TILES = CAP // T
PARTS = ((0, 3), (3, 5))
assert TILES * T == CAP and TILES == 5


def phase_experts_three(nc, a, k, scratch):
    with ExitStack() as stack:
        m = Machine(nc, stack, 'experts3')
        w1 = [m.sb(f'w1_{i}', [P, KD, F1]) for i in range(2)]
        w2 = [m.sb(f'w2_{i}', [P, KF, D]) for i in range(2)]
        rows = m.sb('rows3', [T, 2, TILES, D])
        xT = m.sb('xT3', [P, 2, KD, CAP])
        hT = m.sb('hT3', [P, 2, KF, CAP])
        y = m.sb('y3', [T, 2, TILES, D])
        x_ps = [m.ps(f'x3_ps{i}', [P, BANK]) for i in range(2)]
        h_ps = [m.ps(f'h3_ps{i}', [P, BANK]) for i in range(4)]
        o_ps = [m.ps(f'o3_ps{i}', [P, BANK]) for i in range(2)]

        def load(sync, i, e):
            sync.dma_start(w1[i][:, :, :], a['L3_ffn_W1'][bass.ds(e, 1), :, :]
                           .rearrange("o (c p) n -> p (o c) n", p=P)).then_inc(m.sem(f'w{i}'), 16)
            sync.dma_start(w2[i][:, :, :], a['L3_ffn_W2'][bass.ds(e, 1), :, :]
                           .rearrange("o (c p) n -> p (o c) n", p=P)).then_inc(m.sem(f'w{i}'), 16)

        with nc.Block() as block:
            @block.sync
            def _(sync):
                for i in range(2):
                    load(sync, i, i)
                for i in range(2):
                    sync.wait_ge(m.sem(f'w{i}'), 32)
        m.clear_all()

        with nc.Fori(0, E // 2) as g:
            with nc.Block() as block:
                @block.sync
                def _(sync):
                    for i in range(2):
                        sync.dma_start(rows[:, i, :, :], scratch['moe_x3'][bass.ds((g * 2 + i) * CAP, CAP), :]
                                       .rearrange("(j t) d -> t j d", t=T)).then_inc(m.sem(f'rows_in{i}'), 16)
                    for i in range(2):
                        sync.wait_ge(m.sem('out_done'), TILES * (i + 1))
                        load(sync, i, (g * 2 + i + 2) % E)
                        sync.wait_ge(m.sem('y_copied'), TILES * (i + 1))
                        sync.dma_start(scratch['moe_y3'][bass.ds((g * 2 + i) * CAP, CAP), :]
                                       .rearrange("(j t) d -> t j d", t=T), y[:, i, :, :]).then_inc(m.sem(f'y_out{i}'), 16)
                    for i in range(2):
                        sync.wait_ge(m.sem(f'w{i}'), 32)
                        sync.wait_ge(m.sem(f'y_out{i}'), 16)

                @block.tensor
                def _(pe):
                    def turn(i):
                        pe.wait_ge(m.sem(f'rows_in{i}'), 16)
                        for q, (t0, t1) in enumerate(PARTS):
                            for c in range(KD):
                                use = (i * 2 + q) * KD + c
                                if use >= 2:
                                    pe.wait_ge(m.sem('x_copied'), use - 1)
                                for t in range(t0, t1):
                                    tr = pe.transpose(x_ps[use % 2][:, (t - t0) * T:(t - t0 + 1) * T],
                                                      rows[:, i, t, c * P:(c + 1) * P], k['ident'][0:T, 0:T])
                                tr.then_inc(m.sem('x_turned'), 1)

                    def hidden(i):
                        for q, (t0, t1) in enumerate(PARTS):
                            pe.wait_ge(m.sem('x_copied'), (i * 2 + q + 1) * KD)
                            for f in range(KF):
                                use = (i * 2 + q) * KF + f
                                if use >= 4:
                                    pe.wait_ge(m.sem('h_copied'), use - 3)
                                for c in range(KD):
                                    mm = pe.matmul(h_ps[use % 4][:, 0:(t1 - t0) * T], w1[i][:, c, f * P:(f + 1) * P],
                                                   xT[:, i, c, t0 * T:t1 * T], start=(c == 0), stop=(c == KD - 1))
                                mm.then_inc(m.sem('hidden'), 1)

                    def output(i):
                        for t in range(TILES):
                            use = i * TILES + t
                            pe.wait_ge(m.sem('h_copied'), (i * 2 + (1 if t < PARTS[0][1] else 2)) * KF)
                            if use >= 2:
                                pe.wait_ge(m.sem('y_copied'), use - 1)
                            for f in range(KF):
                                mm = pe.matmul(o_ps[use % 2][0:T, 0:D], hT[:, i, f, t * T:(t + 1) * T],
                                               w2[i][:, f, :], start=(f == 0), stop=(f == KF - 1))
                            mm.then_inc(m.sem('out_done'), 1)

                    turn(0)
                    hidden(0)
                    turn(1)
                    output(0)
                    hidden(1)
                    output(1)

                @block.scalar
                def _(s):
                    for i in range(2):
                        for q, (t0, t1) in enumerate(PARTS):
                            for f in range(KF):
                                use = (i * 2 + q) * KF + f
                                s.wait_ge(m.sem('hidden'), use + 1)
                                s.activation(hT[:, i, f, t0 * T:t1 * T], h_ps[use % 4][:, 0:(t1 - t0) * T], ACT.Relu
                                             ).then_inc(m.sem('h_copied'), 1)

                @block.vector
                def _(v):
                    def copy_x(i):
                        for q, (t0, t1) in enumerate(PARTS):
                            for c in range(KD):
                                use = (i * 2 + q) * KD + c
                                v.wait_ge(m.sem('x_turned'), use + 1)
                                v.tensor_copy(xT[:, i, c, t0 * T:t1 * T], x_ps[use % 2][:, 0:(t1 - t0) * T]
                                              ).then_inc(m.sem('x_copied'), 1)

                    copy_x(0)
                    copy_x(1)
                    for use in range(2 * TILES):
                        v.wait_ge(m.sem('out_done'), use + 1)
                        v.tensor_copy(y[:, use // TILES, use % TILES, :], o_ps[use % 2][0:T, 0:D]
                                      ).then_inc(m.sem('y_copied'), 1)
            m.clear_all()


def phase_gather(nc, k, scratch, K3, out):
    with ExitStack() as stack:
        m = Machine(nc, stack, 'gather')
        x = m.sb('last_x', [T, LANES, D])
        y = m.sb('last_y', [T, LANES, D])
        index = m.sb('last_index', [T, LANES], U32)
        factor = m.sb('last_factor', [T, LANES])
        with nc.Fori(0, GROUPS) as g:
            with nc.Block() as block:
                @block.sync
                def _(sync):
                    for lane in range(LANES):
                        sync.dma_start(x[:, lane, :], scratch['x4'][bass.ds((g * LANES + lane) * T, T), :]
                                       ).then_inc(m.sem(f'x_in{lane}'), 16)
                    for lane in range(LANES):
                        sync.wait_ge(m.sem('final'), lane + 1)
                        sync.dma_start(out[bass.ds(g * LANES + lane, 1), :, :].rearrange("o t d -> (o t) d"),
                                       x[:, lane, :]).then_inc(m.sem('stored'), 16)
                    sync.wait_ge(m.sem('stored'), 16 * LANES)

                @block.vector
                def _(v):
                    v.tensor_copy(factor[:, :], K3['factor'][:, bass.ds(g * LANES, LANES)])
                    v.tensor_copy(index[:, :], K3['slot'][:, 0, bass.ds(g * LANES, LANES)]).then_inc(m.sem('indexed'), 1)
                    v.wait_ge(m.sem('indexed'), 1)
                    for lane in range(LANES):
                        v.wait_ge(m.sem(f'x_in{lane}'), 16)
                        v.wait_ge(k['pool_dma'][f'gathered{lane}'], (g + 1) * 16)
                        v.scalar_tensor_tensor(x[:, lane, :], y[:, lane, :], factor[:, lane:lane + 1], x[:, lane, :],
                                               ALU.mult, ALU.add).then_inc(m.sem('final'), 1)

                @block.gpsimd
                def _(gp):
                    gp.wait_ge(m.sem('indexed'), 1)
                    for lane in range(LANES):
                        gp.indirect_dma_start(y[:, lane, :], None, scratch['moe_y3'],
                                              bass.IndirectOffsetOnAxis(ap=index[:, lane:lane + 1], axis=0)
                                              ).then_inc(k['pool_dma'][f'gathered{lane}'], 16)
            m.clear_all()


def later_phases(nc, a, k, scratch, out):
    with ExitStack() as stack:
        m = Machine(nc, stack, 'keep2')
        K2 = {'slot': m.sb('slot2', [T, 2, B]), 'weight': m.sb('weight2', [T, 2, B]),
              'expert': m.sb('expert2', [1, NBLK], I32), 'row': m.sb('row2', [1, NBLK], I32),
              'one_hot': m.sb('one_hot2', [E, NBLK])}
        phase_route_two(nc, a, k, scratch, K2)
        phase_scatter(nc, k, scratch, scratch['moe_in'], scratch['moe_x2'], K2['slot'], K2['weight'], 2)
        phase_experts_two(nc, a, k, scratch, K2)
    phase_four(nc, a, k, scratch)
    with ExitStack() as stack:
        m = Machine(nc, stack, 'keep3')
        K3 = {'slot': m.sb('slot3', [T, 1, B]), 'factor': m.sb('factor3', [T, B])}
        phase_route_three(nc, a, k, scratch, K3)
        phase_scatter(nc, k, scratch, scratch['moe_y3'][E * CAP:, :], scratch['moe_x3'], K3['slot'], None, 1)
        phase_experts_three(nc, a, k, scratch)
        phase_gather(nc, k, scratch, K3, out)



def build(nc, a, out):
    scratch = {}
    for name, shape in (('turned', [B, D, T]), ('x2', [TOKENS, D]), ('res2', [TOKENS, D]),
                        ('moe_in', [TOKENS, D]), ('route2', [TOKENS, E]),
                        ('moe_x2', [NBLK * BLK, D + 1]), ('x3', [TOKENS, D]), ('x4', [TOKENS, D]),
                        ('route3', [TOKENS, E]), ('moe_x3', [E * CAP + TOKENS, D]),
                        ('moe_y3', [E * CAP + TOKENS, D])):
        scratch[name] = nc.dram_tensor('scratch_' + name, shape, F32).ap()
    with ExitStack() as stack:
        m = Machine(nc, stack, 'all')
        k = {'ident': m.sb('ident', [P, P]), 'tri': m.sb('tri', [P, P]), 'ones': m.sb('ones', [P, P]),
             'ident16': m.sb('ident16', [P, P], BF16), 'minus_half': m.sb('minus_half', [P, LANES]),
             'gate': m.sb('gate', [P, 8]), 'g_xattn': a['g_xattn'], 'g_ffn': a['g_ffn']}
        pool = Machine(nc, stack, 'pool')
        k['pool_dma'] = {name: pool.sem(name) for name in
                         ['scattered1', 'scattered2'] + [f'gathered{lane}' for lane in range(LANES)]}
        make_constants(nc, m, k)
        phase_one(nc, a, k, scratch)
        later_phases(nc, a, k, scratch, out)


_TURNED = {'w_gateT': 'L0_ffn_w_gate', 'w_upT': 'L0_ffn_w_up', 'w_downT': 'L0_ffn_w_down',
           'WkT1': 'L1_xattn_Wk', 'w1T': 'L1_ffn_w1', 'w2T': 'L1_ffn_w2', 'WT2': 'L2_xattn_W',
           'WqT3': 'L3_xattn_Wq', 'WvT3': 'L3_xattn_Wv'}


def kernel(**inputs):
    import numpy as np
    import concourse.bacc as bacc
    from concourse import mybir as mb
    from concourse.bass_utils import run_bass_kernel_spmd as run
    nc = bacc.Bacc("TRN2", target_bir_lowering=False, num_devices=1)
    host = {name: v for name, v in inputs.items() if name not in _TURNED.values()}
    for name, src in _TURNED.items():
        host[name] = np.asarray(inputs[src]).T
    arrays, args = {}, {}
    for name, v in host.items():
        v = np.ascontiguousarray(v)
        arrays[f"in_{name}_dram"] = v
        args[name] = nc.dram_tensor(f"in_{name}_dram", v.shape, mb.dt.from_np(v.dtype),
                                    kind="ExternalInput").ap()
    out = nc.dram_tensor("out_0_dram", (B, T, D), mb.dt.from_np(np.dtype('float32')),
                         kind="ExternalOutput").ap()
    build(nc, args, out)
    r = run(nc, [arrays], core_ids=[0])
    return r.results[0]["out_0_dram"]
```

```python
from contextlib import ExitStack

import concourse.bass as bass
from concourse import mybir

ALU = mybir.AluOpType
ACT = mybir.ActivationFunctionType
F32 = mybir.dt.float32
BF16 = mybir.dt.bfloat16
I32 = mybir.dt.int32
U32 = mybir.dt.uint32
AX = mybir.AxisListType

P = 128
B, T, D, S_CTX = 32, 112, 256, 375
TOKENS = B * T
KD = D // P
SC, NSC = 125, 3
H0 = 768
F1 = 1024
KF = F1 // P
HEADS, HD = 16, 16
CH = P // HD
E = 8
LANES = 4
GROUPS = B // LANES
BANK = 512
EPS = 1e-5
INT8_SCALE = 1.0 / 127.0
MAGIC = 12582912.0
NEG = -1e9
MINUS_BIG = -3.0e38
CAP = int(1.25 * TOKENS / E)
BLK = 128
NBLK = (2 * TOKENS) // BLK + E - 1


class Machine:

    def __init__(self, nc, stack, phase):
        self.nc, self.stack, self.phase, self.sems = nc, stack, phase, {}

    def sb(self, name, shape, dt=F32):
        return self.stack.enter_context(self.nc.sbuf_tensor(f'{self.phase}_{name}', shape, dt))

    def ps(self, name, shape, dt=F32):
        return self.stack.enter_context(self.nc.psum_tensor(f'{self.phase}_{name}', shape, dt))

    def sem(self, name):
        if name not in self.sems:
            self.sems[name] = self.stack.enter_context(self.nc.semaphore(f'{self.phase}_{name}'))
        return self.sems[name]

    def clear_all(self):
        sems = list(self.sems.values())
        with self.nc.Block() as block:
            @block.sync
            def _(sync):
                for s in sems:
                    sync.sem_clear(s)


class Lanes:

    def __init__(self, m, prefix, lanes, first):
        self.m, self.prefix, self.lanes, self.first = m, prefix, lanes, first

    def sem(self, name):
        return self.m.sem(self.prefix + name)

    def n(self, i, lane):
        return len(self.lanes) * i + self.lanes.index(lane) + 1

    def batch(self, lane):
        return self.first + lane


def weave(*programs):
    heads = [[next(program), program] for program in programs]
    while heads:
        heads.sort(key=lambda head: head[0])
        position, program = heads[0]
        heads[0][0] = next(program, None)
        if heads[0][0] is None:
            heads.pop(0)



def make_constants(nc, m, k):
    with nc.Block() as block:
        @block.gpsimd
        def _(g):
            g.memset(k['ones'][:, :], 1.0).then_inc(m.sem('ones_set'), 1)
            g.memset(k['minus_half'][:, :], -0.5)
            g.wait_ge(m.sem('ones_set'), 1)
            g.affine_select(k['ident'][:, :], k['ones'][:, :], [[-1, P]], ALU.is_equal, 0.0,
                            base=0, channel_multiplier=1).then_inc(m.sem('ident_set'), 1)
            g.affine_select(k['tri'][:, :], k['ones'][:, :], [[1, P]], ALU.is_ge, 0.0,
                            base=0, channel_multiplier=-1).then_inc(m.sem('ident_set'), 1)

        @block.vector
        def _(v):
            v.wait_ge(m.sem('ident_set'), 2)
            v.tensor_copy(k['ident16'][:, :], k['ident'][:, :])
            v.memset(k['ones16'][:, :], 1.0)

        @block.sync
        def _(sync):
            sync.dma_start(k['gate'][:, 0:4], k['g_xattn'].partition_broadcast(P)).then_inc(m.sem('gates'), 16)
            sync.dma_start(k['gate'][:, 4:8], k['g_ffn'].partition_broadcast(P)).then_inc(m.sem('gates'), 16)

        @block.scalar
        def _(s):
            s.wait_ge(m.sem('gates'), 32)
            s.activation(k['gate'][:, :], k['gate'][:, :], ACT.Tanh).then_inc(m.sem('gates_tanh'), 1)
    m.clear_all()


def split_three(v, m, i, src, parts):
    step = 4 * i
    for j in range(3):
        v.tensor_copy(parts[j], src).then_inc(m.sem('split_step' if j < 2 else 'split'), 1)
        if j < 2:
            v.wait_ge(m.sem('split_step'), step + 2 * j + 1)
            v.tensor_tensor(src, src, parts[j], ALU.subtract).then_inc(m.sem('split_step'), 1)
            v.wait_ge(m.sem('split_step'), step + 2 * j + 2)



def norm_stats(v, m, L, i, src_of, ready_of):
    for lane in m.lanes:
        src = src_of(lane)
        if ready_of is not None:
            v.wait_ge(*ready_of(lane))
        width = src.shape[1]
        parts = max(1, width // BANK)
        for j in range(parts):
            w = width // parts
            stats = v.bn_stats(L['stats'][:, lane, 6 * j:6 * j + 6], src[:, j * w:(j + 1) * w])
        stats.then_inc(m.sem('norm_stats'), 1)
    for lane in m.lanes:
        width = src_of(lane).shape[1]
        parts = max(1, width // BANK)
        v.wait_ge(m.sem('norm_stats'), m.n(i, lane))
        v.bn_aggr(L['mv'][:, lane, :], L['stats'][:, lane, 0:6 * parts]).then_inc(m.sem('norm_aggr'), 1)


def norm_apply(v, m, L, i, src_of, dst_of):
    for lane in m.lanes:
        v.wait_ge(m.sem('norm_rstd'), m.n(i, lane))
        v.tensor_scalar(dst_of(lane), src_of(lane), L['mv'][:, lane, 0:1], L['rstd'][:, lane, 0:1],
                        ALU.subtract, ALU.mult).then_inc(m.sem('norm_out'), 1)


def norm_rstd(g, m, L, i, minus_half):
    for lane in m.lanes:
        g.wait_ge(m.sem('norm_aggr'), m.n(i, lane))
        g.tensor_scalar(L['var'][:, lane, 0:1], L['mv'][:, lane, 1:2], EPS, None,
                        ALU.add).then_inc(m.sem('norm_var'), 1)
        g.wait_ge(m.sem('norm_var'), m.n(i, lane))
        g.tensor_tensor(L['rstd'][:, lane, 0:1], L['var'][:, lane, 0:1], minus_half,
                        ALU.pow).then_inc(m.sem('norm_rstd'), 1)


def turn_rows(pe, m, k, L, i, src_of, ready_of):
    for lane in m.lanes:
        pe.wait_ge(*ready_of(lane))
        src = src_of(lane)
        for c in range(KD):
            t = pe.transpose(L['ps'][lane][:, c * T:(c + 1) * T], src[:, c * P:(c + 1) * P],
                             k['ident'][0:T, 0:T])
        t.then_inc(m.sem('turned'), 1)


def project_t(pe, m, L, w, src_of, ready_of, bank, done):
    for lane in m.lanes:
        pe.wait_ge(*ready_of(lane))
        for o in range(KD):
            for c in range(KD):
                mm = pe.matmul(L['ps'][lane][:, bank * BANK + o * T:bank * BANK + (o + 1) * T],
                               w[:, c, o * P:(o + 1) * P], src_of(lane)[:, c * T:(c + 1) * T],
                               start=(c == 0), stop=(c == KD - 1))
        mm.then_inc(m.sem(done), 1)


def rows_out(pe, L, lane, w, lhs, chunks, bank, width, bias=None, ones=None, stop=True):
    out = L['ps'][lane][0:T, bank * BANK:bank * BANK + width]
    for c in range(chunks):
        mm = pe.matmul(out, lhs[:, c * T:(c + 1) * T], w[:, c, :], start=(c == 0),
                       stop=(c == chunks - 1 and bias is None))
    if bias is not None:
        mm = pe.matmul(out, ones[0:3, 0:T], bias, start=False, stop=True)
    return mm


def attention_scores(pe, m, L, i, q_of, ready_of):
    for lane in m.lanes:
        pe.wait_ge(*ready_of(lane))
        for c in range(KD):
            mm = pe.matmul(L['ps'][lane][0:T, BANK:BANK + S_CTX], q_of(lane)[:, c * T:(c + 1) * T],
                           L['ctxT'][:, lane, c, :], start=(c == 0), stop=(c == KD - 1))
        mm.then_inc(m.sem('scores'), 1)


def attention_logits(v, m, L, i, scale, mask_of, mask_ready):
    for lane in m.lanes:
        v.wait_ge(m.sem('scores'), m.n(i, lane))
        v.wait_ge(*mask_ready(lane))
        v.scalar_tensor_tensor(L['wide'][0:T, lane, 0:S_CTX], L['ps'][lane][0:T, BANK:BANK + S_CTX], scale,
                               mask_of(lane), ALU.mult, ALU.add).then_inc(m.sem('logits'), 1)
    for lane in m.lanes:
        v.wait_ge(m.sem('logits'), m.n(i, lane))
        v.tensor_reduce(L['nmax'][:, lane, 0:1], L['wide'][0:T, lane, 0:S_CTX], AX.X, ALU.max,
                        negate=True).then_inc(m.sem('row_max'), 1)


def attention_exp(s, m, L, i, from_psum=False):
    for lane in m.lanes:
        s.wait_ge(m.sem('row_max'), m.n(i, lane))
        logits = L['ps'][lane][0:T, BANK:BANK + S_CTX] if from_psum else L['wide'][0:T, lane, 0:S_CTX]
        s.activation(L['wide'][0:T, lane, 384:384 + S_CTX], logits, ACT.Exp,
                     bias=L['nmax'][:, lane, 0:1], scale=1.0,
                     accum_out=L['sum'][:, lane, 0:1]).then_inc(m.sem('probs'), 1)


def attention_norm(v, m, L, i, gate=None):
    for lane in m.lanes:
        v.wait_ge(m.sem('probs'), m.n(i, lane))
        v.reciprocal(L['rsum'][:, lane, 0:1], L['sum'][:, lane, 0:1]).then_inc(m.sem('rsum'), 1)
    for lane in m.lanes:
        v.wait_ge(m.sem('rsum'), m.n(i, lane))
        if gate is not None:
            v.tensor_scalar(L['factor'][:, lane, 0:1], L['rsum'][:, lane, 0:1], gate, None,
                            ALU.mult).then_inc(m.sem('factor'), 1)
        else:
            p = L['wide'][0:T, lane, 384:384 + S_CTX]
            v.tensor_scalar(p, p, L['rsum'][:, lane, 0:1], None, ALU.mult).then_inc(m.sem('probs_normed'), 1)


def turn_probs(pe, m, k, L, i, ready_of):
    for lane in m.lanes:
        pe.wait_ge(*ready_of(lane))
        for c in range(NSC):
            t = pe.transpose(L['ps'][lane][0:SC, c * T:(c + 1) * T],
                             L['wide'][0:T, lane, 384 + c * SC:384 + (c + 1) * SC], k['ident'][0:T, 0:T])
        t.then_inc(m.sem('probs_turned'), 1)


def copy_probs(s, m, L, i):
    for lane in m.lanes:
        s.wait_ge(m.sem('probs_turned'), m.n(i, lane))
        s.activation(L['mid'][0:SC, lane, 0:NSC * T], L['ps'][lane][0:SC, 0:NSC * T],
                     ACT.Copy).then_inc(m.sem('probs_copied'), 1)


def attend_rows(pe, m, L, i):
    for lane in m.lanes:
        pe.wait_ge(m.sem('probs_copied'), m.n(i, lane))
        for c in range(NSC):
            mm = pe.matmul(L['ps'][lane][0:T, BANK:BANK + D], L['mid'][0:SC, lane, c * T:(c + 1) * T],
                           L['ctx'][:, lane, c, :], start=(c == 0), stop=(c == NSC - 1))
        mm.then_inc(m.sem('attended'), 1)


def attend_t(pe, m, L, i):
    for lane in m.lanes:
        pe.wait_ge(m.sem('probs_copied'), m.n(i, lane))
        for o in range(KD):
            for c in range(NSC):
                mm = pe.matmul(L['ps'][lane][:, BANK + o * T:BANK + (o + 1) * T],
                               L['ctx'][:, lane, c, o * P:(o + 1) * P],
                               L['mid'][0:SC, lane, c * T:(c + 1) * T],
                               start=(c == 0), stop=(c == NSC - 1))
        mm.then_inc(m.sem('attended'), 1)


def copy_t(s, m, L, src_bank, dst_of, ready_of, done, scale=None, bias=None):
    for lane in m.lanes:
        s.wait_ge(*ready_of(lane))
        src = L['ps'][lane][:, src_bank * BANK:src_bank * BANK + KD * T]
        if bias is None:
            s.activation(dst_of(lane), src, ACT.Copy).then_inc(m.sem(done), 1)
            continue
        for c in range(KD):
            last = s.activation(dst_of(lane)[:, c * T:(c + 1) * T], src[:, c * T:(c + 1) * T], ACT.Identity,
                                bias=bias[:, c:c + 1], scale=1.0 if scale is None else scale[:, c:c + 1])
        last.then_inc(m.sem(done), 1)


def turn_context(pe, m, k, L):
    for lane in m.lanes:
        for c in range(KD):
            for j in range(NSC):
                t = pe.transpose(L['ps'][lane][:, c * BANK + j * SC:c * BANK + (j + 1) * SC],
                                 L['ctx'][:, lane, j, c * P:(c + 1) * P], k['ident'][0:SC, 0:SC])
        t.then_inc(m.sem('ctx_turned'), 1)


def copy_context(s, m, L):
    for lane in m.lanes:
        s.wait_ge(m.sem('ctx_turned'), m.n(0, lane))
        for c in range(KD):
            last = s.activation(L['ctxT'][:, lane, c, :], L['ps'][lane][:, c * BANK:c * BANK + S_CTX], ACT.Copy)
        last.then_inc(m.sem('ctx_copied'), 1)


def load_context(sync, m, L, ctx_in, first, sems):
    for lane in range(LANES):
        sync.dma_start(L['ctx'][:, lane, :, :],
                       ctx_in[bass.ds(first + lane, 1), :, :].rearrange("o (c p) d -> p (o c) d", p=SC)
                       ).then_inc(m.sem(f'{sems}{lane}'), 16)


def lane_buffers(m, names_widths):
    L = {name: m.sb('lane_' + name, [rows, LANES, *width], F32) for name, rows, width in names_widths}
    L['ps'] = [m.ps(f'lane_ps{lane}', [P, 2 * BANK]) for lane in range(LANES)]
    return L


def pick(L, name):
    return lambda lane: L[name][:, lane, :]


def after(h, name, i=0):
    return lambda lane: (h.sem(name), h.n(i, lane))



def front_sync(sync, h, a, k, W, L, scratch):
    yield 0
    for lane in h.lanes:
        b = h.batch(lane)
        sync.dma_start(L['x'][:, lane, :], a['x'][bass.ds(b, 1), :, :].rearrange("o t d -> (o t) d")
                       ).then_inc(h.sem(f'x_in{lane}'), 16)
        sync.dma_start(L['mid'][0:T, lane, 0:S_CTX].bitcast(I32),
                       a['mask_Bx1xS2_ik0'][bass.ds(b, 1), :, :].rearrange("o u s -> (o u) s")
                       .broadcast_to([T, S_CTX])).then_inc(h.sem(f'mask_in{lane}'), 16)
    yield 282
    for lane in h.lanes:
        sync.wait_ge(h.sem('v1'), h.n(0, lane))
        sync.dma_start(scratch['turned'][bass.ds(h.batch(lane), 1), :, :].rearrange("o (c p) t -> p (o c) t", p=P),
                       L['hT'][:, lane, :].rearrange("p (c t) -> p c t", c=KD)
                       ).then_inc(h.sem(f'turned_out{lane}'), 16)
    yield 290
    for lane in h.lanes:
        sync.wait_ge(h.sem(f'turned_out{lane}'), 16)
        sync.dma_start(L['u'][:, lane, :],
                       scratch['turned'][bass.ds(h.batch(lane), 1), :, :].rearrange("o p t -> (o p t)")
                       .rearrange("(i j) -> i j", j=D)).then_inc(h.sem(f'turned_in{lane}'), 16)


def front_tensor(pe, h, a, k, W, L, scratch):
    yield 0
    turn_context(pe, h, k, L)
    yield 24
    for lane in h.lanes:
        pe.wait_ge(h.sem('ctx_copied'), h.n(0, lane))
    turn_rows(pe, h, k, L, 0, pick(L, 'xh'), after(h, 'norm_out', 0))
    yield 30
    attention_scores(pe, h, L, 0, pick(L, 'hT'), after(h, 'turned_copied', 0))
    yield 55
    turn_probs(pe, h, k, L, 0, after(h, 'probs', 0))
    yield 60
    attend_rows(pe, h, L, 0)
    yield 87
    turn_rows(pe, h, k, L, 1, pick(L, 'xh'), after(h, 'norm_out', 1))
    for r in range(2):
        yield 92 + 40 * r
        for lane in h.lanes:
            pe.wait_ge(h.sem('turned_copied'), h.n(1, lane))
            if r:
                pe.wait_ge(h.sem('hidden0'), h.n(0, lane))
            for bank, w in enumerate((W['w_gateT'], W['w_upT'])):
                for j in range(3):
                    for c in range(KD):
                        o = (3 * r + j) * P
                        mm = pe.matmul(L['ps'][lane][:, bank * BANK + j * T:bank * BANK + (j + 1) * T],
                                       w[:, c, o:o + P], L['hT'][:, lane, c * T:(c + 1) * T],
                                       start=(c == 0), stop=(c == KD - 1))
            mm.then_inc(h.sem('gate_up'), 1)
    yield 164
    for lane in h.lanes:
        pe.wait_ge(h.sem('hidden0'), h.n(1, lane))
        rows_out(pe, L, lane, W['w_downT'], L['block'][:, lane, :], H0 // P, 0, D).then_inc(h.sem('down0'), 1)
    yield 195
    turn_rows(pe, h, k, L, 2, pick(L, 'xh'), after(h, 'norm_out', 2))
    yield 204
    project_t(pe, h, L, W['Wq1'], pick(L, 'hT'), after(h, 'turned_copied', 2), 0, 'q1_raw')
    yield 218
    for lane in h.lanes:
        pe.wait_ge(h.sem('q1'), h.n(0, lane))
        for o in range(KD):
            for c in range(KD):
                pe.matmul(L['ps'][lane][:, BANK + o * T:BANK + (o + 1) * T], W['WkT1'][:, c, o * P:(o + 1) * P],
                          L['qT'][:, lane, c * T:(c + 1) * T], start=(c == 0), stop=(c == KD - 1))
        for c in range(KD):
            mm = pe.matmul(L['ps'][lane][0:T, BANK + KD * T:BANK + KD * T + 1],
                           L['qT'][:, lane, c * T:(c + 1) * T], W['bk1'][:, c:c + 1],
                           start=(c == 0), stop=(c == KD - 1))
        mm.then_inc(h.sem('key_q1'), 1)
    yield 232
    attention_scores(pe, h, L, 1, pick(L, 'hT'), after(h, 'key_q1_copied'))
    yield 256
    turn_probs(pe, h, k, L, 1, after(h, 'probs_normed', 0))
    yield 264
    attend_t(pe, h, L, 1)
    yield 276
    project_t(pe, h, L, W['Wv1'], pick(L, 'qT'), after(h, 'attended_copied'), 0, 'v1_raw')
    yield 300
    turn_rows(pe, h, k, L, 3, pick(L, 'u'), lambda lane: (h.sem(f'turned_in{lane}'), 16))
    yield 306
    for lane in h.lanes:
        pe.wait_ge(h.sem('turned_copied'), h.n(3, lane))
        rows_out(pe, L, lane, W['Wo1'], L['qT'][:, lane, :], KD, 1, D, W['bo1'], k['ones16']
                 ).then_inc(h.sem('o1'), 1)


def front_scalar(s, h, a, k, W, L, scratch):
    yield 2
    copy_context(s, h, L)
    yield 25
    copy_t(s, h, L, 0, pick(L, 'hT'), after(h, 'turned', 0), 'turned_copied')
    yield 52
    attention_exp(s, h, L, 0)
    yield 57
    copy_probs(s, h, L, 0)
    yield 88
    copy_t(s, h, L, 0, pick(L, 'hT'), after(h, 'turned', 1), 'turned_copied')
    for r in range(2):
        yield 105 + 31 * r
        for lane in h.lanes:
            s.wait_ge(h.sem('gate_up'), h.n(r, lane))
            s.activation(L['mid'][:, lane, 0:3 * T], L['ps'][lane][:, 0:3 * T], ACT.Tanh,
                         scale=INT8_SCALE / 2).then_inc(h.sem('gate_tanh'), 1)
    yield 196
    copy_t(s, h, L, 0, pick(L, 'hT'), after(h, 'turned', 2), 'turned_copied')
    yield 207
    copy_t(s, h, L, 0, pick(L, 'qT'), after(h, 'q1_raw'), 'q1', scale=W['qscale1'], bias=W['bq1s'])
    yield 222
    for lane in h.lanes:
        s.wait_ge(h.sem('key_q1'), h.n(0, lane))
        s.activation(L['hT'][:, lane, :], L['ps'][lane][:, BANK:BANK + KD * T], ACT.Copy)
        s.activation(L['row'][:, lane, :], L['ps'][lane][0:T, BANK + KD * T:BANK + KD * T + 1],
                     ACT.Copy).then_inc(h.sem('key_q1_copied'), 1)
    yield 247
    attention_exp(s, h, L, 1, from_psum=True)
    yield 257
    copy_probs(s, h, L, 1)
    yield 267
    copy_t(s, h, L, 1, pick(L, 'qT'), after(h, 'attended', 1), 'attended_copied')
    yield 281
    copy_t(s, h, L, 0, pick(L, 'hT'), after(h, 'v1_raw'), 'v1', bias=W['bv1'])
    yield 301
    copy_t(s, h, L, 0, pick(L, 'qT'), after(h, 'turned', 3), 'turned_copied')


def front_gpsimd(gp, h, a, k, W, L, scratch):
    yield 1
    for lane in h.lanes:
        gp.wait_ge(h.sem(f'mask_in{lane}'), 16)
        gp.tensor_scalar(L['mask'][:, lane, :], L['mid'][0:T, lane, 0:S_CTX].bitcast(I32), NEG, None,
                         ALU.mult).then_inc(h.sem('mask_ready'), 1)
    for i, position in enumerate((19, 83, 192)):
        yield position
        norm_rstd(gp, h, L, i, k['minus_half'][0:T, 0:1])


def update(v, h, L, bank, factor_of, done_sem, use):
    for lane in h.lanes:
        v.wait_ge(h.sem(done_sem), h.n(use, lane))
        v.scalar_tensor_tensor(L['x'][:, lane, :], L['ps'][lane][0:T, bank * BANK:bank * BANK + D],
                               factor_of(lane), L['x'][:, lane, :], ALU.mult,
                               ALU.add).then_inc(h.sem('x_updated'), 1)


def front_vector(v, h, a, k, W, L, scratch):
    gate = k['gate']
    x, xh = pick(L, 'x'), pick(L, 'xh')
    yield 3
    norm_stats(v, h, L, 0, x, lambda lane: (h.sem(f'x_in{lane}'), 16))
    yield 22
    norm_apply(v, h, L, 0, x, xh)
    yield 44
    attention_logits(v, h, L, 0, D ** -0.5, pick(L, 'mask'), after(h, 'mask_ready'))
    yield 54
    attention_norm(v, h, L, 0, gate[0:T, 0:1])
    yield 75
    for lane in h.lanes:
        v.wait_ge(h.sem('factor'), h.n(0, lane))
    update(v, h, L, 1, lambda lane: L['factor'][:, lane, 0:1], 'attended', 0)
    yield 79
    norm_stats(v, h, L, 1, x, after(h, 'x_updated', 0))
    yield 86
    norm_apply(v, h, L, 1, x, xh)
    for r in range(2):
        yield 106 + 31 * r
        for lane in h.lanes:
            v.wait_ge(h.sem('gate_tanh'), h.n(r, lane))
            v.scalar_tensor_tensor(L['wide'][:, lane, 0:3 * T], L['mid'][:, lane, 0:3 * T], 1.0,
                                   L['ps'][lane][:, 0:3 * T], ALU.add, ALU.mult
                                   ).then_inc(h.sem('gate_silu'), 1)
        for lane in h.lanes:
            v.wait_ge(h.sem('gate_silu'), h.n(r, lane))
            v.scalar_tensor_tensor(L['block'][:, lane, r * 3 * T:(r + 1) * 3 * T],
                                   L['ps'][lane][:, BANK:BANK + 3 * T], INT8_SCALE * INT8_SCALE / 2,
                                   L['wide'][:, lane, 0:3 * T], ALU.mult, ALU.mult).then_inc(h.sem('hidden0'), 1)
    yield 180
    update(v, h, L, 0, lambda lane: W['gate_int8'][0:T, 0:1], 'down0', 0)
    yield 188
    norm_stats(v, h, L, 2, x, after(h, 'x_updated', 1))
    yield 194
    norm_apply(v, h, L, 2, x, xh)
    yield 239
    for lane in h.lanes:
        v.wait_ge(h.sem('scores'), h.n(1, lane))
        v.tensor_reduce(L['nmax'][:, lane, 0:1], L['ps'][lane][0:T, BANK:BANK + S_CTX], AX.X, ALU.max,
                        negate=True).then_inc(h.sem('score_max'), 1)
    for lane in h.lanes:
        v.wait_ge(h.sem('score_max'), h.n(0, lane))
        v.tensor_scalar(L['nmax'][:, lane, 0:1], L['nmax'][:, lane, 0:1], L['row'][:, lane, 0:1],
                        L['row'][:, lane, 0:1], ALU.subtract, ALU.add).then_inc(h.sem('row_max'), 1)
    yield 250
    attention_norm(v, h, L, 1)
    yield 315
    update(v, h, L, 1, lambda lane: gate[0:T, 1:2], 'o1', 0)



def back_sync(sync, h, a, k, W, L, scratch):
    yield 146
    for lane in h.lanes:
        b = h.batch(lane)
        sync.wait_ge(h.sem('x_updated'), h.n(1, lane))
        sync.dma_start(scratch['x2'][bass.ds(b * T, T), :], L['x'][:, lane, :]
                       ).then_inc(h.sem(f'x_out{lane}'), 16)
        sync.dma_start(L['ctx'][:, lane, :, :],
                       a['ctx_1024'][bass.ds((b + LANES) % B, 1), :, :]
                       .rearrange("o (c p) d -> p (o c) d", p=SC)).then_inc(h.sem(f'ctx{lane}'), 16)
    for position, ready, name, tile in ((295, 'res2', 'res2', 'xh'), (310, 'moe_bias', 'moe_in', 'u'),
                                        (318, 'route_copied', 'route2', 'logit')):
        yield position
        for lane in h.lanes:
            sync.wait_ge(h.sem(ready), h.n(0, lane))
            sync.dma_start(scratch[name][bass.ds(h.batch(lane) * T, T), :], L[tile][:, lane, :]
                           ).then_inc(h.sem(f'{name}_out{lane}'), 16)
    yield 400
    for lane in h.lanes:
        for name in ['x_out', 'ctx', 'res2_out', 'moe_in_out', 'route2_out']:
            sync.wait_ge(h.sem(f'{name}{lane}'), 16)


def turn_quantised(pe, h, k, L, i, width):
    for lane in h.lanes:
        pe.wait_ge(h.sem('quant'), h.n(i, lane))
        q = L['block'][0:T, lane, 0:width // 2].bitcast(BF16)
        out = L['ps'][lane][:, 0:width // P * T // 2].bitcast(BF16)
        for c in range(width // P):
            t = pe.transpose(out[:, c * T:(c + 1) * T], q[:, c * P:(c + 1) * P], k['ident16'][0:T, 0:T])
        t.then_inc(h.sem('quant_turned'), 1)


def back_tensor(pe, h, a, k, W, L, scratch):
    yield 26
    turn_quantised(pe, h, k, L, 0, D)
    yield 30
    for lane in h.lanes:
        pe.wait_ge(h.sem('quant_copied'), h.n(0, lane))
        qT = L['mid'][:, lane, 0:KD * T // 2].bitcast(BF16)
        for o in range(2):
            for c in range(KD):
                mm = pe.matmul(L['ps'][lane][0:T, o * BANK:(o + 1) * BANK], qT[:, c * T:(c + 1) * T],
                               W['w1q'][:, c, o * BANK:(o + 1) * BANK], start=(c == 0), stop=(c == KD - 1))
        mm.then_inc(h.sem('hidden1_raw'), 1)
    yield 88
    turn_quantised(pe, h, k, L, 1, F1)
    yield 93
    for lane in h.lanes:
        pe.wait_ge(h.sem('quant_copied'), h.n(1, lane))
        rows_out(pe, L, lane, W['w2q'], L['mid'][:, lane, 0:KF * T // 2].bitcast(BF16), KF, 1, D
                 ).then_inc(h.sem('ffn1_raw'), 1)
    yield 107
    turn_rows(pe, h, k, L, 0, pick(L, 'xh'), after(h, 'norm_out', 2))
    yield 111
    project_t(pe, h, L, W['WT2'], pick(L, 'hT'), after(h, 'turned_copied', 0), 0, 'q2_raw')
    yield 118
    attention_scores(pe, h, L, 0, pick(L, 'qT'), after(h, 'q2'))
    yield 130
    turn_probs(pe, h, k, L, 0, after(h, 'probs', 0))
    yield 134
    attend_rows(pe, h, L, 0)
    yield 158
    turn_rows(pe, h, k, L, 1, pick(L, 'u'), after(h, 'norm_out', 4))
    yield 163
    for lane in h.lanes:
        pe.wait_ge(h.sem('turned_copied'), h.n(1, lane))
        hT = L['hT'][:, lane, :]
        for bank in range(2):
            for o in range(KD):
                for c in range(KD):
                    pe.matmul(L['ps'][lane][:, bank * BANK + o * T:bank * BANK + (o + 1) * T],
                              W['w_qkv'][:, c, bank * D + o * P:bank * D + (o + 1) * P],
                              hT[:, c * T:(c + 1) * T], start=(c == 0), stop=(c == KD - 1))
        v_out = L['ps'][lane][0:T, D:2 * D]
        for c in range(KD):
            pe.matmul(v_out, hT[:, c * T:(c + 1) * T], W['w_qkv'][:, c, 2 * D:3 * D], start=(c == 0), stop=False)
        pe.matmul(v_out, k['ones16'][0:3, 0:T], W['bv2'], start=False, stop=True).then_inc(h.sem('qkv'), 1)
    for c in range(KD):
        yield 182 + 24 * c
        for lane in h.lanes:
            pe.wait_ge(h.sem('key_blocks'), h.n(c, lane))
            if c:
                pe.wait_ge(h.sem('self_shifted'), h.n(0, lane))
            for bank in range(2):
                out = L['ps'][lane][0:T, bank * BANK:bank * BANK + 4 * T]
                pe.matmul(out, k['ident16'][0:T, 0:T], W['causal16'][:, :], start=True, stop=False)
                mm = pe.matmul(out, L['qT'][:, lane, c * T:(c + 1) * T],
                               L['block'][:, lane, bank * 4 * T:(bank + 1) * 4 * T], start=False, stop=True)
            mm.then_inc(h.sem('self_scores'), 1)
    for r in range(HEADS // 4):
        yield 222 + 15 * r
        for lane in h.lanes:
            pe.wait_ge(h.sem('self_probs'), h.n(r // 2, lane))
            if r:
                pe.wait_ge(h.sem('self_copied'), h.n(r - 1, lane))
            else:
                pe.wait_ge(h.sem('self_shifted'), h.n(1, lane))
            for j in range(4):
                t = pe.transpose(L['ps'][lane][0:T, j * T:(j + 1) * T],
                                 L['wide'][0:T, lane, (4 * r + j) * T:(4 * r + j + 1) * T], k['ident'][0:T, 0:T])
            t.then_inc(h.sem('self_turned'), 1)
        yield 230 + 15 * r
        for lane in h.lanes:
            pe.wait_ge(h.sem('self_copied'), h.n(r, lane))
            for j in range(4 * r, 4 * r + 4):
                mm = pe.matmul(L['ps'][lane][0:T, BANK + j * (HD + 1):BANK + (j + 1) * (HD + 1)],
                               L['mid'][0:T, lane, (j % 8) * T:(j % 8 + 1) * T],
                               L['mask'][:, lane, j * (HD + 1):(j + 1) * (HD + 1)], start=True, stop=True)
            mm.then_inc(h.sem('self_out'), 1)
    yield 284
    turn_rows(pe, h, k, L, 2, pick(L, 'u'), after(h, 'self_normed'))
    yield 288
    for lane in h.lanes:
        pe.wait_ge(h.sem('turned_copied'), h.n(2, lane))
        rows_out(pe, L, lane, W['w_proj'], L['hT'][:, lane, :], KD, 1, D, W['b_proj'], k['ones16']
                 ).then_inc(h.sem('self_proj'), 1)
    yield 306
    turn_rows(pe, h, k, L, 3, pick(L, 'u'), after(h, 'moe_bias'))
    yield 309
    for lane in h.lanes:
        pe.wait_ge(h.sem('turned_copied'), h.n(3, lane))
        rows_out(pe, L, lane, W['w_route'], L['hT'][:, lane, :], KD, 1, E, W['b_route'], k['ones16']
                 ).then_inc(h.sem('route'), 1)


def back_scalar(s, h, a, k, W, L, scratch):
    for i, (width, position) in enumerate(((D, 27), (F1, 89))):
        if i:
            yield 34
            for lane in h.lanes:
                s.wait_ge(h.sem('hidden1'), h.n(0, lane))
                s.activation(L['wide'][0:T, lane, 0:F1], L['wide'][0:T, lane, 0:F1], ACT.Gelu
                             ).then_inc(h.sem('gelu1'), 1)
            yield 52
            for lane in h.lanes:
                s.wait_ge(h.sem('norm_shift'), h.n(0, lane))
                s.activation(L['wide'][0:T, lane, 0:F1], L['wide'][0:T, lane, 0:F1], ACT.Identity,
                             bias=L['shift'][:, lane, 0:1], scale=L['rstd'][:, lane, 0:1]
                             ).then_inc(h.sem('hidden1_normed'), 1)
        yield position
        for lane in h.lanes:
            s.wait_ge(h.sem('quant_turned'), h.n(i, lane))
            s.activation(L['mid'][:, lane, 0:width // P * T // 2].bitcast(BF16),
                         L['ps'][lane][:, 0:width // P * T // 2].bitcast(BF16), ACT.Copy
                         ).then_inc(h.sem('quant_copied'), 1)
    yield 108
    copy_t(s, h, L, 0, pick(L, 'hT'), after(h, 'turned', 0), 'turned_copied')
    yield 114
    copy_t(s, h, L, 0, pick(L, 'qT'), after(h, 'q2_raw'), 'q2', bias=W['b2x'])
    yield 129
    attention_exp(s, h, L, 0, from_psum=True)
    yield 132
    copy_probs(s, h, L, 0)
    yield 159
    copy_t(s, h, L, 0, pick(L, 'hT'), after(h, 'turned', 1), 'turned_copied', scale=W['ln1_scale'],
           bias=W['ln1_bias'])
    yield 171
    for lane in h.lanes:
        s.wait_ge(h.sem('qkv'), h.n(0, lane))
        for c in range(KD):
            for bank, name, bias, scale in ((0, 'qT', 'bq2s', HD ** -0.5), (1, 'kT', 'bk2', 1.0)):
                s.activation(L[name][:, lane, c * T:(c + 1) * T],
                             L['ps'][lane][:, bank * BANK + c * T:bank * BANK + (c + 1) * T], ACT.Identity,
                             bias=W[bias][:, c:c + 1], scale=scale)
        s.wait_ge(h.sem('values_cleared'), h.n(0, lane))
        s.activation(L['mask'][:, lane, 0:HEADS * (HD + 1)].rearrange("p (h j) -> p h j", h=HEADS)[:, :, 0:HD],
                     L['ps'][lane][0:T, D:2 * D].rearrange("p (h j) -> p h j", h=HEADS), ACT.Copy
                     ).then_inc(h.sem('qkv_copied'), 1)
    for c in range(KD):
        yield 203 + 18 * c
        for lane in h.lanes:
            s.wait_ge(h.sem('self_shifted'), h.n(c, lane))
            w = L['wide'][0:T, lane, c * CH * T:(c + 1) * CH * T]
            s.activation(w, w, ACT.Exp).then_inc(h.sem('self_probs'), 1)
    for r in range(HEADS // 4):
        yield 226 + 15 * r
        for lane in h.lanes:
            s.wait_ge(h.sem('self_turned'), h.n(r, lane))
            s.activation(L['mid'][0:T, lane, (r % 2) * 4 * T:(r % 2 + 1) * 4 * T],
                         L['ps'][lane][0:T, 0:4 * T], ACT.Copy).then_inc(h.sem('self_copied'), 1)
    yield 285
    copy_t(s, h, L, 0, pick(L, 'hT'), after(h, 'turned', 2), 'turned_copied')
    yield 307
    copy_t(s, h, L, 0, pick(L, 'hT'), after(h, 'turned', 3), 'turned_copied')


def back_gpsimd(gp, h, a, k, W, L, scratch):
    for i, position in enumerate((2, 10, 48, 104, 147, 155, 298)):
        yield position
        if i == 0:
            for lane in h.lanes:
                gp.memset(L['mask'][:, lane, 0:HEADS * (HD + 1)], 1.0).then_inc(h.sem('values_cleared'), 1)
        norm_rstd(gp, h, L, i, k['minus_half'][0:T, 0:1])
        if i == 2:
            yield 56
            for lane in h.lanes:
                gp.wait_ge(h.sem('hidden1_normed'), h.n(0, lane))
                gp.tensor_tensor(L['wide'][0:T, lane, 0:F1], L['wide'][0:T, lane, 0:F1], W['ln2_g'][:, :],
                                 ALU.mult).then_inc(h.sem('hidden1_gained'), 1)


def quantise(v, h, L, W, i, src_of, width, positions):
    yield positions[0]
    for lane in h.lanes:
        v.wait_ge(h.sem('quant_in'), h.n(i, lane))
        v.tensor_reduce(L['absmax'][:, lane, :], src_of(lane), AX.X, ALU.max,
                        apply_absolute_value=True).then_inc(h.sem('quant_max'), 1)
    for lane in h.lanes:
        v.wait_ge(h.sem('quant_max'), h.n(i, lane))
        v.tensor_scalar(L['step'][:, lane, :], L['absmax'][:, lane, :], EPS, INT8_SCALE, ALU.max,
                        ALU.mult).then_inc(h.sem('quant_step'), 1)
    for lane in h.lanes:
        v.wait_ge(h.sem('quant_step'), h.n(i, lane))
        v.reciprocal(L['inv'][:, lane, :], L['step'][:, lane, :])
        v.tensor_scalar(L['dq'][:, lane, :], L['step'][:, lane, :], W['wscale'][0:T, i:i + 1], None,
                        ALU.mult).then_inc(h.sem('quant_inv'), 1)
    yield positions[1]
    for lane in h.lanes:
        v.wait_ge(h.sem('quant_inv'), h.n(i, lane))
        v.tensor_scalar(src_of(lane), src_of(lane), L['inv'][:, lane, :], MAGIC, ALU.mult,
                        ALU.add).then_inc(h.sem('quant_rounded'), 1)
    yield positions[2]
    for lane in h.lanes:
        v.wait_ge(h.sem('quant_rounded'), h.n(i, lane))
        v.tensor_scalar(L['block'][0:T, lane, 0:width // 2].bitcast(BF16), src_of(lane), -MAGIC, 127.0,
                        ALU.add, ALU.min).then_inc(h.sem('quant'), 1)


def back_vector(v, h, a, k, W, L, scratch):
    gate = k['gate']
    x, xh, u = pick(L, 'x'), pick(L, 'xh'), pick(L, 'u')
    yield 0
    norm_stats(v, h, L, 0, x, None)
    yield 4
    norm_apply(v, h, L, 0, x, xh)
    yield 8
    norm_stats(v, h, L, 1, xh, after(h, 'norm_out', 0))
    yield 12
    norm_apply(v, h, L, 1, xh, u)
    yield 15
    for lane in h.lanes:
        v.wait_ge(h.sem('norm_out'), h.n(1, lane))
        v.tensor_tensor(L['u'][:, lane, :], L['u'][:, lane, :], W['ln1_g'][:, :], ALU.mult
                        ).then_inc(h.sem('quant_gain'), 1)
    for lane in h.lanes:
        v.wait_ge(h.sem('quant_gain'), h.n(0, lane))
        v.tensor_tensor(L['u'][:, lane, :], L['u'][:, lane, :], W['ln1_b'][:, :], ALU.add
                        ).then_inc(h.sem('quant_in'), 1)
    yield from quantise(v, h, L, W, 0, u, D, (19, 22, 24))
    hidden = lambda lane: L['wide'][0:T, lane, 0:F1]
    yield 33
    for lane in h.lanes:
        v.wait_ge(h.sem('hidden1_raw'), h.n(0, lane))
        v.scalar_tensor_tensor(hidden(lane), L['ps'][lane][0:T, 0:F1], L['dq'][:, lane, 0:1],
                               W['b1'][:, :], ALU.mult, ALU.add).then_inc(h.sem('hidden1'), 1)
    yield 42
    norm_stats(v, h, L, 2, hidden, after(h, 'gelu1'))
    yield 50
    for lane in h.lanes:
        v.wait_ge(h.sem('norm_rstd'), h.n(2, lane))
        v.tensor_scalar(L['shift'][:, lane, 0:1], L['mv'][:, lane, 0:1], L['rstd'][:, lane, 0:1], -1.0,
                        ALU.mult, ALU.mult).then_inc(h.sem('norm_shift'), 1)
    yield 60
    for lane in h.lanes:
        v.wait_ge(h.sem('hidden1_gained'), h.n(0, lane))
        v.tensor_tensor(hidden(lane), hidden(lane), W['ln2_b'][:, :], ALU.add
                        ).then_inc(h.sem('quant_in'), 1)
    yield from quantise(v, h, L, W, 1, hidden, F1, (68, 76, 84))
    yield 97
    for lane in h.lanes:
        v.wait_ge(h.sem('ffn1_raw'), h.n(0, lane))
        v.scalar_tensor_tensor(L['u'][:, lane, :], L['ps'][lane][0:T, BANK:BANK + D], L['dq'][:, lane, 0:1],
                               W['b2'][:, :], ALU.mult, ALU.add).then_inc(h.sem('ffn1'), 1)
    for lane in h.lanes:
        v.wait_ge(h.sem('ffn1'), h.n(0, lane))
        v.scalar_tensor_tensor(L['x'][:, lane, :], L['u'][:, lane, :], gate[0:T, 5:6], L['x'][:, lane, :],
                               ALU.mult, ALU.add).then_inc(h.sem('x_updated'), 1)
    yield 101
    norm_stats(v, h, L, 3, x, after(h, 'x_updated', 0))
    yield 106
    norm_apply(v, h, L, 3, x, xh)
    yield 126
    for lane in h.lanes:
        v.wait_ge(h.sem('scores'), h.n(0, lane))
        v.tensor_reduce(L['nmax'][:, lane, 0:1], L['ps'][lane][0:T, BANK:BANK + S_CTX], AX.X, ALU.max,
                        negate=True).then_inc(h.sem('row_max'), 1)
    yield 131
    attention_norm(v, h, L, 0, gate[0:T, 2:3])
    yield 142
    for lane in h.lanes:
        v.wait_ge(h.sem('factor'), h.n(0, lane))
    update(v, h, L, 1, lambda lane: L['factor'][:, lane, 0:1], 'attended', 0)
    yield 145
    norm_stats(v, h, L, 4, x, after(h, 'x_updated', 1))
    yield 149
    norm_apply(v, h, L, 4, x, xh)
    yield 153
    norm_stats(v, h, L, 5, xh, after(h, 'norm_out', 3))
    yield 157
    norm_apply(v, h, L, 5, xh, u)
    for c in range(KD):
        yield 173 + 28 * c
        for lane in h.lanes:
            if c:
                v.wait_ge(h.sem('self_scores'), h.n(0, lane))
            else:
                v.wait_ge(h.sem('qkv_copied'), h.n(0, lane))
            v.tensor_tensor(L['block'][:, lane, :].rearrange("p (j t) -> p j t", j=CH),
                            L['kT'][:, lane, c * T:(c + 1) * T].unsqueeze(1).broadcast_to([P, CH, T]),
                            W['headmask'][:, :].unsqueeze(2).broadcast_to([P, CH, T]), ALU.mult
                            ).then_inc(h.sem('key_blocks'), 1)
        yield 190 + 24 * c
        for lane in h.lanes:
            v.wait_ge(h.sem('self_scores'), h.n(c, lane))
            for bank in range(2):
                last = v.tensor_reduce(L['hmax'][:, lane, c * CH + 4 * bank:c * CH + 4 * bank + 4],
                                       L['ps'][lane][0:T, bank * BANK:bank * BANK + 4 * T]
                                       .rearrange("p (j t) -> p j t", j=4), AX.X, ALU.max)
            last.then_inc(h.sem('self_max'), 1)
        for lane in h.lanes:
            v.wait_ge(h.sem('self_max'), h.n(c, lane))
            for bank in range(2):
                j0 = c * CH + 4 * bank
                last = v.tensor_tensor(L['wide'][0:T, lane, j0 * T:(j0 + 4) * T].rearrange("p (j t) -> p j t", j=4),
                                       L['ps'][lane][0:T, bank * BANK:bank * BANK + 4 * T]
                                       .rearrange("p (j t) -> p j t", j=4),
                                       L['hmax'][:, lane, j0:j0 + 4].unsqueeze(2).broadcast_to([T, 4, T]),
                                       ALU.subtract)
            last.then_inc(h.sem('self_shifted'), 1)
    sums = lambda lane: L['ps'][lane][0:T, BANK:BANK + HEADS * (HD + 1)].rearrange("p (h j) -> p h j", h=HEADS)
    yield 280
    for lane in h.lanes:
        v.wait_ge(h.sem('self_out'), h.n(3, lane))
        v.reciprocal(L['hmax'][:, lane, :].unsqueeze(2), sums(lane)[:, :, HD:HD + 1]).then_inc(h.sem('self_rsum'), 1)
    for lane in h.lanes:
        v.wait_ge(h.sem('self_rsum'), h.n(0, lane))
        v.tensor_tensor(L['u'][:, lane, :].rearrange("p (h j) -> p h j", h=HEADS), sums(lane)[:, :, 0:HD],
                        L['hmax'][:, lane, :].unsqueeze(2).broadcast_to([T, HEADS, HD]), ALU.mult
                        ).then_inc(h.sem('self_normed'), 1)
    yield 292
    for lane in h.lanes:
        v.wait_ge(h.sem('self_proj'), h.n(0, lane))
        v.tensor_tensor(L['xh'][:, lane, :], L['ps'][lane][0:T, BANK:BANK + D], L['xh'][:, lane, :],
                        ALU.add).then_inc(h.sem('res2'), 1)
    yield 295
    norm_stats(v, h, L, 6, xh, after(h, 'res2'))
    yield 301
    norm_apply(v, h, L, 6, xh, u)
    yield 303
    for lane in h.lanes:
        v.wait_ge(h.sem('norm_out'), h.n(5, lane))
        v.tensor_tensor(L['u'][:, lane, :], L['u'][:, lane, :], W['ln2_scale'][:, :], ALU.mult
                        ).then_inc(h.sem('moe_gain'), 1)
    for lane in h.lanes:
        v.wait_ge(h.sem('moe_gain'), h.n(0, lane))
        v.tensor_tensor(L['u'][:, lane, :], L['u'][:, lane, :], W['ln2_bias'][:, :], ALU.add
                        ).then_inc(h.sem('moe_bias'), 1)
    yield 312
    for lane in h.lanes:
        v.wait_ge(h.sem('route'), h.n(0, lane))
        v.tensor_copy(L['logit'][:, lane, :], L['ps'][lane][0:T, BANK:BANK + E]
                      ).then_inc(h.sem('route_copied'), 1)


FRONT = {'sync': front_sync, 'tensor': front_tensor, 'scalar': front_scalar, 'gpsimd': front_gpsimd,
         'vector': front_vector}
BACK = {'sync': back_sync, 'tensor': back_tensor, 'scalar': back_scalar, 'gpsimd': back_gpsimd,
        'vector': back_vector}


def phase_one(nc, a, k, scratch):
    with ExitStack() as stack:
        m = Machine(nc, stack, 'one')
        W = {}
        for name, rows, cols in [('w_gateT', D, H0), ('w_upT', D, H0), ('w_downT', H0, D), ('Wq1', D, D),
                                 ('WkT1', D, D), ('Wv1', D, D), ('Wo1', D, D), ('WT2', D, D),
                                 ('w_qkv', D, 3 * D), ('w_proj', D, D), ('w_route', D, E)]:
            W[name] = m.sb(name, [P, rows // P, cols])
        for name in ['bq1', 'bq1s', 'qscale1', 'bk1', 'bv1', 'b2x', 'ln1_scale', 'ln1_bias', 'bq2', 'bq2s', 'bk2']:
            W[name] = m.sb(name, [P, KD])
        W['bias_rows'] = m.sb('bias_rows', [3, 3 * D + E], BF16)
        for j, (name, cols) in enumerate([('bo1', D), ('bv2', D), ('b_proj', D), ('b_route', E)]):
            W[name] = W['bias_rows'][:, j * D:j * D + cols]
        for name, cols in [('ln1_g', D), ('ln1_b', D), ('b1', F1), ('ln2_g', F1), ('ln2_b', F1), ('b2', D),
                           ('ln2_scale', D), ('ln2_bias', D)]:
            W[name] = m.sb(name, [T, cols])
        W['w1q'] = m.sb('w1q', [P, KD, F1], BF16)
        W['w2q'] = m.sb('w2q', [P, KF, D], BF16)
        W['wscale'] = m.sb('wscale', [P, 2])
        W['headmask'] = m.sb('headmask', [P, CH])
        W['causal16'] = m.sb('causal16', [T, 4 * T], BF16)
        W['gate_int8'] = m.sb('gate_int8', [P, 1])
        load_weights(nc, a, k, W, scratch)

        L = lane_buffers(m, [('x', T, [D]), ('xh', T, [D]), ('u', T, [D]), ('hT', P, [KD * T]),
                             ('qT', P, [KD * T]), ('kT', P, [KD * T]), ('ctx', SC, [NSC, D]),
                             ('ctxT', P, [KD, S_CTX]), ('mask', T, [S_CTX]), ('block', P, [CH * T]),
                             ('wide', P, [HEADS * T]), ('mid', P, [CH * T]),
                             ('stats', T, [12]), ('mv', T, [2]), ('var', T, [1]), ('rstd', T, [1]),
                             ('nmax', T, [1]), ('sum', T, [1]), ('rsum', T, [1]), ('factor', T, [1]),
                             ('row', T, [1]), ('absmax', T, [1]), ('step', T, [1]), ('inv', T, [1]),
                             ('dq', T, [1]), ('hmax', T, [HEADS]), ('shift', T, [1]),
                             ('logit', T, [E])])

        with nc.Block() as block:
            @block.sync
            def _(sync):
                load_context(sync, m, L, a['ctx_1024'], 0, 'ctx')
                for lane in range(LANES):
                    sync.wait_ge(m.sem(f'ctx{lane}'), 16)
        m.clear_all()

        even, odd = (0, 1), (2, 3)

        def half_step(front=None, back=None):
            sets = []
            if back is not None:
                sets.append((BACK, Lanes(m, 'back_', back[0], back[1] * LANES)))
            if front is not None:
                sets.append((FRONT, Lanes(m, 'front_', front[0], front[1] * LANES)))
            with nc.Block() as block:
                for engine, attach in (('sync', block.sync), ('tensor', block.tensor), ('scalar', block.scalar),
                                       ('gpsimd', block.gpsimd), ('vector', block.vector)):
                    programs = lambda queue, engine=engine: weave(
                        *[half[engine](queue, h, a, k, W, L, scratch) for half, h in sets])
                    attach(programs)
            m.clear_all()

        half_step(front=(even, 0))
        with nc.Fori(0, GROUPS - 1) as g:
            half_step(front=(odd, g), back=(even, g))
            half_step(front=(even, g + 1), back=(odd, g))
        half_step(front=(odd, GROUPS - 1), back=(even, GROUPS - 1))
        half_step(back=(odd, GROUPS - 1))


def load_weights(nc, a, k, W, scratch):
    with ExitStack() as stack:
        m = Machine(nc, stack, 'load')
        w1, w2 = m.sb('w1_raw', [P, KD, F1]), m.sb('w2_raw', [P, KF, D])
        total = m.sb('abs_total', [P, 2])
        inv = m.sb('w_inv', [P, 2])
        causal = m.sb('causal', [T, 4 * T])
        bias_row, bias_parts = m.sb('bias_row', [1, 3 * D + E]), m.sb('bias_parts', [1, 3, 3 * D + E], BF16)
        k['zeros'] = m.sb('zeros', [P, 2320])
        mean_ps = m.ps('mean_ps', [P, 2])

        with nc.Block() as block:
            @block.vector
            def _(v):
                v.memset(k['zeros'][:, :], 0.0)

        with nc.Block() as block:
            @block.sync
            def _(sync):
                loads = 0
                for tile, name in ((w1, 'w1T'), (w2, 'w2T')):
                    sync.dma_start(tile[:, :, :], a[name].rearrange("(c p) n -> p c n", p=P)
                                   ).then_inc(m.sem('w12_in'), 16)
                for name in ('w_gateT', 'w_upT', 'w_downT'):
                    sync.dma_start(W[name][:, :, :].bitcast(I32), a[name].rearrange("(c p) n -> p c n", p=P)
                                   ).then_inc(m.sem('ints_in'), 16)
                for name, src in (('Wq1', 'L1_xattn_Wq'), ('WkT1', 'WkT1'), ('Wv1', 'L1_xattn_Wv'),
                                  ('Wo1', 'L1_xattn_Wo'), ('WT2', 'WT2'), ('w_qkv', 'L2_ffn_w_qkv'),
                                  ('w_proj', 'L2_ffn_w_attnproj'), ('w_route', 'L2_ffn_w_gate')):
                    sync.dma_start(W[name][:, :, :], a[src].rearrange("(c p) n -> p c n", p=P)
                                   ).then_inc(m.sem('rest_in'), 16)
                    loads += 1
                bq = a['L2_ffn_b_qkv']
                with nc.allow_non_contiguous_dma(reason="a few hundred bias values, once"):
                    for name, src in (('bq1', a['L1_xattn_bq']), ('bq2', bq[0:D])):
                        sync.dma_start(W[name][:, :], src.rearrange("(c p) -> p c", p=P)
                                       ).then_inc(m.sem('queries_in'), 16)
                    for name, src in (('bk1', a['L1_xattn_bk']),
                                      ('bv1', a['L1_xattn_bv']), ('b2x', a['L2_xattn_b']),
                                      ('ln1_scale', a['L2_ffn_ln1_scale']), ('ln1_bias', a['L2_ffn_ln1_bias']),
                                      ('bk2', bq[D:2 * D])):
                        sync.dma_start(W[name][:, :], src.rearrange("(c p) -> p c", p=P)
                                       ).then_inc(m.sem('rest_in'), 16)
                        loads += 1
                for j, src in enumerate((a['L1_xattn_bo'], bq[2 * D:3 * D], a['L2_ffn_b_attnproj'],
                                         a['L2_ffn_b_gate'])):
                    sync.dma_start(bias_row[:, j * D:j * D + src.shape[0]], src.partition_broadcast(1)
                                   ).then_inc(m.sem('biases_in'), 16)
                for name, src in (('ln1_g', 'L1_ffn_ln1_g'), ('ln1_b', 'L1_ffn_ln1_b'), ('b1', 'L1_ffn_b1'),
                                  ('ln2_g', 'L1_ffn_ln2_g'), ('ln2_b', 'L1_ffn_ln2_b'), ('b2', 'L1_ffn_b2'),
                                  ('ln2_scale', 'L2_ffn_ln2_scale'), ('ln2_bias', 'L2_ffn_ln2_bias')):
                    sync.dma_start(W[name][:, :], a[src].partition_broadcast(T)).then_inc(m.sem('rest_in'), 16)
                    loads += 1
                sync.wait_ge(m.sem('split'), 1)
                for j in range(3):
                    sync.dma_start(W['bias_rows'][j:j + 1, :], bias_parts[:, j, :]
                                   ).then_inc(m.sem('parts_placed'), 16)
                sync.wait_ge(m.sem('parts_placed'), 48)
                sync.wait_ge(m.sem('rest_in'), 16 * loads)

            @block.scalar
            def _(s):
                zero_fill(s, m, k, scratch)

            @block.gpsimd
            def _(g):
                g.affine_select(W['headmask'][:, :], k['ones'][:, 0:CH], [[-HD, CH]], ALU.is_ge, 0.0,
                                base=0, channel_multiplier=1).then_inc(m.sem('masks'), 1)
                g.wait_ge(m.sem('masks'), 1)
                g.affine_select(W['headmask'][:, :], W['headmask'][:, :], [[HD, CH]], ALU.is_ge, 0.0,
                                base=HD - 1, channel_multiplier=-1)
                g.memset(causal[:, :], 0.0).then_inc(m.sem('masks'), 1)
                g.wait_ge(m.sem('masks'), 2)
                g.affine_select(causal[:, :], causal[:, :], [[0, 4], [-1, T]], ALU.is_ge, -1e30,
                                base=0, channel_multiplier=1).then_inc(m.sem('masks'), 1)

            @block.tensor
            def _(pe):
                pe.wait_ge(m.sem('abs_sums'), 2)
                pe.matmul(mean_ps[:, :], k['ones'][:, :], total[:, :], start=True, stop=True
                          ).then_inc(m.sem('abs_totals'), 1)

            @block.vector
            def _(v):
                v.wait_ge(m.sem('w12_in'), 32)
                for i, w in enumerate((w1, w2)):
                    v.tensor_reduce(total[:, i:i + 1], w[:, :, :], AX.XY, ALU.add, apply_absolute_value=True
                                    ).then_inc(m.sem('abs_sums'), 1)
                v.wait_ge(m.sem('ints_in'), 48)
                for name in ('w_gateT', 'w_upT', 'w_downT'):
                    v.tensor_copy(W[name][:, :, :], W[name][:, :, :].bitcast(I32))
                v.tensor_scalar(W['gate_int8'][:, :], k['gate'][:, 4:5], INT8_SCALE, None, ALU.mult)
                v.wait_ge(m.sem('abs_totals'), 1)
                v.tensor_scalar(W['wscale'][:, :], mean_ps[:, :], 1.0 / (D * F1), EPS, ALU.mult, ALU.max
                                ).then_inc(m.sem('w_mean'), 1)
                v.wait_ge(m.sem('w_mean'), 1)
                v.reciprocal(inv[:, :], W['wscale'][:, :]).then_inc(m.sem('w_mean'), 1)
                v.wait_ge(m.sem('w_mean'), 2)
                for i, w in enumerate((w1, w2)):
                    v.tensor_scalar(w[:, :, :], w[:, :, :], inv[:, i:i + 1], 1.0, ALU.mult, ALU.min
                                    ).then_inc(m.sem('w_step'), 1)
                for i, w in enumerate((w1, w2)):
                    v.wait_ge(m.sem('w_step'), 2)
                    v.tensor_scalar(w[:, :, :], w[:, :, :], -1.0, MAGIC, ALU.max, ALU.add
                                    ).then_inc(m.sem('w_step2'), 1)
                v.wait_ge(m.sem('w_step2'), 2)
                for w, q in ((w1, 'w1q'), (w2, 'w2q')):
                    v.tensor_scalar(W[q][:, :, :], w[:, :, :], -MAGIC, None, ALU.add)
                v.memset(W['qscale1'][:, :], D ** -0.5)
                v.wait_ge(m.sem('queries_in'), 32)
                v.tensor_scalar(W['bq1s'][:, :], W['bq1'][:, :], D ** -0.5, None, ALU.mult)
                v.tensor_scalar(W['bq2s'][:, :], W['bq2'][:, :], HD ** -0.5, None, ALU.mult)
                v.wait_ge(m.sem('masks'), 3)
                v.tensor_copy(W['causal16'][:, :], causal[:, :])
                v.wait_ge(m.sem('biases_in'), 64)
                split_three(v, m, 0, bias_row[:, :], [bias_parts[:, j, :] for j in range(3)])
        m.clear_all()



def zero_fill(queue, m, k, scratch):
    flat2 = scratch['moe_x2'].rearrange("r w -> (r w)").rearrange("(p f) -> p f", p=P)
    step = flat2.shape[1] // 7
    for j in range(7):
        queue.dma_start(flat2[:, j * step:(j + 1) * step], k['zeros'][:, 0:step]).then_inc(m.sem('zeroed'), 16)
    flat3 = scratch['moe_x3'][0:E * CAP, :].rearrange("r w -> (r w)").rearrange("(p f) -> p f", p=P)
    step = flat3.shape[1] // 4
    for j in range(4):
        queue.dma_start(flat3[:, j * step:(j + 1) * step], k['zeros'][:, 0:step]).then_inc(m.sem('zeroed'), 16)
    queue.wait_ge(m.sem('zeroed'), 16 * 11)


def spread(ap, shape):
    return ap.unsqueeze(2).broadcast_to(shape)


def route_block(nc, a, k, scratch, name, top_k, finish, extra, prefetch=None):
    with ExitStack() as stack:
        m = Machine(nc, stack, name)
        R = {t: m.sb('route_' + t, [T, B, E]) for t in
             ('p', 'eq', 'prio', 'oh0', 'oh1', 'taken', 'slot', 'tmp')}
        for t in ('max', 'sum', 'pm0', 'pm1', 'prio_max', 'slot0', 'slot1'):
            R[t] = m.sb('route_' + t, [T, B])
        for t in ('total', 'before'):
            R[t] = m.sb('route_' + t, [T, E, B])
        for t in ('count', 'blocks', 'blocks_to', 'blocks_before', 'base', 'rank', 'ones8'):
            R[t] = m.sb('route_' + t, [T, E])
        R['iota_i'] = m.sb('route_iota_i', [T, 128], I32)
        R['iota'] = m.sb('route_iota', [T, 128])
        R['ones32'] = m.sb('route_ones32', [T, B])
        R['part_i'] = m.sb('route_part_i', [T, 1], I32)
        R['part'] = m.sb('route_part', [T, 1])
        R['ranks'] = m.ps('route_ranks', [P, BANK])
        R['totals'] = m.ps('route_totals', [P, BANK])
        full = [T, B, E]
        extra(m, R)

        with nc.Block() as block:
            @block.sync
            def _(sync):
                sync.dma_start(R['p'][:, :, :], scratch[name].rearrange("(b t) e -> t b e", t=T)
                               ).then_inc(m.sem('logits_in'), 16)
                sync.wait_ge(m.sem('logits_in'), 16)
                if prefetch is not None:
                    prefetch(sync, sync)

            @block.gpsimd
            def _(g):
                g.iota(R['iota_i'][:, :], [[1, 128]], base=0, channel_multiplier=0)
                g.iota(R['part_i'][:, :], [[0, 1]], base=0, channel_multiplier=1).then_inc(m.sem('iota'), 1)

            @block.scalar
            def _(s):
                s.wait_ge(m.sem('shifted'), 1)
                s.activation(R['p'][:, :, :], R['p'][:, :, :], ACT.Exp).then_inc(m.sem('exp'), 1)

            @block.tensor
            def _(pe):
                pe.wait_ge(m.sem('taken'), 1)
                pe.matmul(R['ranks'][0:T, 0:B * E], k['tri'][0:T, 0:T],
                          R['taken'][:, :, :].rearrange("p b e -> p (b e)"), start=True, stop=True)
                pe.matmul(R['totals'][0:T, 0:B * E], k['ones'][0:T, 0:T],
                          R['taken'][:, :, :].rearrange("p b e -> p (b e)"), start=True, stop=True
                          ).then_inc(m.sem('ranked'), 1)

            @block.vector
            def _(v):
                v.memset(R['ones32'][:, :], 1.0)
                v.memset(R['ones8'][:, :], 1.0)
                v.wait_ge(m.sem('iota'), 1)
                v.tensor_copy(R['iota'][:, :], R['iota_i'][:, :]).then_inc(m.sem('iota_f'), 1)
                v.tensor_copy(R['part'][:, :], R['part_i'][:, :])
                v.wait_ge(m.sem('iota_f'), 1)
                v.tensor_scalar(R['rank'][:, :], R['iota'][:, 0:E], -1.0, float(E), ALU.mult, ALU.add)
                v.wait_ge(m.sem('logits_in'), 16)
                v.tensor_reduce(R['max'][:, :], R['p'][:, :, :], AX.X, ALU.max).then_inc(m.sem('max'), 1)
                v.wait_ge(m.sem('max'), 1)
                v.tensor_tensor(R['p'][:, :, :], R['p'][:, :, :], spread(R['max'][:, :], full), ALU.subtract
                                ).then_inc(m.sem('shifted'), 1)
                v.wait_ge(m.sem('exp'), 1)
                v.tensor_reduce(R['sum'][:, :], R['p'][:, :, :], AX.X, ALU.add).then_inc(m.sem('sum'), 1)
                v.wait_ge(m.sem('sum'), 1)
                v.reciprocal(R['sum'][:, :], R['sum'][:, :]).then_inc(m.sem('sum'), 1)
                v.wait_ge(m.sem('sum'), 2)
                v.tensor_tensor(R['p'][:, :, :], R['p'][:, :, :], spread(R['sum'][:, :], full), ALU.mult
                                ).then_inc(m.sem('probs'), 1)
                for c in range(top_k):
                    pm, oh = R[f'pm{c}'], R[f'oh{c}']
                    v.wait_ge(m.sem('probs'), c + 1)
                    v.tensor_reduce(pm[:, :], R['p'][:, :, :], AX.X, ALU.max).then_inc(m.sem('pm'), 1)
                    v.wait_ge(m.sem('pm'), c + 1)
                    v.tensor_tensor(R['eq'][:, :, :], R['p'][:, :, :], spread(pm[:, :], full), ALU.is_equal
                                    ).then_inc(m.sem('equal'), 1)
                    v.wait_ge(m.sem('equal'), c + 1)
                    v.tensor_tensor(R['prio'][:, :, :], R['eq'][:, :, :],
                                    R['rank'][:, :].unsqueeze(1).broadcast_to(full), ALU.mult
                                    ).then_inc(m.sem('prio'), 1)
                    v.wait_ge(m.sem('prio'), c + 1)
                    v.tensor_reduce(R['prio_max'][:, :], R['prio'][:, :, :], AX.X, ALU.max
                                    ).then_inc(m.sem('prio_max'), 1)
                    v.wait_ge(m.sem('prio_max'), c + 1)
                    v.tensor_tensor(oh[:, :, :], R['prio'][:, :, :], spread(R['prio_max'][:, :], full),
                                    ALU.is_equal).then_inc(m.sem('one_hot'), 1)
                    v.wait_ge(m.sem('one_hot'), c + 1)
                    if c + 1 < top_k:
                        v.scalar_tensor_tensor(R['p'][:, :, :], oh[:, :, :], -2.0, R['p'][:, :, :], ALU.mult,
                                               ALU.add).then_inc(m.sem('probs'), 1)
                if top_k == 2:
                    v.tensor_tensor(R['taken'][:, :, :], R['oh0'][:, :, :], R['oh1'][:, :, :], ALU.add
                                    ).then_inc(m.sem('taken'), 1)
                else:
                    v.tensor_copy(R['taken'][:, :, :], R['oh0'][:, :, :]).then_inc(m.sem('taken'), 1)
                v.wait_ge(m.sem('ranked'), 1)
                v.tensor_copy(R['total'][:, :, :], R['totals'][0:T, 0:B * E].rearrange("p (b e) -> p e b", e=E)
                              ).then_inc(m.sem('total'), 1)
                v.wait_ge(m.sem('total'), 1)
                for e in range(E):
                    last = v.tensor_tensor_scan(R['before'][:, e, :], R['ones32'][:, :], R['total'][:, e, :],
                                                0.0, ALU.mult, ALU.add)
                last.then_inc(m.sem('running'), 1)
                v.wait_ge(m.sem('running'), 1)
                v.tensor_copy(R['count'][:, :], R['before'][:, :, B - 1]).then_inc(m.sem('count'), 1)
                v.wait_ge(m.sem('count'), 1)
                v.tensor_tensor(R['before'][:, :, :], R['before'][:, :, :], R['total'][:, :, :], ALU.subtract
                                ).then_inc(m.sem('before'), 1)
                v.wait_ge(m.sem('before'), 1)
                finish(v, m, R)
        m.clear_all()


def slots_of(v, m, R, k, c, count):
    v.tensor_tensor(R['tmp'][:, :, :], R[f'oh{c}'][:, :, :], R['slot'][:, :, :], ALU.mult
                    ).then_inc(m.sem('slot_pick'), 1)
    v.wait_ge(m.sem('slot_pick'), count)
    v.tensor_reduce(R[f'slot{c}'][:, :], R['tmp'][:, :, :], AX.X, ALU.add).then_inc(m.sem('slot_sum'), 1)
    v.wait_ge(m.sem('slot_sum'), count)


def phase_route_two(nc, a, k, scratch, K2, prefetch):
    NJ = TOKENS // BLK

    def finish(v, m, R):
        with_blocks = R['cmp']
        v.tensor_scalar(R['mult'][:, :], R['iota'][:, 0:NJ], float(BLK), None, ALU.mult
                        ).then_inc(m.sem('steps'), 1)
        v.wait_ge(m.sem('steps'), 1)
        v.tensor_tensor(with_blocks[:, :, 0:NJ], R['count'][:, :].unsqueeze(2).broadcast_to([T, E, NJ]),
                        R['mult'][:, :].unsqueeze(1).broadcast_to([T, E, NJ]), ALU.is_gt
                        ).then_inc(m.sem('steps'), 1)
        v.wait_ge(m.sem('steps'), 2)
        v.tensor_reduce(R['blocks'][:, :], with_blocks[:, :, 0:NJ], AX.X, ALU.add).then_inc(m.sem('steps'), 1)
        v.wait_ge(m.sem('steps'), 3)
        v.tensor_tensor_scan(R['blocks_to'][:, :], R['ones8'][:, :], R['blocks'][:, :], 0.0, ALU.mult, ALU.add
                             ).then_inc(m.sem('steps'), 1)
        v.wait_ge(m.sem('steps'), 4)
        v.tensor_tensor(R['blocks_before'][:, :], R['blocks_to'][:, :], R['blocks'][:, :], ALU.subtract
                        ).then_inc(m.sem('steps'), 1)
        v.wait_ge(m.sem('steps'), 5)
        v.tensor_scalar(R['base'][:, :], R['blocks_before'][:, :], float(BLK), -1.0, ALU.mult, ALU.add
                        ).then_inc(m.sem('steps'), 1)
        v.wait_ge(m.sem('steps'), 6)
        v.tensor_tensor(R['before'][:, :, :], R['before'][:, :, :],
                        R['base'][:, :].unsqueeze(2).broadcast_to([T, E, B]), ALU.add).then_inc(m.sem('steps'), 1)
        v.wait_ge(m.sem('steps'), 7)
        v.tensor_tensor(R['slot'][:, :, :], R['ranks'][0:T, 0:B * E].rearrange("p (b e) -> p b e", e=E),
                        R['before'][:, :, :].rearrange("p e b -> p b e"), ALU.add).then_inc(m.sem('steps'), 1)
        v.wait_ge(m.sem('steps'), 8)
        for c in range(2):
            slots_of(v, m, R, k, c, c + 1)
            v.tensor_copy(K2['slot'][:, c, :], R[f'slot{c}'][:, :])
            v.tensor_copy(K2['weight'][:, c, :], R[f'pm{c}'][:, :])
        v.tensor_tensor(R['passed'][:, :, :], R['iota'][:, 0:NBLK].unsqueeze(2).broadcast_to([T, NBLK, E]),
                        R['blocks_to'][:, :].unsqueeze(1).broadcast_to([T, NBLK, E]), ALU.is_ge
                        ).then_inc(m.sem('steps'), 1)
        v.wait_ge(m.sem('steps'), 9)
        v.tensor_reduce(R['expert'][:, :], R['passed'][:, :, :], AX.X, ALU.add).then_inc(m.sem('steps'), 1)
        v.wait_ge(m.sem('steps'), 10)
        v.tensor_tensor(R['passed'][:, :, :], R['passed'][:, :, :],
                        R['blocks'][:, :].unsqueeze(1).broadcast_to([T, NBLK, E]), ALU.mult
                        ).then_inc(m.sem('steps'), 1)
        v.wait_ge(m.sem('steps'), 11)
        v.tensor_scalar(R['expert'][:, :], R['expert'][:, :], float(E - 1), None, ALU.min
                        ).then_inc(m.sem('steps'), 1)
        v.tensor_reduce(R['row'][:, :], R['passed'][:, :, :], AX.X, ALU.add).then_inc(m.sem('steps'), 1)
        v.wait_ge(m.sem('steps'), 13)
        v.tensor_copy(K2['expert'][:, :], R['expert'][0:1, :])
        for turn in range(2):
            v.tensor_scalar(R['wrap'][:, :], R['part'][:, :], float(E), -float(E), ALU.is_ge, ALU.mult
                            ).then_inc(m.sem('wrap'), 1)
            v.wait_ge(m.sem('wrap'), 2 * turn + 1)
            v.tensor_tensor(R['part'][:, :], R['part'][:, :], R['wrap'][:, :], ALU.add).then_inc(m.sem('wrap'), 1)
            v.wait_ge(m.sem('wrap'), 2 * turn + 2)
        v.tensor_scalar(K2['one_hot'][:, :], R['expert'][0:3 * E, :], R['part'][0:3 * E, 0:1], None, ALU.is_equal)
        v.tensor_tensor(R['row'][:, :], R['iota'][:, 0:NBLK], R['row'][:, :], ALU.subtract
                        ).then_inc(m.sem('steps'), 1)
        v.wait_ge(m.sem('steps'), 14)
        v.tensor_scalar(K2['row'][:, :], R['row'][0:1, :], float(NJ - 1), None, ALU.min)

    extra = lambda m, R: R.update(wrap=m.sb('route_wrap', [T, 1]), cmp=m.sb('route_cmp', [T, E, 28]), mult=m.sb('route_mult', [T, 28]),
                                  passed=m.sb('route_passed', [T, NBLK, E]),
                                  expert=m.sb('route_expert', [T, NBLK]), row=m.sb('route_row', [T, NBLK]))
    route_block(nc, a, k, scratch, 'route2', 2, finish, extra, prefetch)


def phase_scatter(nc, k, scratch, src, dst, slot, weight, copies):
    width = D + (1 if weight is not None else 0)
    with ExitStack() as stack:
        m = Machine(nc, stack, f'scatter{copies}')
        rows = m.sb('scatter_rows', [T, LANES, copies, width])
        index = m.sb('scatter_index', [T, LANES, copies], U32)
        scattered = k['pool_dma'][f'scattered{copies}']
        with nc.Fori(0, GROUPS) as g:
            with nc.Block() as block:
                @block.sync
                def _(sync):
                    for lane in range(LANES):
                        for c in range(copies):
                            sync.dma_start(rows[:, lane, c, 0:D], src[bass.ds((g * LANES + lane) * T, T), :]
                                           ).then_inc(m.sem(f'rows_in{lane}'), 16)

                @block.vector
                def _(v):
                    for lane in range(LANES):
                        b = g * LANES + lane
                        for c in range(copies):
                            if weight is not None:
                                v.tensor_copy(rows[:, lane, c, D:D + 1], weight[:, c, bass.ds(b, 1)])
                            last = v.tensor_copy(index[:, lane, c:c + 1], slot[:, c, bass.ds(b, 1)])
                        last.then_inc(m.sem('indexed'), 1)

                @block.gpsimd
                def _(gp):
                    for lane in range(LANES):
                        gp.wait_ge(m.sem(f'rows_in{lane}'), 16 * copies)
                        gp.wait_ge(m.sem('indexed'), lane + 1)
                        for c in range(copies):
                            gp.indirect_dma_start(dst, bass.IndirectOffsetOnAxis(ap=index[:, lane, c:c + 1], axis=0),
                                                  rows[:, lane, c, :], None).then_inc(scattered, 16)
                    gp.wait_ge(scattered, (g + 1) * (16 * LANES * copies))
            m.clear_all()



STEP = 21
RING = 7
assert NBLK % STEP == 0 and STEP % RING == 0


def load_experts_two(queue_a, queue_b, a, X):
    for e in range(E):
        queue_a.dma_start(X['w_fc'][:, e, :, :], a['L2_ffn_w_fc'][e].rearrange("(c p) n -> p c n", p=P)
                          ).then_inc(X['fc_in'], 16)
        queue_b.dma_start(X['w_out'][:, e, :, :], a['L2_ffn_w_fcproj'][e].rearrange("(c p) n -> p c n", p=P)
                          ).then_inc(X['out_in'], 16)


def phase_experts_two(nc, a, k, scratch, K2, X):
    NJ = TOKENS // BLK
    w_fc, w_out, acc = X['w_fc'], X['w_out'], X['acc']
    with ExitStack() as stack:
        m = Machine(nc, stack, 'experts2')
        b_fc, b_out = m.sb('b_fc', [3 * E, F1], BF16), m.sb('b_out', [3 * E, D], BF16)
        rows = m.sb('moe_rows', [P, RING, D + 1])
        xT = m.sb('moe_xT', [P, 2, KD * P])
        hid = m.sb('moe_hidden', [P, 2, F1])
        hT = m.sb('moe_hiddenT', [P, KF * P])
        pick = m.sb('moe_pick', [3 * E, 2, P], BF16)
        x_ps = m.ps('moe_x_ps', [P, BANK])
        h_ps = [m.ps(f'moe_h_ps{i}', [P, 2 * BANK]) for i in range(2)]
        t_ps = m.ps('moe_t_ps', [P, 2 * BANK])
        o_ps = m.ps('moe_o_ps', [P, BANK])

        parts = {'b_fc': (hid[0:E, 0, :], b_fc, F1), 'b_out': (hid[0:E, 1, 0:D], b_out, D)}
        split = {'b_fc': m.sb('b_fc_parts', [E, 3, F1], BF16), 'b_out': m.sb('b_out_parts', [E, 3, D], BF16)}
        with nc.Block() as block:
            @block.sync
            def _(sync):
                sync.dma_start(hid[0:E, 0, :], a['L2_ffn_b_fc']).then_inc(m.sem('biases_in'), 16)
                sync.dma_start(hid[0:E, 1, 0:D], a['L2_ffn_b_fcproj']).then_inc(m.sem('biases_in'), 16)
                sync.wait_ge(m.sem('split'), 2)
                for name, (_, dst, _) in parts.items():
                    for j in range(3):
                        sync.dma_start(dst[j * E:(j + 1) * E, :], split[name][:, j, :]
                                       ).then_inc(m.sem('parts_placed'), 16)
                sync.wait_ge(m.sem('parts_placed'), 16 * 6)
                sync.wait_ge(X['fc_in'], 16 * E)
                sync.wait_ge(X['out_in'], 16 * E)

            @block.vector
            def _(v):
                v.memset(acc[:, :, :], 0.0)
                v.wait_ge(m.sem('biases_in'), 32)
                for i, (name, (src, _, _)) in enumerate(parts.items()):
                    split_three(v, m, i, src, [split[name][:, j, :] for j in range(3)])
        m.clear_all()

        with nc.Fori(0, NBLK // STEP) as g:
            with nc.Block() as block:
                @block.sync
                def _(sync):
                    for j in range(STEP):
                        if j >= RING:
                            sync.wait_ge(m.sem('added'), j - RING + 1)
                        sync.dma_start(rows[:, j % RING, :],
                                       scratch['moe_x2'][bass.ds((g * STEP + j) * BLK, BLK), :]
                                       ).then_inc(m.sem(f'rows_in{j % RING}'), 16)

                @block.tensor
                def _(pe):
                    def turn_x(j):
                        pe.wait_ge(m.sem(f'rows_in{j % RING}'), 16 * (j // RING + 1))
                        if j:
                            pe.wait_ge(m.sem('x_copied'), j)
                        for c in range(KD):
                            t = pe.transpose(x_ps[:, c * P:(c + 1) * P], rows[:, j % RING, c * P:(c + 1) * P],
                                             k['ident'][:, :])
                        t.then_inc(m.sem('x_turned'), 1)

                    def hidden(j):
                        e = pe.value_load(K2['expert'][0:1, bass.ds(g * STEP + j, 1)], min_val=0, max_val=E - 1)
                        pe.wait_ge(m.sem('x_copied'), j + 1)
                        pe.wait_ge(m.sem('picked'), j + 1)
                        if j >= 2:
                            pe.wait_ge(m.sem('activated'), j - 1)
                        for o in range(2):
                            out = h_ps[j % 2][:, o * BANK:(o + 1) * BANK]
                            pe.matmul(out, pick[:, j % 2, :], b_fc[:, o * BANK:(o + 1) * BANK],
                                      start=True, stop=False)
                            for c in range(KD):
                                mm = pe.matmul(out, xT[:, j % 2, c * P:(c + 1) * P],
                                               w_fc[:, bass.ds(e, 1), c, o * BANK:(o + 1) * BANK]
                                               .rearrange("p o n -> p (o n)"), start=False, stop=(c == KD - 1))
                        mm.then_inc(m.sem('hidden'), 1)
                        return e

                    def turn_hidden(j):
                        pe.wait_ge(m.sem('activated'), j + 1)
                        if j:
                            pe.wait_ge(m.sem('h_copied'), 2 * j)
                        for o in range(2):
                            for c in range(4 * o, 4 * o + 4):
                                t = pe.transpose(t_ps[:, c * P:(c + 1) * P], hid[:, j % 2, c * P:(c + 1) * P],
                                                 k['ident'][:, :])
                            t.then_inc(m.sem('h_turned'), 1)

                    def output(j, e):
                        if j:
                            pe.wait_ge(m.sem('added'), j)
                        pe.matmul(o_ps[:, 0:D], pick[:, j % 2, :], b_out[:, :], start=True, stop=False)
                        for c in range(KF):
                            if c % 4 == 0:
                                pe.wait_ge(m.sem('h_copied'), 2 * j + 1 + c // 4)
                            mm = pe.matmul(o_ps[:, 0:D], hT[:, c * P:(c + 1) * P],
                                           w_out[:, bass.ds(e, 1), c, :].rearrange("p o n -> p (o n)"),
                                           start=False, stop=(c == KF - 1))
                        mm.then_inc(m.sem('out'), 1)

                    turn_x(0)
                    e = hidden(0)
                    for j in range(STEP):
                        if j + 1 < STEP:
                            turn_x(j + 1)
                        turn_hidden(j)
                        after = hidden(j + 1) if j + 1 < STEP else None
                        output(j, e)
                        e = after

                @block.scalar
                def _(s):
                    for j in range(STEP):
                        s.wait_ge(m.sem('hidden'), j + 1)
                        if j >= 2:
                            s.wait_ge(m.sem('h_turned'), 2 * (j - 1))
                        s.activation(hid[:, j % 2, :], h_ps[j % 2][:, :], ACT.Gelu_apprx_tanh
                                     ).then_inc(m.sem('activated'), 1)

                @block.vector
                def _(v):
                    def copy_x(j):
                        if j >= 2:
                            v.wait_ge(m.sem('out'), j - 1)
                        v.tensor_copy(pick[:, j % 2, :],
                                      K2['one_hot'][:, bass.ds(g * STEP + j, 1)].broadcast_to([3 * E, P])
                                      ).then_inc(m.sem('picked'), 1)
                        v.wait_ge(m.sem('x_turned'), j + 1)
                        v.tensor_copy(xT[:, j % 2, :], x_ps[:, 0:KD * P]).then_inc(m.sem('x_copied'), 1)

                    def add(j):
                        row = v.value_load(K2['row'][0:1, bass.ds(g * STEP + j, 1)], min_val=0, max_val=NJ - 1)
                        v.wait_ge(m.sem('out'), j + 1)
                        if j:
                            v.wait_ge(m.sem('added'), j)
                        place = acc[:, bass.ds(row, 1), :].rearrange("p o n -> p (o n)")
                        v.scalar_tensor_tensor(place, o_ps[:, 0:D], rows[:, j % RING, D:D + 1], place,
                                               ALU.mult, ALU.add).then_inc(m.sem('added'), 1)

                    copy_x(0)
                    for j in range(STEP):
                        if j:
                            add(j - 1)
                        if j + 1 < STEP:
                            copy_x(j + 1)
                        for o in range(2):
                            v.wait_ge(m.sem('h_turned'), 2 * j + 1 + o)
                            v.tensor_copy(hT[:, o * BANK:(o + 1) * BANK], t_ps[:, o * BANK:(o + 1) * BANK]
                                          ).then_inc(m.sem('h_copied'), 1)
                    add(STEP - 1)
            m.clear_all()


def phase_combine_two(nc, k, scratch, acc):
    NJ = TOKENS // BLK
    if True:
        with ExitStack() as stack:
            m = Machine(nc, stack, 'combine2')
            x2, res = m.sb('x2_rows', [P, NJ, D]), m.sb('res_rows', [P, NJ, D])
            parts, w = 4, NJ // 4
            by_rows = lambda ap, j: ap[j * w * P:(j + 1) * w * P, :].rearrange("(j p) d -> p j d", p=P)
            with nc.Block() as block:
                @block.sync
                def _(sync):
                    for j in range(parts):
                        sync.dma_start(res[:, j * w:(j + 1) * w, :], by_rows(scratch['res2'], j)
                                       ).then_inc(m.sem(f'in{j}'), 16)
                        sync.dma_start(x2[:, j * w:(j + 1) * w, :], by_rows(scratch['x2'], j)
                                       ).then_inc(m.sem(f'in{j}'), 16)
                    for j in range(parts):
                        sync.wait_ge(m.sem('combined'), j + 1)
                        sync.dma_start(by_rows(scratch['x3'], j), x2[:, j * w:(j + 1) * w, :]
                                       ).then_inc(m.sem('x3_out'), 16)
                    sync.wait_ge(m.sem('x3_out'), 16 * parts)

                @block.vector
                def _(v):
                    for j in range(parts):
                        s = slice(j * w, (j + 1) * w)
                        v.wait_ge(m.sem(f'in{j}'), 32)
                        v.tensor_tensor(res[:, s, :], res[:, s, :], acc[:, s, :], ALU.add).then_inc(m.sem('summed'), 1)
                        v.wait_ge(m.sem('summed'), j + 1)
                        v.scalar_tensor_tensor(x2[:, s, :], res[:, s, :], k['gate'][:, 6:7], x2[:, s, :], ALU.mult,
                                               ALU.add).then_inc(m.sem('combined'), 1)
            m.clear_all()



def phase_four(nc, a, k, scratch):
    with ExitStack() as stack:
        m = Machine(nc, stack, 'four')
        W = {}
        for name, cols in [('WqT3', D), ('Wk3', D), ('WvT3', D), ('Wr', E)]:
            W[name] = m.sb(name, [P, KD, cols])
        for name in ('bq3', 'bq3s', 'bk3', 'qscale'):
            W[name] = m.sb(name, [P, KD])
        W['bv3'] = m.sb('bv3', [3, D], BF16)
        bv3_row, bv3_parts = m.sb('bv3_row', [1, D]), m.sb('bv3_parts', [1, 3, D], BF16)
        L = lane_buffers(m, [('x', T, [D]), ('xh', T, [D]), ('u', T, [D]), ('hT', P, [KD * T]),
                             ('qT', P, [KD * T]), ('ctx', SC, [NSC, D]), ('ctxT', P, [KD, S_CTX]),
                             ('mask', T, [S_CTX]), ('wide', P, [2 * 384]), ('mid', P, [384]),
                             ('stats', T, [12]), ('mv', T, [2]), ('var', T, [1]), ('rstd', T, [1]),
                             ('nmax', T, [1]), ('sum', T, [1]), ('rsum', T, [1]), ('factor', T, [1]),
                             ('row', T, [1]), ('logit', T, [E])])
        rows3 = scratch['moe_y3']

        with nc.Block() as block:
            @block.sync
            def _(sync):
                load_context(sync, m, L, a['ctx_1024'], 0, 'ctx')
                for name, src in (('WqT3', 'WqT3'), ('Wk3', 'L3_xattn_Wk'), ('WvT3', 'WvT3'), ('Wr', 'L3_ffn_Wr')):
                    sync.dma_start(W[name][:, :, :], a[src].rearrange("(c p) n -> p c n", p=P)
                                   ).then_inc(m.sem('w_in'), 16)
                with nc.allow_non_contiguous_dma(reason="a few hundred bias values, once"):
                    for name, src in (('bq3', 'L3_xattn_bq'), ('bk3', 'L3_xattn_bk')):
                        sync.dma_start(W[name][:, :], a[src].rearrange("(c p) -> p c", p=P)
                                       ).then_inc(m.sem('w_in'), 16)
                sync.dma_start(bv3_row[:, :], a['L3_xattn_bv'].partition_broadcast(1)).then_inc(m.sem('w_in'), 16)
                sync.wait_ge(m.sem('w_in'), 16 * 7)
                sync.wait_ge(m.sem('split'), 1)
                for j in range(3):
                    sync.dma_start(W['bv3'][j:j + 1, :], bv3_parts[:, j, :]).then_inc(m.sem('parts_placed'), 16)
                sync.wait_ge(m.sem('parts_placed'), 48)
                for lane in range(LANES):
                    sync.wait_ge(m.sem(f'ctx{lane}'), 16)

            @block.vector
            def _(v):
                v.memset(W['qscale'][:, :], D ** -0.5)
                v.wait_ge(m.sem('w_in'), 16 * 7)
                v.tensor_scalar(W['bq3s'][:, :], W['bq3'][:, :], D ** -0.5, None, ALU.mult)
                split_three(v, m, 0, bv3_row[:, :], [bv3_parts[:, j, :] for j in range(3)])
        m.clear_all()

        with nc.Fori(0, GROUPS) as g:
            every = Lanes(m, '', tuple(range(LANES)), g * LANES)
            with nc.Block() as block:
                @block.sync
                def _(sync):
                    for lane in every.lanes:
                        b = every.batch(lane)
                        sync.dma_start(L['x'][:, lane, :], scratch['x3'][bass.ds(b * T, T), :]
                                       ).then_inc(m.sem(f'x_in{lane}'), 16)
                        sync.dma_start(L['mid'][0:T, lane, 0:S_CTX].bitcast(I32),
                                       a['mask_BxS2_ik1'][bass.ds(b, 1), :].broadcast_to([T, S_CTX])
                                       ).then_inc(m.sem(f'mask_in{lane}'), 16)
                    for lane in every.lanes:
                        sync.wait_ge(m.sem('attended'), every.n(0, lane))
                        sync.dma_start(L['ctx'][:, lane, :, :],
                                       a['ctx_1024'][bass.ds((every.batch(lane) + LANES) % B, 1), :, :]
                                       .rearrange("o (c p) d -> p (o c) d", p=SC)).then_inc(m.sem(f'ctx{lane}'), 16)
                    for lane in every.lanes:
                        b = every.batch(lane)
                        sync.wait_ge(m.sem('x_updated'), every.n(0, lane))
                        sync.dma_start(scratch['x4'][bass.ds(b * T, T), :], L['x'][:, lane, :]
                                       ).then_inc(m.sem(f'x_out{lane}'), 16)
                    for lane in every.lanes:
                        b = every.batch(lane)
                        sync.wait_ge(m.sem('norm_out'), every.n(1, lane))
                        sync.dma_start(rows3[bass.ds(b * T + E * CAP, T), :], L['u'][:, lane, :]
                                       ).then_inc(m.sem(f'h_out{lane}'), 16)
                    for lane in every.lanes:
                        b = every.batch(lane)
                        sync.wait_ge(m.sem('route_copied'), every.n(0, lane))
                        sync.dma_start(scratch['route3'][bass.ds(b * T, T), :], L['logit'][:, lane, :]
                                       ).then_inc(m.sem(f'route_out{lane}'), 16)
                    for lane in every.lanes:
                        for name in ('x_out', 'h_out', 'route_out', 'ctx'):
                            sync.wait_ge(m.sem(f'{name}{lane}'), 16)

                @block.tensor
                def _(pe):
                    turn_context(pe, every, k, L)
                    for lane in every.lanes:
                        pe.wait_ge(m.sem('ctx_copied'), every.n(0, lane))
                    turn_rows(pe, every, k, L, 0, pick(L, 'xh'), after(every, 'norm_out', 0))
                    project_t(pe, every, L, W['WqT3'], pick(L, 'hT'), after(every, 'turned_copied', 0), 0, 'q3_raw')
                    for lane in every.lanes:
                        pe.wait_ge(m.sem('q3'), every.n(0, lane))
                        for o in range(KD):
                            for c in range(KD):
                                pe.matmul(L['ps'][lane][:, BANK + o * T:BANK + (o + 1) * T],
                                          W['Wk3'][:, c, o * P:(o + 1) * P], L['qT'][:, lane, c * T:(c + 1) * T],
                                          start=(c == 0), stop=(c == KD - 1))
                        for c in range(KD):
                            mm = pe.matmul(L['ps'][lane][0:T, BANK + KD * T:BANK + KD * T + 1],
                                           L['qT'][:, lane, c * T:(c + 1) * T], W['bk3'][:, c:c + 1],
                                           start=(c == 0), stop=(c == KD - 1))
                        mm.then_inc(m.sem('key_q3'), 1)
                    attention_scores(pe, every, L, 0, pick(L, 'hT'), after(every, 'key_q3_copied'))
                    turn_probs(pe, every, k, L, 0, after(every, 'probs_normed', 0))
                    attend_t(pe, every, L, 0)
                    for lane in every.lanes:
                        pe.wait_ge(m.sem('attended_copied'), every.n(0, lane))
                        rows_out(pe, L, lane, W['WvT3'], L['qT'][:, lane, :], KD, 0, D, W['bv3'][:, :], k['ones16']
                                 ).then_inc(m.sem('v3'), 1)
                    turn_rows(pe, every, k, L, 1, pick(L, 'u'), after(every, 'norm_out', 1))
                    for lane in every.lanes:
                        pe.wait_ge(m.sem('turned_copied'), every.n(1, lane))
                        rows_out(pe, L, lane, W['Wr'], L['hT'][:, lane, :], KD, 1, E).then_inc(m.sem('route'), 1)

                @block.scalar
                def _(s):
                    copy_context(s, every, L)
                    copy_t(s, every, L, 0, pick(L, 'hT'), after(every, 'turned', 0), 'turned_copied')
                    copy_t(s, every, L, 0, pick(L, 'qT'), after(every, 'q3_raw'), 'q3', scale=W['qscale'], bias=W['bq3s'])
                    for lane in every.lanes:
                        s.wait_ge(m.sem('key_q3'), every.n(0, lane))
                        s.activation(L['hT'][:, lane, :], L['ps'][lane][:, BANK:BANK + KD * T], ACT.Copy)
                        s.activation(L['row'][:, lane, :], L['ps'][lane][0:T, BANK + KD * T:BANK + KD * T + 1],
                                     ACT.Copy).then_inc(m.sem('key_q3_copied'), 1)
                    attention_exp(s, every, L, 0)
                    copy_probs(s, every, L, 0)
                    copy_t(s, every, L, 1, pick(L, 'qT'), after(every, 'attended', 0), 'attended_copied')
                    copy_t(s, every, L, 0, pick(L, 'hT'), after(every, 'turned', 1), 'turned_copied')

                @block.gpsimd
                def _(gp):
                    for lane in every.lanes:
                        gp.wait_ge(m.sem(f'mask_in{lane}'), 16)
                        gp.tensor_scalar(L['mask'][:, lane, :], L['mid'][0:T, lane, 0:S_CTX].bitcast(I32), 0.0,
                                         MINUS_BIG, ALU.is_equal, ALU.mult).then_inc(m.sem('mask_ready'), 1)
                    for i in range(2):
                        norm_rstd(gp, every, L, i, k['minus_half'][0:T, 0:1])

                @block.vector
                def _(v):
                    norm_stats(v, every, L, 0, pick(L, 'x'), lambda lane: (m.sem(f'x_in{lane}'), 16))
                    norm_apply(v, every, L, 0, pick(L, 'x'), pick(L, 'xh'))
                    for lane in every.lanes:
                        v.wait_ge(m.sem('key_q3_copied'), every.n(0, lane))
                        v.wait_ge(m.sem('mask_ready'), every.n(0, lane))
                        v.wait_ge(m.sem('scores'), every.n(0, lane))
                        v.scalar_tensor_tensor(L['wide'][0:T, lane, 0:S_CTX], L['ps'][lane][0:T, BANK:BANK + S_CTX],
                                               L['row'][:, lane, 0:1], L['mask'][:, lane, :], ALU.add,
                                               ALU.add).then_inc(m.sem('logits'), 1)
                    for lane in every.lanes:
                        v.wait_ge(m.sem('logits'), every.n(0, lane))
                        v.tensor_reduce(L['nmax'][:, lane, 0:1], L['wide'][0:T, lane, 0:S_CTX], AX.X, ALU.max,
                                        negate=True).then_inc(m.sem('row_max'), 1)
                    attention_norm(v, every, L, 0)
                    for lane in every.lanes:
                        v.wait_ge(m.sem('v3'), every.n(0, lane))
                        v.scalar_tensor_tensor(L['x'][:, lane, :], L['ps'][lane][0:T, 0:D], k['gate'][0:T, 3:4],
                                               L['x'][:, lane, :], ALU.mult, ALU.add
                                               ).then_inc(m.sem('x_updated'), 1)
                    norm_stats(v, every, L, 1, pick(L, 'x'), after(every, 'x_updated', 0))
                    norm_apply(v, every, L, 1, pick(L, 'x'), pick(L, 'u'))
                    for lane in every.lanes:
                        v.wait_ge(m.sem('route'), every.n(0, lane))
                        v.tensor_copy(L['logit'][:, lane, :], L['ps'][lane][0:T, BANK:BANK + E]
                                      ).then_inc(m.sem('route_copied'), 1)
            m.clear_all()



def phase_route_three(nc, a, k, scratch, K3):
    def finish(v, m, R):
        step = [0]

        def done(ins):
            step[0] += 1
            ins.then_inc(m.sem('steps'), 1)
            v.wait_ge(m.sem('steps'), step[0])
        done(v.tensor_tensor(R['slot'][:, :, :], R['ranks'][0:T, 0:B * E].rearrange("p (b e) -> p b e", e=E),
                             R['before'][:, :, :].rearrange("p e b -> p b e"), ALU.add))
        slots_of(v, m, R, k, 0, 1)
        done(v.tensor_scalar(R['slot0'][:, :], R['slot0'][:, :], -1.0, None, ALU.add))
        done(v.tensor_scalar(R['kept'][:, :], R['slot0'][:, :], float(CAP), None, ALU.is_lt))
        done(v.tensor_scalar(R['slot1'][:, :], R['prio_max'][:, :], -float(CAP), float(E * CAP), ALU.mult, ALU.add))
        done(v.tensor_tensor(R['slot0'][:, :], R['slot0'][:, :], R['slot1'][:, :], ALU.add))
        done(v.tensor_scalar(R['own'][:, :], R['iota'][:, 0:B], float(T), float(E * CAP), ALU.mult, ALU.add))
        done(v.tensor_scalar(R['own'][:, :], R['own'][:, :], R['part'][:, 0:1], None, ALU.add))
        done(v.tensor_tensor(R['slot0'][:, :], R['slot0'][:, :], R['own'][:, :], ALU.subtract))
        done(v.tensor_tensor(R['slot0'][:, :], R['slot0'][:, :], R['kept'][:, :], ALU.mult))
        done(v.tensor_tensor(R['slot0'][:, :], R['slot0'][:, :], R['own'][:, :], ALU.add))
        v.tensor_copy(K3['slot'][:, 0, :], R['slot0'][:, :])
        done(v.tensor_tensor(R['pm0'][:, :], R['pm0'][:, :], R['kept'][:, :], ALU.mult))
        done(v.tensor_scalar(R['kept'][:, :], R['kept'][:, :], -1.0, 1.0, ALU.mult, ALU.add))
        done(v.tensor_tensor(R['pm0'][:, :], R['pm0'][:, :], R['kept'][:, :], ALU.add))
        v.tensor_scalar(K3['factor'][:, :], R['pm0'][:, :], k['gate'][0:T, 7:8], None, ALU.mult)

    extra = lambda m, R: R.update(kept=m.sb('route_kept', [T, B]), own=m.sb('route_own', [T, B]))
    route_block(nc, a, k, scratch, 'route3', 1, finish, extra)


TILES = CAP // T
PARTS = ((0, 3), (3, 5))
assert TILES * T == CAP and TILES == 5


def phase_experts_three(nc, a, k, scratch):
    with ExitStack() as stack:
        m = Machine(nc, stack, 'experts3')
        w1 = [m.sb(f'w1_{i}', [P, KD, F1]) for i in range(2)]
        w2 = [m.sb(f'w2_{i}', [P, KF, D]) for i in range(2)]
        rows = m.sb('rows3', [T, 2, TILES, D])
        xT = m.sb('xT3', [P, 2, KD, CAP])
        hT = m.sb('hT3', [P, 2, KF, CAP])
        y = m.sb('y3', [T, 2, TILES, D])
        x_ps = [m.ps(f'x3_ps{i}', [P, BANK]) for i in range(2)]
        h_ps = [m.ps(f'h3_ps{i}', [P, BANK]) for i in range(4)]
        o_ps = [m.ps(f'o3_ps{i}', [P, BANK]) for i in range(2)]

        def load(sync, i, e):
            sync.dma_start(w1[i][:, :, :], a['L3_ffn_W1'][bass.ds(e, 1), :, :]
                           .rearrange("o (c p) n -> p (o c) n", p=P)).then_inc(m.sem(f'w{i}'), 16)
            sync.dma_start(w2[i][:, :, :], a['L3_ffn_W2'][bass.ds(e, 1), :, :]
                           .rearrange("o (c p) n -> p (o c) n", p=P)).then_inc(m.sem(f'w{i}'), 16)

        with nc.Block() as block:
            @block.sync
            def _(sync):
                for i in range(2):
                    load(sync, i, i)
                for i in range(2):
                    sync.wait_ge(m.sem(f'w{i}'), 32)
        m.clear_all()

        with nc.Fori(0, E // 2) as g:
            with nc.Block() as block:
                @block.sync
                def _(sync):
                    for i in range(2):
                        sync.dma_start(rows[:, i, :, :], scratch['moe_x3'][bass.ds((g * 2 + i) * CAP, CAP), :]
                                       .rearrange("(j t) d -> t j d", t=T)).then_inc(m.sem(f'rows_in{i}'), 16)
                    for i in range(2):
                        sync.wait_ge(m.sem('out_done'), TILES * (i + 1))
                        load(sync, i, (g * 2 + i + 2) % E)
                        sync.wait_ge(m.sem('y_copied'), TILES * (i + 1))
                        sync.dma_start(scratch['moe_y3'][bass.ds((g * 2 + i) * CAP, CAP), :]
                                       .rearrange("(j t) d -> t j d", t=T), y[:, i, :, :]).then_inc(m.sem(f'y_out{i}'), 16)
                    for i in range(2):
                        sync.wait_ge(m.sem(f'w{i}'), 32)
                        sync.wait_ge(m.sem(f'y_out{i}'), 16)

                @block.tensor
                def _(pe):
                    def turn(i):
                        pe.wait_ge(m.sem(f'rows_in{i}'), 16)
                        for q, (t0, t1) in enumerate(PARTS):
                            for c in range(KD):
                                use = (i * 2 + q) * KD + c
                                if use >= 2:
                                    pe.wait_ge(m.sem('x_copied'), use - 1)
                                for t in range(t0, t1):
                                    tr = pe.transpose(x_ps[use % 2][:, (t - t0) * T:(t - t0 + 1) * T],
                                                      rows[:, i, t, c * P:(c + 1) * P], k['ident'][0:T, 0:T])
                                tr.then_inc(m.sem('x_turned'), 1)

                    def hidden(i):
                        for q, (t0, t1) in enumerate(PARTS):
                            pe.wait_ge(m.sem('x_copied'), (i * 2 + q + 1) * KD)
                            for f in range(KF):
                                use = (i * 2 + q) * KF + f
                                if use >= 4:
                                    pe.wait_ge(m.sem('h_copied'), use - 3)
                                for c in range(KD):
                                    mm = pe.matmul(h_ps[use % 4][:, 0:(t1 - t0) * T], w1[i][:, c, f * P:(f + 1) * P],
                                                   xT[:, i, c, t0 * T:t1 * T], start=(c == 0), stop=(c == KD - 1))
                                mm.then_inc(m.sem('hidden'), 1)

                    def output(i):
                        for t in range(TILES):
                            use = i * TILES + t
                            pe.wait_ge(m.sem('h_copied'), (i * 2 + (1 if t < PARTS[0][1] else 2)) * KF)
                            if use >= 2:
                                pe.wait_ge(m.sem('y_copied'), use - 1)
                            for f in range(KF):
                                mm = pe.matmul(o_ps[use % 2][0:T, 0:D], hT[:, i, f, t * T:(t + 1) * T],
                                               w2[i][:, f, :], start=(f == 0), stop=(f == KF - 1))
                            mm.then_inc(m.sem('out_done'), 1)

                    turn(0)
                    hidden(0)
                    turn(1)
                    output(0)
                    hidden(1)
                    output(1)

                @block.scalar
                def _(s):
                    for i in range(2):
                        for q, (t0, t1) in enumerate(PARTS):
                            for f in range(KF):
                                use = (i * 2 + q) * KF + f
                                s.wait_ge(m.sem('hidden'), use + 1)
                                s.activation(hT[:, i, f, t0 * T:t1 * T], h_ps[use % 4][:, 0:(t1 - t0) * T], ACT.Relu
                                             ).then_inc(m.sem('h_copied'), 1)

                @block.vector
                def _(v):
                    def copy_x(i):
                        for q, (t0, t1) in enumerate(PARTS):
                            for c in range(KD):
                                use = (i * 2 + q) * KD + c
                                v.wait_ge(m.sem('x_turned'), use + 1)
                                v.tensor_copy(xT[:, i, c, t0 * T:t1 * T], x_ps[use % 2][:, 0:(t1 - t0) * T]
                                              ).then_inc(m.sem('x_copied'), 1)

                    copy_x(0)
                    copy_x(1)
                    for use in range(2 * TILES):
                        v.wait_ge(m.sem('out_done'), use + 1)
                        v.tensor_copy(y[:, use // TILES, use % TILES, :], o_ps[use % 2][0:T, 0:D]
                                      ).then_inc(m.sem('y_copied'), 1)
            m.clear_all()


def phase_gather(nc, k, scratch, K3, out):
    with ExitStack() as stack:
        m = Machine(nc, stack, 'gather')
        x = m.sb('last_x', [T, LANES, D])
        y = m.sb('last_y', [T, LANES, D])
        index = m.sb('last_index', [T, LANES], U32)
        factor = m.sb('last_factor', [T, LANES])
        with nc.Fori(0, GROUPS) as g:
            with nc.Block() as block:
                @block.sync
                def _(sync):
                    for lane in range(LANES):
                        sync.dma_start(x[:, lane, :], scratch['x4'][bass.ds((g * LANES + lane) * T, T), :]
                                       ).then_inc(m.sem(f'x_in{lane}'), 16)
                    for lane in range(LANES):
                        sync.wait_ge(m.sem('final'), lane + 1)
                        sync.dma_start(out[bass.ds(g * LANES + lane, 1), :, :].rearrange("o t d -> (o t) d"),
                                       x[:, lane, :]).then_inc(m.sem('stored'), 16)
                    sync.wait_ge(m.sem('stored'), 16 * LANES)

                @block.vector
                def _(v):
                    v.tensor_copy(factor[:, :], K3['factor'][:, bass.ds(g * LANES, LANES)])
                    v.tensor_copy(index[:, :], K3['slot'][:, 0, bass.ds(g * LANES, LANES)]).then_inc(m.sem('indexed'), 1)
                    v.wait_ge(m.sem('indexed'), 1)
                    for lane in range(LANES):
                        v.wait_ge(m.sem(f'x_in{lane}'), 16)
                        v.wait_ge(k['pool_dma'][f'gathered{lane}'], (g + 1) * 16)
                        v.scalar_tensor_tensor(x[:, lane, :], y[:, lane, :], factor[:, lane:lane + 1], x[:, lane, :],
                                               ALU.mult, ALU.add).then_inc(m.sem('final'), 1)

                @block.gpsimd
                def _(gp):
                    gp.wait_ge(m.sem('indexed'), 1)
                    for lane in range(LANES):
                        gp.indirect_dma_start(y[:, lane, :], None, scratch['moe_y3'],
                                              bass.IndirectOffsetOnAxis(ap=index[:, lane:lane + 1], axis=0)
                                              ).then_inc(k['pool_dma'][f'gathered{lane}'], 16)
            m.clear_all()


def later_phases(nc, a, k, scratch, out):
    with ExitStack() as stack:
        m = Machine(nc, stack, 'keep2')
        K2 = {'slot': m.sb('slot2', [T, 2, B]), 'weight': m.sb('weight2', [T, 2, B]),
              'expert': m.sb('expert2', [1, NBLK], I32), 'row': m.sb('row2', [1, NBLK], I32),
              'one_hot': m.sb('one_hot2', [3 * E, NBLK])}
        X = {'acc': m.sb('moe_acc', [P, TOKENS // BLK, D])}
        with ExitStack() as inner:
            w = Machine(nc, inner, 'weights2')
            X.update(w_fc=w.sb('w_fc', [P, E, KD, F1]), w_out=w.sb('w_out', [P, E, KF, D]),
                     fc_in=w.sem('fc_in'), out_in=w.sem('out_in'))
            phase_route_two(nc, a, k, scratch, K2, lambda sync, s: load_experts_two(sync, s, a, X))
            phase_scatter(nc, k, scratch, scratch['moe_in'], scratch['moe_x2'], K2['slot'], K2['weight'], 2)
            phase_experts_two(nc, a, k, scratch, K2, X)
            w.clear_all()
        phase_combine_two(nc, k, scratch, X['acc'])
    phase_four(nc, a, k, scratch)
    with ExitStack() as stack:
        m = Machine(nc, stack, 'keep3')
        K3 = {'slot': m.sb('slot3', [T, 1, B]), 'factor': m.sb('factor3', [T, B])}
        phase_route_three(nc, a, k, scratch, K3)
        phase_scatter(nc, k, scratch, scratch['moe_y3'][E * CAP:, :], scratch['moe_x3'], K3['slot'], None, 1)
        phase_experts_three(nc, a, k, scratch)
        phase_gather(nc, k, scratch, K3, out)



def build(nc, a, out):
    scratch = {}
    for name, shape in (('turned', [B, D, T]), ('x2', [TOKENS, D]), ('res2', [TOKENS, D]),
                        ('moe_in', [TOKENS, D]), ('route2', [TOKENS, E]),
                        ('moe_x2', [NBLK * BLK, D + 1]), ('x3', [TOKENS, D]), ('x4', [TOKENS, D]),
                        ('route3', [TOKENS, E]), ('moe_x3', [E * CAP + TOKENS, D]),
                        ('moe_y3', [E * CAP + TOKENS, D])):
        scratch[name] = nc.dram_tensor('scratch_' + name, shape, F32).ap()
    with ExitStack() as stack:
        m = Machine(nc, stack, 'all')
        k = {'ident': m.sb('ident', [P, P]), 'tri': m.sb('tri', [P, P]), 'ones': m.sb('ones', [P, P]),
             'ident16': m.sb('ident16', [P, P], BF16), 'ones16': m.sb('ones16', [3, P], BF16), 'minus_half': m.sb('minus_half', [P, LANES]),
             'gate': m.sb('gate', [P, 8]), 'g_xattn': a['g_xattn'], 'g_ffn': a['g_ffn']}
        pool = Machine(nc, stack, 'pool')
        k['pool_dma'] = {name: pool.sem(name) for name in
                         ['scattered1', 'scattered2'] + [f'gathered{lane}' for lane in range(LANES)]}
        make_constants(nc, m, k)
        phase_one(nc, a, k, scratch)
        later_phases(nc, a, k, scratch, out)


_TURNED = {'w_gateT': 'L0_ffn_w_gate', 'w_upT': 'L0_ffn_w_up', 'w_downT': 'L0_ffn_w_down',
           'WkT1': 'L1_xattn_Wk', 'w1T': 'L1_ffn_w1', 'w2T': 'L1_ffn_w2', 'WT2': 'L2_xattn_W',
           'WqT3': 'L3_xattn_Wq', 'WvT3': 'L3_xattn_Wv'}


def kernel(**inputs):
    import numpy as np
    import concourse.bacc as bacc
    from concourse import mybir as mb
    from concourse.bass_utils import run_bass_kernel_spmd as run
    nc = bacc.Bacc("TRN2", target_bir_lowering=False, num_devices=1)
    host = {name: v for name, v in inputs.items() if name not in _TURNED.values()}
    for name, src in _TURNED.items():
        host[name] = np.asarray(inputs[src]).T
    arrays, args = {}, {}
    for name, v in host.items():
        v = np.ascontiguousarray(v)
        arrays[f"in_{name}_dram"] = v
        args[name] = nc.dram_tensor(f"in_{name}_dram", v.shape, mb.dt.from_np(v.dtype),
                                    kind="ExternalInput").ap()
    out = nc.dram_tensor("out_0_dram", (B, T, D), mb.dt.from_np(np.dtype('float32')),
                         kind="ExternalOutput").ap()
    build(nc, args, out)
    r = run(nc, [arrays], core_ids=[0])
    return r.results[0]["out_0_dram"]
```

```python
from contextlib import ExitStack

import concourse.bass as bass
from concourse import mybir

ALU = mybir.AluOpType
ACT = mybir.ActivationFunctionType
F32 = mybir.dt.float32
BF16 = mybir.dt.bfloat16
I32 = mybir.dt.int32
U32 = mybir.dt.uint32
AX = mybir.AxisListType

P = 128
B, T, D, S_CTX = 32, 112, 256, 375
TOKENS = B * T
KD = D // P
SC, NSC = 125, 3
H0 = 768
F1 = 1024
KF = F1 // P
HEADS, HD = 16, 16
CH = P // HD
E = 8
LANES = 4
BANK = 512
EPS = 1e-5
INT8_SCALE = 1.0 / 127.0
MAGIC = 12582912.0
NEG = -1e9
MINUS_BIG = -3.0e38
CAP = int(1.25 * TOKENS / E)
BLK = 128
NBLK = (2 * TOKENS) // BLK + E - 1


class Machine:

    def __init__(self, nc, stack, phase):
        self.nc, self.stack, self.phase, self.sems = nc, stack, phase, {}

    def sb(self, name, shape, dt=F32):
        return self.stack.enter_context(self.nc.sbuf_tensor(f'{self.phase}_{name}', shape, dt))

    def ps(self, name, shape, dt=F32):
        return self.stack.enter_context(self.nc.psum_tensor(f'{self.phase}_{name}', shape, dt))

    def sem(self, name):
        if name not in self.sems:
            self.sems[name] = self.stack.enter_context(self.nc.semaphore(f'{self.phase}_{name}'))
        return self.sems[name]

    def clear_all(self):
        sems = list(self.sems.values())
        with self.nc.Block() as block:
            for i, attach in enumerate((block.sync, block.tensor, block.scalar, block.gpsimd, block.vector)):
                def share(queue, i=i):
                    for s in sems[i::5]:
                        queue.sem_clear(s)
                attach(share)


class Lanes:

    def __init__(self, m, prefix, lanes, first, turn=0, uses=(), before=None):
        self.m, self.prefix, self.lanes, self.first = m, prefix, lanes, first
        self.turn, self.uses, self.before = turn, dict(uses), before

    def sem(self, name):
        return self.m.sem(self.prefix + name)

    def at(self, name, i, lane):
        before = self.turn * self.uses.get(name, 1) + i
        return self.sem(name), len(self.lanes) * before + self.lanes.index(lane) + 1

    def landed(self, name, lane):
        return self.sem(f'{name}{lane}'), 16 * (self.turn // LANES + 1)

    def batch(self, lane):
        return self.first + lane


def weave(*programs):
    heads = []
    for program, times in programs:
        next(program)
        heads.append([program, list(times)])
    while heads:
        head = min(heads, key=lambda head: head[1][0])
        program, times = head
        times.pop(0)
        if next(program, 'done') == 'done':
            assert not times
            heads.remove(head)


class Chain:

    def __init__(self, programs, uses, times, period, leaves):
        self.quarters, self.programs, self.uses = tuple(programs), programs, uses
        self.times, self.period, self.leaves = times, period, leaves

    def quarters_of(self, m, base, steps):
        ran, turns, out = {}, {quarter: 0 for quarter in self.quarters}, []
        for t in steps:
            now = {}
            for q, quarter in enumerate(self.quarters):
                b = t - q
                if not isinstance(base, int) or 0 <= b < B:
                    lane = b % LANES
                    now[lane] = Lanes(m, quarter + '_', (lane,), base + (b - lane), turns[quarter],
                                      self.uses.get(quarter, {}), ran.get(lane))
                    turns[quarter] += 1
                    out.append((t - steps[0], quarter, now[lane]))
            ran.update(now)
        return out


def run_steps(nc, m, chain, base, steps, a, k, W, L, scratch):
    work = chain.quarters_of(m, base, steps)
    with nc.Block() as block:
        for engine, attach in (('sync', block.sync), ('tensor', block.tensor), ('scalar', block.scalar),
                               ('gpsimd', block.gpsimd), ('vector', block.vector)):
            def programs(queue, engine=engine):
                weave(*[(chain.programs[quarter][engine](queue, h, a, k, W, L, scratch),
                         [step * chain.period + time for time in chain.times[quarter][engine]])
                        for step, quarter, h in work if engine in chain.programs[quarter]])
                if engine == 'sync':
                    for _, quarter, h in work:
                        if quarter == chain.quarters[-1]:
                            for name in chain.leaves:
                                queue.wait_ge(*h.landed(name, h.lanes[0]))
            attach(programs)
    m.clear_all()


def run_chain(nc, m, chain, unroll, a, k, W, L, scratch):
    run_steps(nc, m, chain, 0, range(0, LANES - 1), a, k, W, L, scratch)
    turns = (B - LANES + 1) // unroll
    with nc.Fori(0, turns) as g:
        run_steps(nc, m, chain, g * unroll, range(LANES - 1, LANES - 1 + unroll), a, k, W, L, scratch)
    run_steps(nc, m, chain, 0, range(LANES - 1 + turns * unroll, B + LANES - 1), a, k, W, L, scratch)



def make_constants(nc, m, k):
    with nc.Block() as block:
        @block.gpsimd
        def _(g):
            g.memset(k['ones'][:, :], 1.0).then_inc(m.sem('ones_set'), 1)
            g.memset(k['minus_half'][:, :], -0.5)
            g.wait_ge(m.sem('ones_set'), 1)
            g.affine_select(k['ident'][:, :], k['ones'][:, :], [[-1, P]], ALU.is_equal, 0.0,
                            base=0, channel_multiplier=1).then_inc(m.sem('ident_set'), 1)
            g.affine_select(k['tri'][:, :], k['ones'][:, :], [[1, P]], ALU.is_ge, 0.0,
                            base=0, channel_multiplier=-1).then_inc(m.sem('ident_set'), 1)

        @block.vector
        def _(v):
            v.wait_ge(m.sem('ident_set'), 2)
            v.tensor_copy(k['ident16'][:, :], k['ident'][:, :])
            v.memset(k['ones16'][:, :], 1.0)

        @block.sync
        def _(sync):
            sync.dma_start(k['gate'][:, 0:4], k['g_xattn'].partition_broadcast(P)).then_inc(m.sem('gates'), 16)
            sync.dma_start(k['gate'][:, 4:8], k['g_ffn'].partition_broadcast(P)).then_inc(m.sem('gates'), 16)

        @block.scalar
        def _(s):
            s.wait_ge(m.sem('gates'), 32)
            s.activation(k['gate'][:, :], k['gate'][:, :], ACT.Tanh).then_inc(m.sem('gates_tanh'), 1)
    m.clear_all()


def split_three(v, m, i, src, parts):
    step = 4 * i
    for j in range(3):
        v.tensor_copy(parts[j], src).then_inc(m.sem('split_step' if j < 2 else 'split'), 1)
        if j < 2:
            v.wait_ge(m.sem('split_step'), step + 2 * j + 1)
            v.tensor_tensor(src, src, parts[j], ALU.subtract).then_inc(m.sem('split_step'), 1)
            v.wait_ge(m.sem('split_step'), step + 2 * j + 2)



def norm_stats(v, m, L, i, src_of, ready_of):
    for lane in m.lanes:
        src = src_of(lane)
        if ready_of is not None:
            v.wait_ge(*ready_of(lane))
        width = src.shape[1]
        parts = max(1, width // BANK)
        for j in range(parts):
            w = width // parts
            stats = v.bn_stats(L['stats'][:, lane, 6 * j:6 * j + 6], src[:, j * w:(j + 1) * w])
        stats.then_inc(m.sem('norm_stats'), 1)
    for lane in m.lanes:
        width = src_of(lane).shape[1]
        parts = max(1, width // BANK)
        v.wait_ge(*m.at('norm_stats', i, lane))
        v.bn_aggr(L['mv'][:, lane, :], L['stats'][:, lane, 0:6 * parts]).then_inc(m.sem('norm_aggr'), 1)


def norm_apply(v, m, L, i, src_of, dst_of):
    for lane in m.lanes:
        v.wait_ge(*m.at('norm_rstd', i, lane))
        v.tensor_scalar(dst_of(lane), src_of(lane), L['mv'][:, lane, 0:1], L['rstd'][:, lane, 0:1],
                        ALU.subtract, ALU.mult).then_inc(m.sem('norm_out'), 1)


def norm_rstd(g, m, L, i, minus_half):
    for lane in m.lanes:
        g.wait_ge(*m.at('norm_aggr', i, lane))
        g.tensor_scalar(L['var'][:, lane, 0:1], L['mv'][:, lane, 1:2], EPS, None,
                        ALU.add).then_inc(m.sem('norm_var'), 1)
        g.wait_ge(*m.at('norm_var', i, lane))
        g.tensor_tensor(L['rstd'][:, lane, 0:1], L['var'][:, lane, 0:1], minus_half,
                        ALU.pow).then_inc(m.sem('norm_rstd'), 1)


def turn_rows(pe, m, k, L, i, src_of, ready_of):
    for lane in m.lanes:
        pe.wait_ge(*ready_of(lane))
        src = src_of(lane)
        for c in range(KD):
            t = pe.transpose(L['ps'][lane][:, c * T:(c + 1) * T], src[:, c * P:(c + 1) * P],
                             k['ident'][0:T, 0:T])
        t.then_inc(m.sem('turned'), 1)


def project_t(pe, m, L, w, src_of, ready_of, bank, done):
    for lane in m.lanes:
        pe.wait_ge(*ready_of(lane))
        for o in range(KD):
            for c in range(KD):
                mm = pe.matmul(L['ps'][lane][:, bank * BANK + o * T:bank * BANK + (o + 1) * T],
                               w[:, c, o * P:(o + 1) * P], src_of(lane)[:, c * T:(c + 1) * T],
                               start=(c == 0), stop=(c == KD - 1))
        mm.then_inc(m.sem(done), 1)


def rows_out(pe, L, lane, w, lhs, chunks, bank, width, bias=None, ones=None, stop=True):
    out = L['ps'][lane][0:T, bank * BANK:bank * BANK + width]
    for c in range(chunks):
        mm = pe.matmul(out, lhs[:, c * T:(c + 1) * T], w[:, c, :], start=(c == 0),
                       stop=(c == chunks - 1 and bias is None))
    if bias is not None:
        mm = pe.matmul(out, ones[0:3, 0:T], bias, start=False, stop=True)
    return mm


def attention_scores(pe, m, L, i, q_of, ready_of):
    for lane in m.lanes:
        pe.wait_ge(*ready_of(lane))
        for c in range(KD):
            mm = pe.matmul(L['ps'][lane][0:T, BANK:BANK + S_CTX], q_of(lane)[:, c * T:(c + 1) * T],
                           L['ctxT'][:, lane, c, :], start=(c == 0), stop=(c == KD - 1))
        mm.then_inc(m.sem('scores'), 1)


def attention_logits(v, m, L, i, scale, mask_of, mask_ready):
    for lane in m.lanes:
        v.wait_ge(*m.at('scores', i, lane))
        v.wait_ge(*mask_ready(lane))
        v.scalar_tensor_tensor(L['wide'][0:T, lane, 0:S_CTX], L['ps'][lane][0:T, BANK:BANK + S_CTX], scale,
                               mask_of(lane), ALU.mult, ALU.add).then_inc(m.sem('logits'), 1)
    for lane in m.lanes:
        v.wait_ge(*m.at('logits', i, lane))
        v.tensor_reduce(L['nmax'][:, lane, 0:1], L['wide'][0:T, lane, 0:S_CTX], AX.X, ALU.max,
                        negate=True).then_inc(m.sem('row_max'), 1)


def attention_exp(s, m, L, i, from_psum=False):
    for lane in m.lanes:
        s.wait_ge(*m.at('row_max', i, lane))
        logits = L['ps'][lane][0:T, BANK:BANK + S_CTX] if from_psum else L['wide'][0:T, lane, 0:S_CTX]
        s.activation(L['wide'][0:T, lane, 384:384 + S_CTX], logits, ACT.Exp,
                     bias=L['nmax'][:, lane, 0:1], scale=1.0,
                     accum_out=L['sum'][:, lane, 0:1]).then_inc(m.sem('probs'), 1)


def attention_norm(v, m, L, i, gate=None):
    for lane in m.lanes:
        v.wait_ge(*m.at('probs', i, lane))
        v.reciprocal(L['rsum'][:, lane, 0:1], L['sum'][:, lane, 0:1]).then_inc(m.sem('rsum'), 1)
    for lane in m.lanes:
        v.wait_ge(*m.at('rsum', i, lane))
        if gate is not None:
            v.tensor_scalar(L['factor'][:, lane, 0:1], L['rsum'][:, lane, 0:1], gate, None,
                            ALU.mult).then_inc(m.sem('factor'), 1)
        else:
            p = L['wide'][0:T, lane, 384:384 + S_CTX]
            v.tensor_scalar(p, p, L['rsum'][:, lane, 0:1], None, ALU.mult).then_inc(m.sem('probs_normed'), 1)


def turn_probs(pe, m, k, L, i, ready_of):
    for lane in m.lanes:
        pe.wait_ge(*ready_of(lane))
        for c in range(NSC):
            t = pe.transpose(L['ps'][lane][0:SC, c * T:(c + 1) * T],
                             L['wide'][0:T, lane, 384 + c * SC:384 + (c + 1) * SC], k['ident'][0:T, 0:T])
        t.then_inc(m.sem('probs_turned'), 1)


def copy_probs(s, m, L, i):
    for lane in m.lanes:
        s.wait_ge(*m.at('probs_turned', i, lane))
        s.activation(L['mid'][0:SC, lane, 0:NSC * T], L['ps'][lane][0:SC, 0:NSC * T],
                     ACT.Copy).then_inc(m.sem('probs_copied'), 1)


def attend_rows(pe, m, L, i):
    for lane in m.lanes:
        pe.wait_ge(*m.at('probs_copied', i, lane))
        for c in range(NSC):
            mm = pe.matmul(L['ps'][lane][0:T, BANK:BANK + D], L['mid'][0:SC, lane, c * T:(c + 1) * T],
                           L['ctx'][:, lane, c, :], start=(c == 0), stop=(c == NSC - 1))
        mm.then_inc(m.sem('attended'), 1)


def attend_t(pe, m, L, i):
    for lane in m.lanes:
        pe.wait_ge(*m.at('probs_copied', i, lane))
        for o in range(KD):
            for c in range(NSC):
                mm = pe.matmul(L['ps'][lane][:, BANK + o * T:BANK + (o + 1) * T],
                               L['ctx'][:, lane, c, o * P:(o + 1) * P],
                               L['mid'][0:SC, lane, c * T:(c + 1) * T],
                               start=(c == 0), stop=(c == NSC - 1))
        mm.then_inc(m.sem('attended'), 1)


def copy_t(s, m, L, src_bank, dst_of, ready_of, done, scale=None, bias=None):
    for lane in m.lanes:
        s.wait_ge(*ready_of(lane))
        src = L['ps'][lane][:, src_bank * BANK:src_bank * BANK + KD * T]
        if bias is None:
            s.activation(dst_of(lane), src, ACT.Copy).then_inc(m.sem(done), 1)
            continue
        for c in range(KD):
            last = s.activation(dst_of(lane)[:, c * T:(c + 1) * T], src[:, c * T:(c + 1) * T], ACT.Identity,
                                bias=bias[:, c:c + 1], scale=1.0 if scale is None else scale[:, c:c + 1])
        last.then_inc(m.sem(done), 1)


def turn_context(pe, m, k, L):
    for lane in m.lanes:
        for c in range(KD):
            for j in range(NSC):
                t = pe.transpose(L['ps'][lane][:, c * BANK + j * SC:c * BANK + (j + 1) * SC],
                                 L['ctx'][:, lane, j, c * P:(c + 1) * P], k['ident'][0:SC, 0:SC])
        t.then_inc(m.sem('ctx_turned'), 1)


def copy_context(s, m, L):
    for lane in m.lanes:
        s.wait_ge(*m.at('ctx_turned', 0, lane))
        for c in range(KD):
            last = s.activation(L['ctxT'][:, lane, c, :], L['ps'][lane][:, c * BANK:c * BANK + S_CTX], ACT.Copy)
        last.then_inc(m.sem('ctx_copied'), 1)


def load_context(sync, m, L, ctx_in, first, sems):
    for lane in range(LANES):
        sync.dma_start(L['ctx'][:, lane, :, :],
                       ctx_in[bass.ds(first + lane, 1), :, :].rearrange("o (c p) d -> p (o c) d", p=SC)
                       ).then_inc(m.sem(f'{sems}{lane}'), 16)


def lane_buffers(m, names_widths):
    L = {name: m.sb('lane_' + name, [rows, LANES, *width], F32) for name, rows, width in names_widths}
    L['ps'] = [m.ps(f'lane_ps{lane}', [P, 2 * BANK]) for lane in range(LANES)]
    return L



def pick(L, name):
    return lambda lane: L[name][:, lane, :]


def after(h, name, i=0):
    return lambda lane: h.at(name, i, lane)



def layer0_sync(sync, h, a, k, W, L, scratch):
    yield
    for lane in h.lanes:
        b = h.batch(lane)
        if h.before is not None:
            for name in STORES:
                sync.wait_ge(*h.before.landed(name, lane))
        sync.dma_start(L['x'][:, lane, :], a['x'][bass.ds(b, 1), :, :].rearrange("o t d -> (o t) d")
                       ).then_inc(h.sem(f'x_in{lane}'), 16)
        sync.dma_start(L['mid'][0:T, lane, 0:S_CTX].bitcast(I32),
                       a['mask_Bx1xS2_ik0'][bass.ds(b, 1), :, :].rearrange("o u s -> (o u) s")
                       .broadcast_to([T, S_CTX])).then_inc(h.sem(f'mask_in{lane}'), 16)


def cross1_sync(sync, h, a, k, W, L, scratch):
    yield
    for lane in h.lanes:
        sync.wait_ge(*h.at('v1', 0, lane))
        sync.dma_start(scratch['turned'][bass.ds(h.batch(lane), 1), :, :].rearrange("o (c p) t -> p (o c) t", p=P),
                       L['hT'][:, lane, :].rearrange("p (c t) -> p c t", c=KD)
                       ).then_inc(h.sem('turned_out'), 16)
    yield
    for lane in h.lanes:
        sync.wait_ge(h.sem('turned_out'), 16 * (h.turn + 1))
        sync.dma_start(L['u'][:, lane, :],
                       scratch['turned'][bass.ds(h.batch(lane), 1), :, :].rearrange("o p t -> (o p t)")
                       .rearrange("(i j) -> i j", j=D)).then_inc(h.sem('turned_in'), 16)


STORES = ('x_out', 'res2_out', 'moe_in_out', 'route2_out')


def self2_sync(sync, h, a, k, W, L, scratch):
    yield
    for lane in h.lanes:
        b = h.batch(lane)
        if h.before is not None:
            sync.wait_ge(*h.before.at('x_updated', 1, lane))
        sync.dma_start(scratch['x2'][bass.ds(b * T, T), :], L['x'][:, lane, :]
                       ).then_inc(h.sem(f'x_out{lane}'), 16)
        sync.dma_start(L['ctx'][:, lane, :, :],
                       a['ctx_1024'][bass.ds((b + LANES) % B, 1), :, :]
                       .rearrange("o (c p) d -> p (o c) d", p=SC)).then_inc(h.sem(f'ctx_in{lane}'), 16)
    for ready, name, tile in (('res2', 'res2', 'xh'), ('moe_bias', 'moe_in', 'u'),
                              ('route_copied', 'route2', 'logit')):
        yield
        for lane in h.lanes:
            sync.wait_ge(*h.at(ready, 0, lane))
            sync.dma_start(scratch[name][bass.ds(h.batch(lane) * T, T), :], L[tile][:, lane, :]
                           ).then_inc(h.sem(f'{name}_out{lane}'), 16)


def layer0_tensor(pe, h, a, k, W, L, scratch):
    yield
    if h.before is not None:
        for lane in h.lanes:
            pe.wait_ge(*h.before.landed('ctx_in', lane))
            pe.wait_ge(*h.before.at('route_copied', 0, lane))
    turn_context(pe, h, k, L)
    yield
    for lane in h.lanes:
        pe.wait_ge(*h.at('ctx_copied', 0, lane))
    turn_rows(pe, h, k, L, 0, pick(L, 'xh'), after(h, 'norm_out', 0))
    yield
    attention_scores(pe, h, L, 0, pick(L, 'hT'), after(h, 'turned_copied', 0))
    yield
    turn_probs(pe, h, k, L, 0, after(h, 'probs', 0))
    yield
    attend_rows(pe, h, L, 0)
    yield
    turn_rows(pe, h, k, L, 1, pick(L, 'xh'), after(h, 'norm_out', 1))
    for r in range(2):
        yield
        for lane in h.lanes:
            pe.wait_ge(*h.at('turned_copied', 1, lane))
            if r:
                pe.wait_ge(*h.at('hidden0', 0, lane))
            for bank, w in enumerate((W['w_gateT'], W['w_upT'])):
                for j in range(3):
                    for c in range(KD):
                        o = (3 * r + j) * P
                        mm = pe.matmul(L['ps'][lane][:, bank * BANK + j * T:bank * BANK + (j + 1) * T],
                                       w[:, c, o:o + P], L['hT'][:, lane, c * T:(c + 1) * T],
                                       start=(c == 0), stop=(c == KD - 1))
            mm.then_inc(h.sem('gate_up'), 1)
    yield
    for lane in h.lanes:
        pe.wait_ge(*h.at('hidden0', 1, lane))
        rows_out(pe, L, lane, W['w_downT'], L['block'][:, lane, :], H0 // P, 0, D).then_inc(h.sem('down0'), 1)


def cross1_tensor(pe, h, a, k, W, L, scratch):
    yield
    turn_rows(pe, h, k, L, 0, pick(L, 'xh'), after(h, 'norm_out', 0))
    yield
    project_t(pe, h, L, W['Wq1'], pick(L, 'hT'), after(h, 'turned_copied', 0), 0, 'q1_raw')
    yield
    for lane in h.lanes:
        pe.wait_ge(*h.at('q1', 0, lane))
        for o in range(KD):
            for c in range(KD):
                pe.matmul(L['ps'][lane][:, BANK + o * T:BANK + (o + 1) * T], W['WkT1'][:, c, o * P:(o + 1) * P],
                          L['qT'][:, lane, c * T:(c + 1) * T], start=(c == 0), stop=(c == KD - 1))
        for c in range(KD):
            mm = pe.matmul(L['ps'][lane][0:T, BANK + KD * T:BANK + KD * T + 1],
                           L['qT'][:, lane, c * T:(c + 1) * T], W['bk1'][:, c:c + 1],
                           start=(c == 0), stop=(c == KD - 1))
        mm.then_inc(h.sem('key_q1'), 1)
    yield
    attention_scores(pe, h, L, 0, pick(L, 'hT'), after(h, 'key_q1_copied'))
    yield
    turn_probs(pe, h, k, L, 0, after(h, 'probs_normed', 0))
    yield
    attend_t(pe, h, L, 0)
    yield
    project_t(pe, h, L, W['Wv1'], pick(L, 'qT'), after(h, 'attended_copied'), 0, 'v1_raw')
    yield
    turn_rows(pe, h, k, L, 1, pick(L, 'u'), lambda lane: (h.sem('turned_in'), 16 * (h.turn + 1)))
    yield
    for lane in h.lanes:
        pe.wait_ge(*h.at('turned_copied', 1, lane))
        rows_out(pe, L, lane, W['Wo1'], L['qT'][:, lane, :], KD, 1, D, W['bo1'], k['ones16']
                 ).then_inc(h.sem('o1'), 1)


def layer0_scalar(s, h, a, k, W, L, scratch):
    yield
    copy_context(s, h, L)
    yield
    copy_t(s, h, L, 0, pick(L, 'hT'), after(h, 'turned', 0), 'turned_copied')
    yield
    attention_exp(s, h, L, 0)
    yield
    copy_probs(s, h, L, 0)
    yield
    copy_t(s, h, L, 0, pick(L, 'hT'), after(h, 'turned', 1), 'turned_copied')
    for r in range(2):
        yield
        for lane in h.lanes:
            s.wait_ge(*h.at('gate_up', r, lane))
            s.activation(L['mid'][:, lane, 0:3 * T], L['ps'][lane][:, 0:3 * T], ACT.Tanh,
                         scale=INT8_SCALE / 2).then_inc(h.sem('gate_tanh'), 1)


def cross1_scalar(s, h, a, k, W, L, scratch):
    yield
    copy_t(s, h, L, 0, pick(L, 'hT'), after(h, 'turned', 0), 'turned_copied')
    yield
    copy_t(s, h, L, 0, pick(L, 'qT'), after(h, 'q1_raw'), 'q1', scale=W['qscale1'], bias=W['bq1s'])
    yield
    for lane in h.lanes:
        s.wait_ge(*h.at('key_q1', 0, lane))
        s.activation(L['hT'][:, lane, :], L['ps'][lane][:, BANK:BANK + KD * T], ACT.Copy)
        s.activation(L['row'][:, lane, :], L['ps'][lane][0:T, BANK + KD * T:BANK + KD * T + 1],
                     ACT.Copy).then_inc(h.sem('key_q1_copied'), 1)
    yield
    attention_exp(s, h, L, 0, from_psum=True)
    yield
    copy_probs(s, h, L, 0)
    yield
    copy_t(s, h, L, 1, pick(L, 'qT'), after(h, 'attended'), 'attended_copied')
    yield
    copy_t(s, h, L, 0, pick(L, 'hT'), after(h, 'v1_raw'), 'v1', bias=W['bv1'])
    yield
    copy_t(s, h, L, 0, pick(L, 'qT'), after(h, 'turned', 1), 'turned_copied')


def layer0_gpsimd(gp, h, a, k, W, L, scratch):
    yield
    for lane in h.lanes:
        gp.wait_ge(*h.landed('mask_in', lane))
        gp.tensor_scalar(L['mask'][:, lane, :], L['mid'][0:T, lane, 0:S_CTX].bitcast(I32), NEG, None,
                         ALU.mult).then_inc(h.sem('mask_ready'), 1)
    for i in range(2):
        yield
        norm_rstd(gp, h, L, i, k['minus_half'][0:T, 0:1])


def cross1_gpsimd(gp, h, a, k, W, L, scratch):
    yield
    norm_rstd(gp, h, L, 0, k['minus_half'][0:T, 0:1])


def updated_before(h):
    if h.before is None:
        return None
    return lambda lane: h.before.at('x_updated', h.before.uses.get('x_updated', 1) - 1, lane)


def update(v, h, L, bank, factor_of, done_sem, use):
    for lane in h.lanes:
        v.wait_ge(*h.at(done_sem, use, lane))
        v.scalar_tensor_tensor(L['x'][:, lane, :], L['ps'][lane][0:T, bank * BANK:bank * BANK + D],
                               factor_of(lane), L['x'][:, lane, :], ALU.mult,
                               ALU.add).then_inc(h.sem('x_updated'), 1)


def layer0_vector(v, h, a, k, W, L, scratch):
    gate = k['gate']
    x, xh = pick(L, 'x'), pick(L, 'xh')
    yield
    norm_stats(v, h, L, 0, x, lambda lane: h.landed('x_in', lane))
    yield
    norm_apply(v, h, L, 0, x, xh)
    yield
    attention_logits(v, h, L, 0, D ** -0.5, pick(L, 'mask'), after(h, 'mask_ready'))
    yield
    attention_norm(v, h, L, 0, gate[0:T, 0:1])
    yield
    for lane in h.lanes:
        v.wait_ge(*h.at('factor', 0, lane))
    update(v, h, L, 1, lambda lane: L['factor'][:, lane, 0:1], 'attended', 0)
    yield
    norm_stats(v, h, L, 1, x, after(h, 'x_updated', 0))
    yield
    norm_apply(v, h, L, 1, x, xh)
    for r in range(2):
        yield
        for lane in h.lanes:
            v.wait_ge(*h.at('gate_tanh', r, lane))
            v.scalar_tensor_tensor(L['wide'][:, lane, 0:3 * T], L['mid'][:, lane, 0:3 * T], 1.0,
                                   L['ps'][lane][:, 0:3 * T], ALU.add, ALU.mult
                                   ).then_inc(h.sem('gate_silu'), 1)
        for lane in h.lanes:
            v.wait_ge(*h.at('gate_silu', r, lane))
            v.scalar_tensor_tensor(L['block'][:, lane, r * 3 * T:(r + 1) * 3 * T],
                                   L['ps'][lane][:, BANK:BANK + 3 * T], INT8_SCALE * INT8_SCALE / 2,
                                   L['wide'][:, lane, 0:3 * T], ALU.mult, ALU.mult).then_inc(h.sem('hidden0'), 1)
    yield
    update(v, h, L, 0, lambda lane: W['gate_int8'][0:T, 0:1], 'down0', 0)


def cross1_vector(v, h, a, k, W, L, scratch):
    x, xh = pick(L, 'x'), pick(L, 'xh')
    yield
    norm_stats(v, h, L, 0, x, updated_before(h))
    yield
    norm_apply(v, h, L, 0, x, xh)
    yield
    for lane in h.lanes:
        v.wait_ge(*h.at('scores', 0, lane))
        v.tensor_reduce(L['nmax'][:, lane, 0:1], L['ps'][lane][0:T, BANK:BANK + S_CTX], AX.X, ALU.max,
                        negate=True).then_inc(h.sem('score_max'), 1)
    for lane in h.lanes:
        v.wait_ge(*h.at('score_max', 0, lane))
        v.tensor_scalar(L['nmax'][:, lane, 0:1], L['nmax'][:, lane, 0:1], L['row'][:, lane, 0:1],
                        L['row'][:, lane, 0:1], ALU.subtract, ALU.add).then_inc(h.sem('row_max'), 1)
    yield
    attention_norm(v, h, L, 0)
    yield
    update(v, h, L, 1, lambda lane: k['gate'][0:T, 1:2], 'o1', 0)



def turn_quantised(pe, h, k, L, i, width):
    for lane in h.lanes:
        pe.wait_ge(*h.at('quant', i, lane))
        q = L['block'][0:T, lane, 0:width // 2].bitcast(BF16)
        out = L['ps'][lane][:, 0:width // P * T // 2].bitcast(BF16)
        for c in range(width // P):
            t = pe.transpose(out[:, c * T:(c + 1) * T], q[:, c * P:(c + 1) * P], k['ident16'][0:T, 0:T])
        t.then_inc(h.sem('quant_turned'), 1)


def ffn1_tensor(pe, h, a, k, W, L, scratch):
    yield
    turn_quantised(pe, h, k, L, 0, D)
    yield
    for lane in h.lanes:
        pe.wait_ge(*h.at('quant_copied', 0, lane))
        qT = L['mid'][:, lane, 0:KD * T // 2].bitcast(BF16)
        for o in range(2):
            for c in range(KD):
                mm = pe.matmul(L['ps'][lane][0:T, o * BANK:(o + 1) * BANK], qT[:, c * T:(c + 1) * T],
                               W['w1q'][:, c, o * BANK:(o + 1) * BANK], start=(c == 0), stop=(c == KD - 1))
        mm.then_inc(h.sem('hidden1_raw'), 1)
    yield
    turn_quantised(pe, h, k, L, 1, F1)
    yield
    for lane in h.lanes:
        pe.wait_ge(*h.at('quant_copied', 1, lane))
        rows_out(pe, L, lane, W['w2q'], L['mid'][:, lane, 0:KF * T // 2].bitcast(BF16), KF, 1, D
                 ).then_inc(h.sem('ffn1_raw'), 1)
    yield
    turn_rows(pe, h, k, L, 0, pick(L, 'xh'), after(h, 'norm_out', 2))
    yield
    project_t(pe, h, L, W['WT2'], pick(L, 'hT'), after(h, 'turned_copied', 0), 0, 'q2_raw')
    yield
    attention_scores(pe, h, L, 0, pick(L, 'qT'), after(h, 'q2'))
    yield
    turn_probs(pe, h, k, L, 0, after(h, 'probs', 0))
    yield
    attend_rows(pe, h, L, 0)


def self2_tensor(pe, h, a, k, W, L, scratch):
    yield
    turn_rows(pe, h, k, L, 0, pick(L, 'u'), after(h, 'norm_out', 1))
    yield
    for lane in h.lanes:
        pe.wait_ge(*h.at('turned_copied', 0, lane))
        hT = L['hT'][:, lane, :]
        for bank in range(2):
            for o in range(KD):
                for c in range(KD):
                    pe.matmul(L['ps'][lane][:, bank * BANK + o * T:bank * BANK + (o + 1) * T],
                              W['w_qkv'][:, c, bank * D + o * P:bank * D + (o + 1) * P],
                              hT[:, c * T:(c + 1) * T], start=(c == 0), stop=(c == KD - 1))
        v_out = L['ps'][lane][0:T, D:2 * D]
        for c in range(KD):
            pe.matmul(v_out, hT[:, c * T:(c + 1) * T], W['w_qkv'][:, c, 2 * D:3 * D], start=(c == 0), stop=False)
        pe.matmul(v_out, k['ones16'][0:3, 0:T], W['bv2'], start=False, stop=True).then_inc(h.sem('qkv'), 1)
    for c in range(KD):
        yield
        for lane in h.lanes:
            pe.wait_ge(*h.at('key_blocks', c, lane))
            if c:
                pe.wait_ge(*h.at('self_shifted', 0, lane))
            for bank in range(2):
                out = L['ps'][lane][0:T, bank * BANK:bank * BANK + 4 * T]
                pe.matmul(out, k['ident16'][0:T, 0:T], W['causal16'][:, :], start=True, stop=False)
                mm = pe.matmul(out, L['qT'][:, lane, c * T:(c + 1) * T],
                               L['block'][:, lane, bank * 4 * T:(bank + 1) * 4 * T], start=False, stop=True)
            mm.then_inc(h.sem('self_scores'), 1)
    for r in range(HEADS // 4):
        yield
        for lane in h.lanes:
            pe.wait_ge(*h.at('self_probs', r // 2, lane))
            if r:
                pe.wait_ge(*h.at('self_copied', r - 1, lane))
            else:
                pe.wait_ge(*h.at('self_shifted', 1, lane))
            for j in range(4):
                t = pe.transpose(L['ps'][lane][0:T, j * T:(j + 1) * T],
                                 L['wide'][0:T, lane, (4 * r + j) * T:(4 * r + j + 1) * T], k['ident'][0:T, 0:T])
            t.then_inc(h.sem('self_turned'), 1)
        yield
        for lane in h.lanes:
            pe.wait_ge(*h.at('self_copied', r, lane))
            for j in range(4 * r, 4 * r + 4):
                mm = pe.matmul(L['ps'][lane][0:T, BANK + j * (HD + 1):BANK + (j + 1) * (HD + 1)],
                               L['mid'][0:T, lane, (j % 8) * T:(j % 8 + 1) * T],
                               L['mask'][:, lane, j * (HD + 1):(j + 1) * (HD + 1)], start=True, stop=True)
            mm.then_inc(h.sem('self_out'), 1)
    yield
    turn_rows(pe, h, k, L, 1, pick(L, 'u'), after(h, 'self_normed'))
    yield
    for lane in h.lanes:
        pe.wait_ge(*h.at('turned_copied', 1, lane))
        rows_out(pe, L, lane, W['w_proj'], L['hT'][:, lane, :], KD, 1, D, W['b_proj'], k['ones16']
                 ).then_inc(h.sem('self_proj'), 1)
    yield
    turn_rows(pe, h, k, L, 2, pick(L, 'u'), after(h, 'moe_bias'))
    yield
    for lane in h.lanes:
        pe.wait_ge(*h.at('turned_copied', 2, lane))
        rows_out(pe, L, lane, W['w_route'], L['hT'][:, lane, :], KD, 1, E, W['b_route'], k['ones16']
                 ).then_inc(h.sem('route'), 1)


def ffn1_scalar(s, h, a, k, W, L, scratch):
    for i, width in enumerate((D, F1)):
        if i:
            yield
            for lane in h.lanes:
                s.wait_ge(*h.at('hidden1', 0, lane))
                s.activation(L['wide'][0:T, lane, 0:F1], L['wide'][0:T, lane, 0:F1], ACT.Gelu
                             ).then_inc(h.sem('gelu1'), 1)
            yield
            for lane in h.lanes:
                s.wait_ge(*h.at('norm_shift', 0, lane))
                s.activation(L['wide'][0:T, lane, 0:F1], L['wide'][0:T, lane, 0:F1], ACT.Identity,
                             bias=L['shift'][:, lane, 0:1], scale=L['rstd'][:, lane, 0:1]
                             ).then_inc(h.sem('hidden1_normed'), 1)
        yield
        for lane in h.lanes:
            s.wait_ge(*h.at('quant_turned', i, lane))
            s.activation(L['mid'][:, lane, 0:width // P * T // 2].bitcast(BF16),
                         L['ps'][lane][:, 0:width // P * T // 2].bitcast(BF16), ACT.Copy
                         ).then_inc(h.sem('quant_copied'), 1)
    yield
    copy_t(s, h, L, 0, pick(L, 'hT'), after(h, 'turned', 0), 'turned_copied')
    yield
    copy_t(s, h, L, 0, pick(L, 'qT'), after(h, 'q2_raw'), 'q2', bias=W['b2x'])
    yield
    attention_exp(s, h, L, 0, from_psum=True)
    yield
    copy_probs(s, h, L, 0)


def self2_scalar(s, h, a, k, W, L, scratch):
    yield
    copy_t(s, h, L, 0, pick(L, 'hT'), after(h, 'turned', 0), 'turned_copied', scale=W['ln1_scale'],
           bias=W['ln1_bias'])
    yield
    for lane in h.lanes:
        s.wait_ge(*h.at('qkv', 0, lane))
        for c in range(KD):
            for bank, name, bias, scale in ((0, 'qT', 'bq2s', HD ** -0.5), (1, 'kT', 'bk2', 1.0)):
                s.activation(L[name][:, lane, c * T:(c + 1) * T],
                             L['ps'][lane][:, bank * BANK + c * T:bank * BANK + (c + 1) * T], ACT.Identity,
                             bias=W[bias][:, c:c + 1], scale=scale)
        s.wait_ge(*h.at('values_cleared', 0, lane))
        s.activation(L['mask'][:, lane, 0:HEADS * (HD + 1)].rearrange("p (h j) -> p h j", h=HEADS)[:, :, 0:HD],
                     L['ps'][lane][0:T, D:2 * D].rearrange("p (h j) -> p h j", h=HEADS), ACT.Copy
                     ).then_inc(h.sem('qkv_copied'), 1)
    for c in range(KD):
        yield
        for lane in h.lanes:
            s.wait_ge(*h.at('self_shifted', c, lane))
            w = L['wide'][0:T, lane, c * CH * T:(c + 1) * CH * T]
            s.activation(w, w, ACT.Exp).then_inc(h.sem('self_probs'), 1)
    for r in range(HEADS // 4):
        yield
        for lane in h.lanes:
            s.wait_ge(*h.at('self_turned', r, lane))
            s.activation(L['mid'][0:T, lane, (r % 2) * 4 * T:(r % 2 + 1) * 4 * T],
                         L['ps'][lane][0:T, 0:4 * T], ACT.Copy).then_inc(h.sem('self_copied'), 1)
    yield
    copy_t(s, h, L, 0, pick(L, 'hT'), after(h, 'turned', 1), 'turned_copied')
    yield
    copy_t(s, h, L, 0, pick(L, 'hT'), after(h, 'turned', 2), 'turned_copied')


def ffn1_gpsimd(gp, h, a, k, W, L, scratch):
    for i in range(4):
        yield
        norm_rstd(gp, h, L, i, k['minus_half'][0:T, 0:1])


def self2_gpsimd(gp, h, a, k, W, L, scratch):
    for i in range(3):
        yield
        norm_rstd(gp, h, L, i, k['minus_half'][0:T, 0:1])
        if i == 0:
            for lane in h.lanes:
                gp.memset(L['mask'][:, lane, 0:HEADS * (HD + 1)], 1.0).then_inc(h.sem('values_cleared'), 1)


def quantise(v, h, L, W, i, src_of, width):
    yield
    for lane in h.lanes:
        v.wait_ge(*h.at('quant_in', i, lane))
        v.tensor_reduce(L['absmax'][:, lane, :], src_of(lane), AX.X, ALU.max,
                        apply_absolute_value=True).then_inc(h.sem('quant_max'), 1)
    for lane in h.lanes:
        v.wait_ge(*h.at('quant_max', i, lane))
        v.tensor_scalar(L['step'][:, lane, :], L['absmax'][:, lane, :], EPS, INT8_SCALE, ALU.max,
                        ALU.mult).then_inc(h.sem('quant_step'), 1)
    for lane in h.lanes:
        v.wait_ge(*h.at('quant_step', i, lane))
        v.reciprocal(L['inv'][:, lane, :], L['step'][:, lane, :])
        v.tensor_scalar(L['dq'][:, lane, :], L['step'][:, lane, :], W['wscale'][0:T, i:i + 1], None,
                        ALU.mult).then_inc(h.sem('quant_inv'), 1)
    yield
    for lane in h.lanes:
        v.wait_ge(*h.at('quant_inv', i, lane))
        v.tensor_scalar(src_of(lane), src_of(lane), L['inv'][:, lane, :], MAGIC, ALU.mult,
                        ALU.add).then_inc(h.sem('quant_rounded'), 1)
    yield
    for lane in h.lanes:
        v.wait_ge(*h.at('quant_rounded', i, lane))
        v.tensor_scalar(L['block'][0:T, lane, 0:width // 2].bitcast(BF16), src_of(lane), -MAGIC, 127.0,
                        ALU.add, ALU.min).then_inc(h.sem('quant'), 1)


def ffn1_vector(v, h, a, k, W, L, scratch):
    gate = k['gate']
    x, xh, u = pick(L, 'x'), pick(L, 'xh'), pick(L, 'u')
    yield
    norm_stats(v, h, L, 0, x, updated_before(h))
    yield
    norm_apply(v, h, L, 0, x, xh)
    yield
    norm_stats(v, h, L, 1, xh, after(h, 'norm_out', 0))
    yield
    norm_apply(v, h, L, 1, xh, u)
    yield
    for lane in h.lanes:
        v.wait_ge(*h.at('norm_out', 1, lane))
        v.tensor_tensor(L['u'][:, lane, :], L['u'][:, lane, :], W['ln1_g'][:, :], ALU.mult
                        ).then_inc(h.sem('quant_gain'), 1)
    for lane in h.lanes:
        v.wait_ge(*h.at('quant_gain', 0, lane))
        v.tensor_tensor(L['u'][:, lane, :], L['u'][:, lane, :], W['ln1_b'][:, :], ALU.add
                        ).then_inc(h.sem('quant_in'), 1)
    yield from quantise(v, h, L, W, 0, u, D)
    hidden = lambda lane: L['wide'][0:T, lane, 0:F1]
    yield
    for lane in h.lanes:
        v.wait_ge(*h.at('hidden1_raw', 0, lane))
        v.scalar_tensor_tensor(hidden(lane), L['ps'][lane][0:T, 0:F1], L['dq'][:, lane, 0:1],
                               W['b1'][:, :], ALU.mult, ALU.add).then_inc(h.sem('hidden1'), 1)
    yield
    norm_stats(v, h, L, 2, hidden, after(h, 'gelu1'))
    yield
    for lane in h.lanes:
        v.wait_ge(*h.at('norm_rstd', 2, lane))
        v.tensor_scalar(L['shift'][:, lane, 0:1], L['mv'][:, lane, 0:1], L['rstd'][:, lane, 0:1], -1.0,
                        ALU.mult, ALU.mult).then_inc(h.sem('norm_shift'), 1)
    yield
    for lane in h.lanes:
        v.wait_ge(*h.at('hidden1_normed', 0, lane))
        v.tensor_tensor(hidden(lane), hidden(lane), W['ln2_g'][:, :], ALU.mult
                        ).then_inc(h.sem('hidden1_gained'), 1)
    yield
    for lane in h.lanes:
        v.wait_ge(*h.at('hidden1_gained', 0, lane))
        v.tensor_tensor(hidden(lane), hidden(lane), W['ln2_b'][:, :], ALU.add
                        ).then_inc(h.sem('quant_in'), 1)
    yield from quantise(v, h, L, W, 1, hidden, F1)
    yield
    for lane in h.lanes:
        v.wait_ge(*h.at('ffn1_raw', 0, lane))
        v.scalar_tensor_tensor(L['u'][:, lane, :], L['ps'][lane][0:T, BANK:BANK + D], L['dq'][:, lane, 0:1],
                               W['b2'][:, :], ALU.mult, ALU.add).then_inc(h.sem('ffn1'), 1)
    for lane in h.lanes:
        v.wait_ge(*h.at('ffn1', 0, lane))
        v.scalar_tensor_tensor(L['x'][:, lane, :], L['u'][:, lane, :], gate[0:T, 5:6], L['x'][:, lane, :],
                               ALU.mult, ALU.add).then_inc(h.sem('x_updated'), 1)
    yield
    norm_stats(v, h, L, 3, x, after(h, 'x_updated', 0))
    yield
    norm_apply(v, h, L, 3, x, xh)
    yield
    for lane in h.lanes:
        v.wait_ge(*h.at('scores', 0, lane))
        v.tensor_reduce(L['nmax'][:, lane, 0:1], L['ps'][lane][0:T, BANK:BANK + S_CTX], AX.X, ALU.max,
                        negate=True).then_inc(h.sem('row_max'), 1)
    yield
    attention_norm(v, h, L, 0, gate[0:T, 2:3])
    yield
    for lane in h.lanes:
        v.wait_ge(*h.at('factor', 0, lane))
    update(v, h, L, 1, lambda lane: L['factor'][:, lane, 0:1], 'attended', 0)


def self2_vector(v, h, a, k, W, L, scratch):
    x, xh, u = pick(L, 'x'), pick(L, 'xh'), pick(L, 'u')
    yield
    norm_stats(v, h, L, 0, x, updated_before(h))
    yield
    norm_apply(v, h, L, 0, x, xh)
    yield
    norm_stats(v, h, L, 1, xh, after(h, 'norm_out', 0))
    yield
    norm_apply(v, h, L, 1, xh, u)
    for c in range(KD):
        yield
        for lane in h.lanes:
            if c:
                v.wait_ge(*h.at('self_scores', 0, lane))
            else:
                v.wait_ge(*h.at('qkv_copied', 0, lane))
            v.tensor_tensor(L['block'][:, lane, :].rearrange("p (j t) -> p j t", j=CH),
                            L['kT'][:, lane, c * T:(c + 1) * T].unsqueeze(1).broadcast_to([P, CH, T]),
                            W['headmask'][:, :].unsqueeze(2).broadcast_to([P, CH, T]), ALU.mult
                            ).then_inc(h.sem('key_blocks'), 1)
        yield
        for lane in h.lanes:
            v.wait_ge(*h.at('self_scores', c, lane))
            for bank in range(2):
                last = v.tensor_reduce(L['by_head'][:, lane, c * CH + 4 * bank:c * CH + 4 * bank + 4],
                                       L['ps'][lane][0:T, bank * BANK:bank * BANK + 4 * T]
                                       .rearrange("p (j t) -> p j t", j=4), AX.X, ALU.max)
            last.then_inc(h.sem('self_max'), 1)
        for lane in h.lanes:
            v.wait_ge(*h.at('self_max', c, lane))
            for bank in range(2):
                j0 = c * CH + 4 * bank
                last = v.tensor_tensor(L['wide'][0:T, lane, j0 * T:(j0 + 4) * T].rearrange("p (j t) -> p j t", j=4),
                                       L['ps'][lane][0:T, bank * BANK:bank * BANK + 4 * T]
                                       .rearrange("p (j t) -> p j t", j=4),
                                       L['by_head'][:, lane, j0:j0 + 4].unsqueeze(2).broadcast_to([T, 4, T]),
                                       ALU.subtract)
            last.then_inc(h.sem('self_shifted'), 1)
    sums = lambda lane: L['ps'][lane][0:T, BANK:BANK + HEADS * (HD + 1)].rearrange("p (h j) -> p h j", h=HEADS)
    yield
    for lane in h.lanes:
        v.wait_ge(*h.at('self_out', 3, lane))
        v.reciprocal(L['by_head'][:, lane, :].unsqueeze(2), sums(lane)[:, :, HD:HD + 1]).then_inc(h.sem('self_rsum'), 1)
    for lane in h.lanes:
        v.wait_ge(*h.at('self_rsum', 0, lane))
        v.tensor_tensor(L['u'][:, lane, :].rearrange("p (h j) -> p h j", h=HEADS), sums(lane)[:, :, 0:HD],
                        L['by_head'][:, lane, :].unsqueeze(2).broadcast_to([T, HEADS, HD]), ALU.mult
                        ).then_inc(h.sem('self_normed'), 1)
    yield
    for lane in h.lanes:
        v.wait_ge(*h.at('self_proj', 0, lane))
        v.tensor_tensor(L['xh'][:, lane, :], L['ps'][lane][0:T, BANK:BANK + D], L['xh'][:, lane, :],
                        ALU.add).then_inc(h.sem('res2'), 1)
    yield
    norm_stats(v, h, L, 2, xh, after(h, 'res2'))
    yield
    norm_apply(v, h, L, 2, xh, u)
    yield
    for lane in h.lanes:
        v.wait_ge(*h.at('norm_out', 2, lane))
        v.tensor_tensor(L['u'][:, lane, :], L['u'][:, lane, :], W['ln2_scale'][:, :], ALU.mult
                        ).then_inc(h.sem('moe_gain'), 1)
    for lane in h.lanes:
        v.wait_ge(*h.at('moe_gain', 0, lane))
        v.tensor_tensor(L['u'][:, lane, :], L['u'][:, lane, :], W['ln2_bias'][:, :], ALU.add
                        ).then_inc(h.sem('moe_bias'), 1)
    yield
    for lane in h.lanes:
        v.wait_ge(*h.at('route', 0, lane))
        v.tensor_copy(L['logit'][:, lane, :], L['ps'][lane][0:T, BANK:BANK + E]
                      ).then_inc(h.sem('route_copied'), 1)


FIRST_PROGRAMS = {
    'layer0': {'sync': layer0_sync, 'tensor': layer0_tensor, 'scalar': layer0_scalar,
               'gpsimd': layer0_gpsimd, 'vector': layer0_vector},
    'cross1': {'sync': cross1_sync, 'tensor': cross1_tensor, 'scalar': cross1_scalar,
               'gpsimd': cross1_gpsimd, 'vector': cross1_vector},
    'ffn1': {'tensor': ffn1_tensor, 'scalar': ffn1_scalar, 'gpsimd': ffn1_gpsimd, 'vector': ffn1_vector},
    'self2': {'sync': self2_sync, 'tensor': self2_tensor, 'scalar': self2_scalar,
              'gpsimd': self2_gpsimd, 'vector': self2_vector},
}
FIRST_USES = {
    'layer0': {'turned': 2, 'gate_up': 2, 'turned_copied': 2, 'gate_tanh': 2, 'norm_var': 2, 'norm_rstd':
              2, 'norm_stats': 2, 'norm_aggr': 2, 'norm_out': 2, 'x_updated': 2, 'gate_silu': 2,
              'hidden0': 2},
    'cross1': {'turned': 2, 'turned_copied': 2},
    'ffn1': {'quant_turned': 2, 'quant_copied': 2, 'norm_var': 4, 'norm_rstd': 4, 'norm_stats': 4,
              'norm_aggr': 4, 'norm_out': 3, 'quant_in': 2, 'quant_max': 2, 'quant_step': 2,
              'quant_inv': 2, 'quant_rounded': 2, 'quant': 2, 'x_updated': 2},
    'self2': {'turned': 3, 'self_scores': 2, 'self_turned': 4, 'self_out': 4, 'turned_copied': 3,
              'self_probs': 2, 'self_copied': 4, 'norm_var': 3, 'norm_rstd': 3, 'norm_stats': 3,
              'norm_aggr': 3, 'norm_out': 3, 'key_blocks': 2, 'self_max': 2, 'self_shifted': 2},
}
FIRST_PERIOD = 4764
FIRST_TIMES = {
    'layer0': {
        'sync': (506,),
        'tensor': (376, 1628, 1734, 2297, 2501, 3378, 3483, 3926, 4407),
        'scalar': (463, 1667, 2225, 2388, 3417, 3761, 4203),
        'gpsimd': (738, 980, 3249),
        'vector': (915, 1064, 2109, 3101, 3139, 3177, 3318, 3809, 4251, 4686),
    },
    'cross1': {
        'sync': (1979, 2205),
        'tensor': (205, 290, 485, 705, 1101, 1205, 1648, 2716, 2801),
        'scalar': (244, 396, 633, 928, 1150, 1354, 1916, 2755),
        'gpsimd': (64,),
        'vector': (0, 141, 851, 1000, 3359),
    },
    'ffn1': {
        'tensor': (1150, 1351, 3121, 3286, 3741, 3840, 4281, 4667, 4771),
        'scalar': (1305, 1821, 2275, 3181, 3794, 3945, 4501, 4716),
        'gpsimd': (273, 478, 2122, 3550),
        'vector': (209, 350, 395, 555, 666, 757, 967, 1097, 1458, 1971, 2212, 2442, 2568, 2693,
                   2863, 2988, 3394, 3485, 3626, 4444, 4719, 4920),
    },
    'self2': {
        'sync': (286, 4392, 4669, 5025),
        'tensor': (686, 832, 1440, 1991, 2462, 2630, 2736, 2899, 2984, 3162, 3247, 3398, 3760,
                   4183, 4696, 4901),
        'scalar': (725, 1183, 2094, 2455, 2539, 2794, 3043, 3306, 3818, 4749),
        'gpsimd': (344, 557, 4456),
        'vector': (268, 447, 492, 633, 1320, 1648, 1872, 2218, 3537, 4346, 4392, 4533, 4578, 5005),
    },
}
FIRST_CHAIN = Chain(FIRST_PROGRAMS, FIRST_USES, FIRST_TIMES, FIRST_PERIOD, STORES + ('ctx_in',))


def phase_one(nc, a, k, scratch):
    with ExitStack() as stack:
        m = Machine(nc, stack, 'one')
        W = {}
        for name, rows, cols in [('w_gateT', D, H0), ('w_upT', D, H0), ('w_downT', H0, D), ('Wq1', D, D),
                                 ('WkT1', D, D), ('Wv1', D, D), ('Wo1', D, D), ('WT2', D, D),
                                 ('w_qkv', D, 3 * D), ('w_proj', D, D), ('w_route', D, E)]:
            W[name] = m.sb(name, [P, rows // P, cols])
        for name in ['bq1', 'bq1s', 'qscale1', 'bk1', 'bv1', 'b2x', 'ln1_scale', 'ln1_bias', 'bq2', 'bq2s', 'bk2']:
            W[name] = m.sb(name, [P, KD])
        W['bias_rows'] = m.sb('bias_rows', [3, 3 * D + E], BF16)
        for j, (name, cols) in enumerate([('bo1', D), ('bv2', D), ('b_proj', D), ('b_route', E)]):
            W[name] = W['bias_rows'][:, j * D:j * D + cols]
        for name, cols in [('ln1_g', D), ('ln1_b', D), ('b1', F1), ('ln2_g', F1), ('ln2_b', F1), ('b2', D),
                           ('ln2_scale', D), ('ln2_bias', D)]:
            W[name] = m.sb(name, [T, cols])
        W['w1q'] = m.sb('w1q', [P, KD, F1], BF16)
        W['w2q'] = m.sb('w2q', [P, KF, D], BF16)
        W['wscale'] = m.sb('wscale', [P, 2])
        W['headmask'] = m.sb('headmask', [P, CH])
        W['causal16'] = m.sb('causal16', [T, 4 * T], BF16)
        W['gate_int8'] = m.sb('gate_int8', [P, 1])
        load_weights(nc, a, k, W, scratch)

        L = lane_buffers(m, [('x', T, [D]), ('xh', T, [D]), ('u', T, [D]), ('hT', P, [KD * T]),
                             ('qT', P, [KD * T]), ('kT', P, [KD * T]), ('ctx', SC, [NSC, D]),
                             ('ctxT', P, [KD, S_CTX]), ('mask', T, [S_CTX]), ('block', P, [CH * T]),
                             ('wide', P, [HEADS * T]), ('mid', P, [CH * T]),
                             ('stats', T, [12]), ('mv', T, [2]), ('var', T, [1]), ('rstd', T, [1]),
                             ('nmax', T, [1]), ('sum', T, [1]), ('rsum', T, [1]), ('factor', T, [1]),
                             ('row', T, [1]), ('absmax', T, [1]), ('step', T, [1]), ('inv', T, [1]),
                             ('dq', T, [1]), ('by_head', T, [HEADS]), ('shift', T, [1]),
                             ('logit', T, [E])])

        with nc.Block() as block:
            @block.sync
            def _(sync):
                load_context(sync, m, L, a['ctx_1024'], 0, 'self2_ctx_in')
                for lane in range(LANES):
                    sync.wait_ge(m.sem(f'self2_ctx_in{lane}'), 16)
        m.clear_all()

        run_chain(nc, m, FIRST_CHAIN, 2 * LANES, a, k, W, L, scratch)


def load_weights(nc, a, k, W, scratch):
    with ExitStack() as stack:
        m = Machine(nc, stack, 'load')
        w1, w2 = m.sb('w1_raw', [P, KD, F1]), m.sb('w2_raw', [P, KF, D])
        total = m.sb('abs_total', [P, 2])
        inv = m.sb('w_inv', [P, 2])
        causal = m.sb('causal', [T, 4 * T])
        bias_row, bias_parts = m.sb('bias_row', [1, 3 * D + E]), m.sb('bias_parts', [1, 3, 3 * D + E], BF16)
        mean_ps = m.ps('mean_ps', [P, 2])

        with nc.Block() as block:
            @block.vector
            def _(v):
                v.memset(k['zeros'][:, :], 0.0)

        with nc.Block() as block:
            @block.sync
            def _(sync):
                loads = 0
                for tile, name in ((w1, 'w1T'), (w2, 'w2T')):
                    sync.dma_start(tile[:, :, :], a[name].rearrange("(c p) n -> p c n", p=P)
                                   ).then_inc(m.sem('w12_in'), 16)
                for name, src in (('Wq1', 'L1_xattn_Wq'), ('WkT1', 'WkT1'), ('Wv1', 'L1_xattn_Wv'),
                                  ('Wo1', 'L1_xattn_Wo'), ('WT2', 'WT2'), ('w_qkv', 'L2_ffn_w_qkv'),
                                  ('w_proj', 'L2_ffn_w_attnproj'), ('w_route', 'L2_ffn_w_gate')):
                    sync.dma_start(W[name][:, :, :], a[src].rearrange("(c p) n -> p c n", p=P)
                                   ).then_inc(m.sem('rest_in'), 16)
                    loads += 1
                for name, src in (('ln1_g', 'L1_ffn_ln1_g'), ('ln1_b', 'L1_ffn_ln1_b'), ('b1', 'L1_ffn_b1'),
                                  ('ln2_g', 'L1_ffn_ln2_g'), ('ln2_b', 'L1_ffn_ln2_b'), ('b2', 'L1_ffn_b2'),
                                  ('ln2_scale', 'L2_ffn_ln2_scale'), ('ln2_bias', 'L2_ffn_ln2_bias')):
                    sync.dma_start(W[name][:, :], a[src].partition_broadcast(T)).then_inc(m.sem('rest_in'), 16)
                    loads += 1
                sync.wait_ge(m.sem('split'), 1)
                for j in range(3):
                    sync.dma_start(W['bias_rows'][j:j + 1, :], bias_parts[:, j, :]
                                   ).then_inc(m.sem('parts_placed'), 16)
                sync.wait_ge(m.sem('parts_placed'), 48)
                sync.wait_ge(m.sem('rest_in'), 16 * loads)

            @block.scalar
            def _(s):
                for name in ('w_gateT', 'w_upT', 'w_downT'):
                    s.dma_start(W[name][:, :, :].bitcast(I32), a[name].rearrange("(c p) n -> p c n", p=P)
                                   ).then_inc(m.sem('ints_in'), 16)
                bq = a['L2_ffn_b_qkv']
                with nc.allow_non_contiguous_dma(reason="a few hundred bias values, once"):
                    for name, src in (('bq1', a['L1_xattn_bq']), ('bq2', bq[0:D])):
                        s.dma_start(W[name][:, :], src.rearrange("(c p) -> p c", p=P)
                                       ).then_inc(m.sem('queries_in'), 16)
                    for name, src in (('bk1', a['L1_xattn_bk']),
                                      ('bv1', a['L1_xattn_bv']), ('b2x', a['L2_xattn_b']),
                                      ('ln1_scale', a['L2_ffn_ln1_scale']), ('ln1_bias', a['L2_ffn_ln1_bias']),
                                      ('bk2', bq[D:2 * D])):
                        s.dma_start(W[name][:, :], src.rearrange("(c p) -> p c", p=P)
                                       ).then_inc(m.sem('features_in'), 16)
                for j, src in enumerate((a['L1_xattn_bo'], bq[2 * D:3 * D], a['L2_ffn_b_attnproj'],
                                         a['L2_ffn_b_gate'])):
                    s.dma_start(bias_row[:, j * D:j * D + src.shape[0]], src.partition_broadcast(1)
                                   ).then_inc(m.sem('biases_in'), 16)
                s.wait_ge(m.sem('features_in'), 16 * 6)
                s.wait_ge(m.sem('queries_in'), 32)
                zero_fill(s, k, scratch)

            @block.gpsimd
            def _(g):
                g.affine_select(W['headmask'][:, :], k['ones'][:, 0:CH], [[-HD, CH]], ALU.is_ge, 0.0,
                                base=0, channel_multiplier=1).then_inc(m.sem('masks'), 1)
                g.wait_ge(m.sem('masks'), 1)
                g.affine_select(W['headmask'][:, :], W['headmask'][:, :], [[HD, CH]], ALU.is_ge, 0.0,
                                base=HD - 1, channel_multiplier=-1)
                g.memset(causal[:, :], 0.0).then_inc(m.sem('masks'), 1)
                g.wait_ge(m.sem('masks'), 2)
                g.affine_select(causal[:, :], causal[:, :], [[0, 4], [-1, T]], ALU.is_ge, -1e30,
                                base=0, channel_multiplier=1).then_inc(m.sem('masks'), 1)

            @block.tensor
            def _(pe):
                pe.wait_ge(m.sem('abs_sums'), 2)
                pe.matmul(mean_ps[:, :], k['ones'][:, :], total[:, :], start=True, stop=True
                          ).then_inc(m.sem('abs_totals'), 1)

            @block.vector
            def _(v):
                v.wait_ge(m.sem('w12_in'), 32)
                for i, w in enumerate((w1, w2)):
                    v.tensor_reduce(total[:, i:i + 1], w[:, :, :], AX.XY, ALU.add, apply_absolute_value=True
                                    ).then_inc(m.sem('abs_sums'), 1)
                v.wait_ge(m.sem('ints_in'), 48)
                for name in ('w_gateT', 'w_upT', 'w_downT'):
                    v.tensor_copy(W[name][:, :, :], W[name][:, :, :].bitcast(I32))
                v.tensor_scalar(W['gate_int8'][:, :], k['gate'][:, 4:5], INT8_SCALE, None, ALU.mult)
                v.wait_ge(m.sem('abs_totals'), 1)
                v.tensor_scalar(W['wscale'][:, :], mean_ps[:, :], 1.0 / (D * F1), EPS, ALU.mult, ALU.max
                                ).then_inc(m.sem('w_mean'), 1)
                v.wait_ge(m.sem('w_mean'), 1)
                v.reciprocal(inv[:, :], W['wscale'][:, :]).then_inc(m.sem('w_mean'), 1)
                v.wait_ge(m.sem('w_mean'), 2)
                for i, w in enumerate((w1, w2)):
                    v.tensor_scalar(w[:, :, :], w[:, :, :], inv[:, i:i + 1], 1.0, ALU.mult, ALU.min
                                    ).then_inc(m.sem('w_step'), 1)
                for i, w in enumerate((w1, w2)):
                    v.wait_ge(m.sem('w_step'), 2)
                    v.tensor_scalar(w[:, :, :], w[:, :, :], -1.0, MAGIC, ALU.max, ALU.add
                                    ).then_inc(m.sem('w_step2'), 1)
                v.wait_ge(m.sem('w_step2'), 2)
                for w, q in ((w1, 'w1q'), (w2, 'w2q')):
                    v.tensor_scalar(W[q][:, :, :], w[:, :, :], -MAGIC, None, ALU.add)
                v.memset(W['qscale1'][:, :], D ** -0.5)
                v.wait_ge(m.sem('queries_in'), 32)
                v.tensor_scalar(W['bq1s'][:, :], W['bq1'][:, :], D ** -0.5, None, ALU.mult)
                v.tensor_scalar(W['bq2s'][:, :], W['bq2'][:, :], HD ** -0.5, None, ALU.mult)
                v.wait_ge(m.sem('masks'), 3)
                v.tensor_copy(W['causal16'][:, :], causal[:, :])
                v.wait_ge(m.sem('biases_in'), 64)
                split_three(v, m, 0, bias_row[:, :], [bias_parts[:, j, :] for j in range(3)])
        m.clear_all()



def zero_fill(queue, k, scratch):
    for name, rows in (('moe_x2', NBLK * BLK), ('moe_x3', E * CAP)):
        flat = scratch[name][0:rows, :].rearrange("r w -> (r w)").rearrange("(p f) -> p f", p=P)
        width = scratch[name].shape[1]
        times = flat.shape[1] // width
        queue.dma_start(flat.rearrange("p (j w) -> p j w", w=width),
                        k['zeros'][:, 0:width].unsqueeze(1).broadcast_to([P, times, width])
                        ).then_inc(k['zeroed'], 16)


def spread(ap, shape):
    return ap.unsqueeze(2).broadcast_to(shape)


def route_block(nc, a, k, scratch, name, top_k, finish, extra, prefetch=None):
    with ExitStack() as stack:
        m = Machine(nc, stack, name)
        R = {t: m.sb('route_' + t, [T, B, E]) for t in
             ('p', 'eq', 'prio', 'oh0', 'oh1', 'taken', 'slot', 'tmp')}
        for t in ('max', 'sum', 'pm0', 'pm1', 'prio_max', 'slot0', 'slot1'):
            R[t] = m.sb('route_' + t, [T, B])
        for t in ('total', 'before'):
            R[t] = m.sb('route_' + t, [T, E, B])
        for t in ('count', 'blocks', 'blocks_to', 'blocks_before', 'base', 'rank', 'ones8'):
            R[t] = m.sb('route_' + t, [T, E])
        R['iota_i'] = m.sb('route_iota_i', [T, 128], I32)
        R['iota'] = m.sb('route_iota', [T, 128])
        R['ones32'] = m.sb('route_ones32', [T, B])
        R['part_i'] = m.sb('route_part_i', [T, 1], I32)
        R['part'] = m.sb('route_part', [T, 1])
        R['ranks'] = m.ps('route_ranks', [P, BANK])
        R['totals'] = m.ps('route_totals', [P, BANK])
        full = [T, B, E]
        extra(m, R)

        with nc.Block() as block:
            @block.sync
            def _(sync):
                sync.dma_start(R['p'][:, :, :], scratch[name].rearrange("(b t) e -> t b e", t=T)
                               ).then_inc(m.sem('logits_in'), 16)
                if prefetch is not None:
                    sync.wait_ge(m.sem('logits_in'), 16)
                    prefetch(sync, sync)

            @block.gpsimd
            def _(g):
                g.iota(R['iota_i'][:, :], [[1, 128]], base=0, channel_multiplier=0)
                g.iota(R['part_i'][:, :], [[0, 1]], base=0, channel_multiplier=1).then_inc(m.sem('iota'), 1)

            @block.scalar
            def _(s):
                s.wait_ge(m.sem('shifted'), 1)
                s.activation(R['p'][:, :, :], R['p'][:, :, :], ACT.Exp).then_inc(m.sem('exp'), 1)

            @block.tensor
            def _(pe):
                pe.wait_ge(m.sem('taken'), 1)
                pe.matmul(R['ranks'][0:T, 0:B * E], k['tri'][0:T, 0:T],
                          R['taken'][:, :, :].rearrange("p b e -> p (b e)"), start=True, stop=True)
                pe.matmul(R['totals'][0:T, 0:B * E], k['ones'][0:T, 0:T],
                          R['taken'][:, :, :].rearrange("p b e -> p (b e)"), start=True, stop=True
                          ).then_inc(m.sem('ranked'), 1)

            @block.vector
            def _(v):
                v.memset(R['ones32'][:, :], 1.0)
                v.memset(R['ones8'][:, :], 1.0)
                v.wait_ge(m.sem('iota'), 1)
                v.tensor_copy(R['iota'][:, :], R['iota_i'][:, :]).then_inc(m.sem('iota_f'), 1)
                v.tensor_copy(R['part'][:, :], R['part_i'][:, :])
                v.wait_ge(m.sem('iota_f'), 1)
                v.tensor_scalar(R['rank'][:, :], R['iota'][:, 0:E], -1.0, float(E), ALU.mult, ALU.add)
                v.wait_ge(m.sem('logits_in'), 16)
                v.tensor_reduce(R['max'][:, :], R['p'][:, :, :], AX.X, ALU.max).then_inc(m.sem('max'), 1)
                v.wait_ge(m.sem('max'), 1)
                v.tensor_tensor(R['p'][:, :, :], R['p'][:, :, :], spread(R['max'][:, :], full), ALU.subtract
                                ).then_inc(m.sem('shifted'), 1)
                v.wait_ge(m.sem('exp'), 1)
                v.tensor_reduce(R['sum'][:, :], R['p'][:, :, :], AX.X, ALU.add).then_inc(m.sem('sum'), 1)
                v.wait_ge(m.sem('sum'), 1)
                v.reciprocal(R['sum'][:, :], R['sum'][:, :]).then_inc(m.sem('sum'), 1)
                v.wait_ge(m.sem('sum'), 2)
                v.tensor_tensor(R['p'][:, :, :], R['p'][:, :, :], spread(R['sum'][:, :], full), ALU.mult
                                ).then_inc(m.sem('probs'), 1)
                for c in range(top_k):
                    pm, oh = R[f'pm{c}'], R[f'oh{c}']
                    v.wait_ge(m.sem('probs'), c + 1)
                    v.tensor_reduce(pm[:, :], R['p'][:, :, :], AX.X, ALU.max).then_inc(m.sem('pm'), 1)
                    v.wait_ge(m.sem('pm'), c + 1)
                    v.tensor_tensor(R['eq'][:, :, :], R['p'][:, :, :], spread(pm[:, :], full), ALU.is_equal
                                    ).then_inc(m.sem('equal'), 1)
                    v.wait_ge(m.sem('equal'), c + 1)
                    v.tensor_tensor(R['prio'][:, :, :], R['eq'][:, :, :],
                                    R['rank'][:, :].unsqueeze(1).broadcast_to(full), ALU.mult
                                    ).then_inc(m.sem('prio'), 1)
                    v.wait_ge(m.sem('prio'), c + 1)
                    v.tensor_reduce(R['prio_max'][:, :], R['prio'][:, :, :], AX.X, ALU.max
                                    ).then_inc(m.sem('prio_max'), 1)
                    v.wait_ge(m.sem('prio_max'), c + 1)
                    v.tensor_tensor(oh[:, :, :], R['prio'][:, :, :], spread(R['prio_max'][:, :], full),
                                    ALU.is_equal).then_inc(m.sem('one_hot'), 1)
                    v.wait_ge(m.sem('one_hot'), c + 1)
                    if c + 1 < top_k:
                        v.scalar_tensor_tensor(R['p'][:, :, :], oh[:, :, :], -2.0, R['p'][:, :, :], ALU.mult,
                                               ALU.add).then_inc(m.sem('probs'), 1)
                if top_k == 2:
                    v.tensor_tensor(R['taken'][:, :, :], R['oh0'][:, :, :], R['oh1'][:, :, :], ALU.add
                                    ).then_inc(m.sem('taken'), 1)
                else:
                    v.tensor_copy(R['taken'][:, :, :], R['oh0'][:, :, :]).then_inc(m.sem('taken'), 1)
                v.wait_ge(m.sem('ranked'), 1)
                v.tensor_copy(R['total'][:, :, :], R['totals'][0:T, 0:B * E].rearrange("p (b e) -> p e b", e=E)
                              ).then_inc(m.sem('total'), 1)
                v.wait_ge(m.sem('total'), 1)
                for e in range(E):
                    last = v.tensor_tensor_scan(R['before'][:, e, :], R['ones32'][:, :], R['total'][:, e, :],
                                                0.0, ALU.mult, ALU.add)
                last.then_inc(m.sem('running'), 1)
                v.wait_ge(m.sem('running'), 1)
                v.tensor_copy(R['count'][:, :], R['before'][:, :, B - 1]).then_inc(m.sem('count'), 1)
                v.wait_ge(m.sem('count'), 1)
                v.tensor_tensor(R['before'][:, :, :], R['before'][:, :, :], R['total'][:, :, :], ALU.subtract
                                ).then_inc(m.sem('before'), 1)
                v.wait_ge(m.sem('before'), 1)
                finish(v, m, R)
        m.clear_all()


def slots_of(v, m, R, k, c, count):
    v.tensor_tensor(R['tmp'][:, :, :], R[f'oh{c}'][:, :, :], R['slot'][:, :, :], ALU.mult
                    ).then_inc(m.sem('slot_pick'), 1)
    v.wait_ge(m.sem('slot_pick'), count)
    v.tensor_reduce(R[f'slot{c}'][:, :], R['tmp'][:, :, :], AX.X, ALU.add).then_inc(m.sem('slot_sum'), 1)
    v.wait_ge(m.sem('slot_sum'), count)


def phase_route_two(nc, a, k, scratch, K2, prefetch):
    NJ = TOKENS // BLK

    def finish(v, m, R):
        with_blocks = R['cmp']
        v.tensor_scalar(R['mult'][:, :], R['iota'][:, 0:NJ], float(BLK), None, ALU.mult
                        ).then_inc(m.sem('steps'), 1)
        v.wait_ge(m.sem('steps'), 1)
        v.tensor_tensor(with_blocks[:, :, 0:NJ], R['count'][:, :].unsqueeze(2).broadcast_to([T, E, NJ]),
                        R['mult'][:, :].unsqueeze(1).broadcast_to([T, E, NJ]), ALU.is_gt
                        ).then_inc(m.sem('steps'), 1)
        v.wait_ge(m.sem('steps'), 2)
        v.tensor_reduce(R['blocks'][:, :], with_blocks[:, :, 0:NJ], AX.X, ALU.add).then_inc(m.sem('steps'), 1)
        v.wait_ge(m.sem('steps'), 3)
        v.tensor_tensor_scan(R['blocks_to'][:, :], R['ones8'][:, :], R['blocks'][:, :], 0.0, ALU.mult, ALU.add
                             ).then_inc(m.sem('steps'), 1)
        v.wait_ge(m.sem('steps'), 4)
        v.tensor_tensor(R['blocks_before'][:, :], R['blocks_to'][:, :], R['blocks'][:, :], ALU.subtract
                        ).then_inc(m.sem('steps'), 1)
        v.wait_ge(m.sem('steps'), 5)
        v.tensor_scalar(R['base'][:, :], R['blocks_before'][:, :], float(BLK), -1.0, ALU.mult, ALU.add
                        ).then_inc(m.sem('steps'), 1)
        v.wait_ge(m.sem('steps'), 6)
        v.tensor_tensor(R['before'][:, :, :], R['before'][:, :, :],
                        R['base'][:, :].unsqueeze(2).broadcast_to([T, E, B]), ALU.add).then_inc(m.sem('steps'), 1)
        v.wait_ge(m.sem('steps'), 7)
        v.tensor_tensor(R['slot'][:, :, :], R['ranks'][0:T, 0:B * E].rearrange("p (b e) -> p b e", e=E),
                        R['before'][:, :, :].rearrange("p e b -> p b e"), ALU.add).then_inc(m.sem('steps'), 1)
        v.wait_ge(m.sem('steps'), 8)
        for c in range(2):
            slots_of(v, m, R, k, c, c + 1)
            v.tensor_copy(K2['slot'][:, c, :], R[f'slot{c}'][:, :])
            v.tensor_copy(K2['weight'][:, c, :], R[f'pm{c}'][:, :])
        v.tensor_tensor(R['passed'][:, :, :], R['iota'][:, 0:NBLK].unsqueeze(2).broadcast_to([T, NBLK, E]),
                        R['blocks_to'][:, :].unsqueeze(1).broadcast_to([T, NBLK, E]), ALU.is_ge
                        ).then_inc(m.sem('steps'), 1)
        v.wait_ge(m.sem('steps'), 9)
        v.tensor_reduce(R['expert'][:, :], R['passed'][:, :, :], AX.X, ALU.add).then_inc(m.sem('steps'), 1)
        v.wait_ge(m.sem('steps'), 10)
        v.tensor_tensor(R['passed'][:, :, :], R['passed'][:, :, :],
                        R['blocks'][:, :].unsqueeze(1).broadcast_to([T, NBLK, E]), ALU.mult
                        ).then_inc(m.sem('steps'), 1)
        v.wait_ge(m.sem('steps'), 11)
        v.tensor_scalar(R['expert'][:, :], R['expert'][:, :], float(E - 1), None, ALU.min
                        ).then_inc(m.sem('steps'), 1)
        v.tensor_reduce(R['row'][:, :], R['passed'][:, :, :], AX.X, ALU.add).then_inc(m.sem('steps'), 1)
        v.wait_ge(m.sem('steps'), 13)
        v.tensor_copy(K2['expert'][:, :], R['expert'][0:1, :])
        for turn in range(2):
            v.tensor_scalar(R['wrap'][:, :], R['part'][:, :], float(E), -float(E), ALU.is_ge, ALU.mult
                            ).then_inc(m.sem('wrap'), 1)
            v.wait_ge(m.sem('wrap'), 2 * turn + 1)
            v.tensor_tensor(R['part'][:, :], R['part'][:, :], R['wrap'][:, :], ALU.add).then_inc(m.sem('wrap'), 1)
            v.wait_ge(m.sem('wrap'), 2 * turn + 2)
        v.tensor_scalar(K2['one_hot'][:, :], R['expert'][0:3 * E, :], R['part'][0:3 * E, 0:1], None, ALU.is_equal)
        v.tensor_tensor(R['row'][:, :], R['iota'][:, 0:NBLK], R['row'][:, :], ALU.subtract
                        ).then_inc(m.sem('steps'), 1)
        v.wait_ge(m.sem('steps'), 14)
        v.tensor_scalar(K2['row'][:, :], R['row'][0:1, :], float(NJ - 1), None, ALU.min)

    extra = lambda m, R: R.update(wrap=m.sb('route_wrap', [T, 1]), cmp=m.sb('route_cmp', [T, E, NJ]),
                                  mult=m.sb('route_mult', [T, NJ]),
                                  passed=m.sb('route_passed', [T, NBLK, E]),
                                  expert=m.sb('route_expert', [T, NBLK]), row=m.sb('route_row', [T, NBLK]))
    route_block(nc, a, k, scratch, 'route2', 2, finish, extra, prefetch)


AT_ONCE = 16


def phase_scatter(nc, k, scratch, src, dst, slot, weight, copies):
    width = D + (1 if weight is not None else 0)
    with ExitStack() as stack:
        m = Machine(nc, stack, f'scatter{copies}')
        rows = m.sb('scatter_rows', [T, AT_ONCE, copies, width])
        index = m.sb('scatter_index', [T, AT_ONCE, copies], U32)
        scattered = k['pool_dma'][f'scattered{copies}']
        with nc.Fori(0, B // AT_ONCE) as g:
            with nc.Block() as block:
                @block.sync
                def _(sync):
                    sync.wait_ge(k['zeroed'], 32)
                    for i in range(AT_ONCE):
                        for c in range(copies):
                            sync.dma_start(rows[:, i, c, 0:D], src[bass.ds((g * AT_ONCE + i) * T, T), :]
                                           ).then_inc(m.sem(f'rows_in{i}'), 16)

                @block.vector
                def _(v):
                    for i in range(AT_ONCE):
                        b = g * AT_ONCE + i
                        for c in range(copies):
                            if weight is not None:
                                v.tensor_copy(rows[:, i, c, D:D + 1], weight[:, c, bass.ds(b, 1)])
                            last = v.tensor_copy(index[:, i, c:c + 1], slot[:, c, bass.ds(b, 1)])
                        last.then_inc(m.sem('indexed'), 1)

                @block.gpsimd
                def _(gp):
                    for i in range(AT_ONCE):
                        gp.wait_ge(m.sem(f'rows_in{i}'), 16 * copies)
                        gp.wait_ge(m.sem('indexed'), i + 1)
                        for c in range(copies):
                            gp.indirect_dma_start(dst, bass.IndirectOffsetOnAxis(ap=index[:, i, c:c + 1], axis=0),
                                                  rows[:, i, c, :], None).then_inc(scattered, 16)
                    gp.wait_ge(scattered, (g + 1) * (16 * AT_ONCE * copies))
            m.clear_all()



STEP = 21
RING = 7
assert NBLK % STEP == 0 and STEP % RING == 0


def load_experts_two(queue_a, queue_b, a, X):
    for e in range(E):
        queue_a.dma_start(X['w_fc'][:, e, :, :], a['L2_ffn_w_fc'][e].rearrange("(c p) n -> p c n", p=P)
                          ).then_inc(X['fc_in'], 16)
        queue_b.dma_start(X['w_out'][:, e, :, :], a['L2_ffn_w_fcproj'][e].rearrange("(c p) n -> p c n", p=P)
                          ).then_inc(X['out_in'], 16)


def phase_experts_two(nc, a, k, scratch, K2, X):
    NJ = TOKENS // BLK
    w_fc, w_out, acc = X['w_fc'], X['w_out'], X['acc']
    with ExitStack() as stack:
        m = Machine(nc, stack, 'experts2')
        b_fc, b_out = m.sb('b_fc', [3 * E, F1], BF16), m.sb('b_out', [3 * E, D], BF16)
        rows = m.sb('moe_rows', [P, RING, D + 1])
        xT = m.sb('moe_xT', [P, 2, KD * P])
        hid = m.sb('moe_hidden', [P, 2, F1])
        hT = m.sb('moe_hiddenT', [P, KF * P])
        pick = m.sb('moe_pick', [3 * E, 2, P], BF16)
        x_ps = m.ps('moe_x_ps', [P, BANK])
        h_ps = [m.ps(f'moe_h_ps{i}', [P, 2 * BANK]) for i in range(2)]
        t_ps = m.ps('moe_t_ps', [P, 2 * BANK])
        o_ps = m.ps('moe_o_ps', [P, BANK])

        parts = {'b_fc': (hid[0:E, 0, :], b_fc, F1), 'b_out': (hid[0:E, 1, 0:D], b_out, D)}
        split = {'b_fc': m.sb('b_fc_parts', [E, 3, F1], BF16), 'b_out': m.sb('b_out_parts', [E, 3, D], BF16)}
        with nc.Block() as block:
            @block.sync
            def _(sync):
                sync.dma_start(hid[0:E, 0, :], a['L2_ffn_b_fc']).then_inc(m.sem('biases_in'), 16)
                sync.dma_start(hid[0:E, 1, 0:D], a['L2_ffn_b_fcproj']).then_inc(m.sem('biases_in'), 16)
                sync.wait_ge(m.sem('split'), 2)
                for name, (_, dst, _) in parts.items():
                    for j in range(3):
                        sync.dma_start(dst[j * E:(j + 1) * E, :], split[name][:, j, :]
                                       ).then_inc(m.sem('parts_placed'), 16)
                sync.wait_ge(m.sem('parts_placed'), 16 * 6)
                sync.wait_ge(X['fc_in'], 16 * E)
                sync.wait_ge(X['out_in'], 16 * E)

            @block.vector
            def _(v):
                v.memset(acc[:, :, :], 0.0)
                v.wait_ge(m.sem('biases_in'), 32)
                for i, (name, (src, _, _)) in enumerate(parts.items()):
                    split_three(v, m, i, src, [split[name][:, j, :] for j in range(3)])
        m.clear_all()

        with nc.Fori(0, NBLK // STEP) as g:
            with nc.Block() as block:
                @block.sync
                def _(sync):
                    for j in range(STEP):
                        if j >= RING:
                            sync.wait_ge(m.sem('added'), j - RING + 1)
                        sync.dma_start(rows[:, j % RING, :],
                                       scratch['moe_x2'][bass.ds((g * STEP + j) * BLK, BLK), :]
                                       ).then_inc(m.sem(f'rows_in{j % RING}'), 16)

                @block.tensor
                def _(pe):
                    def turn_x(j):
                        pe.wait_ge(m.sem(f'rows_in{j % RING}'), 16 * (j // RING + 1))
                        if j:
                            pe.wait_ge(m.sem('x_copied'), j)
                        for c in range(KD):
                            t = pe.transpose(x_ps[:, c * P:(c + 1) * P], rows[:, j % RING, c * P:(c + 1) * P],
                                             k['ident'][:, :])
                        t.then_inc(m.sem('x_turned'), 1)

                    def hidden(j):
                        e = pe.value_load(K2['expert'][0:1, bass.ds(g * STEP + j, 1)], min_val=0, max_val=E - 1)
                        pe.wait_ge(m.sem('x_copied'), j + 1)
                        pe.wait_ge(m.sem('picked'), j + 1)
                        if j >= 2:
                            pe.wait_ge(m.sem('activated'), j - 1)
                        for o in range(2):
                            out = h_ps[j % 2][:, o * BANK:(o + 1) * BANK]
                            pe.matmul(out, pick[:, j % 2, :], b_fc[:, o * BANK:(o + 1) * BANK],
                                      start=True, stop=False)
                            for c in range(KD):
                                mm = pe.matmul(out, xT[:, j % 2, c * P:(c + 1) * P],
                                               w_fc[:, bass.ds(e, 1), c, o * BANK:(o + 1) * BANK]
                                               .rearrange("p o n -> p (o n)"), start=False, stop=(c == KD - 1))
                        mm.then_inc(m.sem('hidden'), 1)
                        return e

                    def turn_hidden(j):
                        pe.wait_ge(m.sem('activated'), j + 1)
                        if j:
                            pe.wait_ge(m.sem('h_copied'), 2 * j)
                        for o in range(2):
                            for c in range(4 * o, 4 * o + 4):
                                t = pe.transpose(t_ps[:, c * P:(c + 1) * P], hid[:, j % 2, c * P:(c + 1) * P],
                                                 k['ident'][:, :])
                            t.then_inc(m.sem('h_turned'), 1)

                    def output(j, e):
                        if j:
                            pe.wait_ge(m.sem('added'), j)
                        pe.matmul(o_ps[:, 0:D], pick[:, j % 2, :], b_out[:, :], start=True, stop=False)
                        for c in range(KF):
                            if c % 4 == 0:
                                pe.wait_ge(m.sem('h_copied'), 2 * j + 1 + c // 4)
                            mm = pe.matmul(o_ps[:, 0:D], hT[:, c * P:(c + 1) * P],
                                           w_out[:, bass.ds(e, 1), c, :].rearrange("p o n -> p (o n)"),
                                           start=False, stop=(c == KF - 1))
                        mm.then_inc(m.sem('out'), 1)

                    turn_x(0)
                    e = hidden(0)
                    for j in range(STEP):
                        if j + 1 < STEP:
                            turn_x(j + 1)
                        turn_hidden(j)
                        after = hidden(j + 1) if j + 1 < STEP else None
                        output(j, e)
                        e = after

                @block.scalar
                def _(s):
                    for j in range(STEP):
                        s.wait_ge(m.sem('hidden'), j + 1)
                        if j >= 2:
                            s.wait_ge(m.sem('h_turned'), 2 * (j - 1))
                        s.activation(hid[:, j % 2, :], h_ps[j % 2][:, :], ACT.Gelu_apprx_tanh
                                     ).then_inc(m.sem('activated'), 1)

                @block.vector
                def _(v):
                    def copy_x(j):
                        if j >= 2:
                            v.wait_ge(m.sem('out'), j - 1)
                        v.tensor_copy(pick[:, j % 2, :],
                                      K2['one_hot'][:, bass.ds(g * STEP + j, 1)].broadcast_to([3 * E, P])
                                      ).then_inc(m.sem('picked'), 1)
                        v.wait_ge(m.sem('x_turned'), j + 1)
                        v.tensor_copy(xT[:, j % 2, :], x_ps[:, 0:KD * P]).then_inc(m.sem('x_copied'), 1)

                    def add(j):
                        row = v.value_load(K2['row'][0:1, bass.ds(g * STEP + j, 1)], min_val=0, max_val=NJ - 1)
                        v.wait_ge(m.sem('out'), j + 1)
                        if j:
                            v.wait_ge(m.sem('added'), j)
                        place = acc[:, bass.ds(row, 1), :].rearrange("p o n -> p (o n)")
                        v.scalar_tensor_tensor(place, o_ps[:, 0:D], rows[:, j % RING, D:D + 1], place,
                                               ALU.mult, ALU.add).then_inc(m.sem('added'), 1)

                    copy_x(0)
                    for j in range(STEP):
                        if j:
                            add(j - 1)
                        if j + 1 < STEP:
                            copy_x(j + 1)
                        for o in range(2):
                            v.wait_ge(m.sem('h_turned'), 2 * j + 1 + o)
                            v.tensor_copy(hT[:, o * BANK:(o + 1) * BANK], t_ps[:, o * BANK:(o + 1) * BANK]
                                          ).then_inc(m.sem('h_copied'), 1)
                    add(STEP - 1)
            m.clear_all()


def phase_combine_two(nc, k, scratch, acc):
    NJ = TOKENS // BLK
    with ExitStack() as stack:
        m = Machine(nc, stack, 'combine2')
        x2, res = m.sb('x2_rows', [P, NJ, D]), m.sb('res_rows', [P, NJ, D])
        parts, w = 4, NJ // 4
        by_rows = lambda ap, j: ap[j * w * P:(j + 1) * w * P, :].rearrange("(j p) d -> p j d", p=P)
        with nc.Block() as block:
            @block.sync
            def _(sync):
                for j in range(parts):
                    sync.dma_start(res[:, j * w:(j + 1) * w, :], by_rows(scratch['res2'], j)
                                   ).then_inc(m.sem(f'in{j}'), 16)
                    sync.dma_start(x2[:, j * w:(j + 1) * w, :], by_rows(scratch['x2'], j)
                                   ).then_inc(m.sem(f'in{j}'), 16)
                for j in range(parts):
                    sync.wait_ge(m.sem('combined'), j + 1)
                    sync.dma_start(by_rows(scratch['x3'], j), x2[:, j * w:(j + 1) * w, :]
                                   ).then_inc(m.sem('x3_out'), 16)
                sync.wait_ge(m.sem('x3_out'), 16 * parts)

            @block.vector
            def _(v):
                for j in range(parts):
                    s = slice(j * w, (j + 1) * w)
                    v.wait_ge(m.sem(f'in{j}'), 32)
                    v.tensor_tensor(res[:, s, :], res[:, s, :], acc[:, s, :], ALU.add).then_inc(m.sem('summed'), 1)
                    v.wait_ge(m.sem('summed'), j + 1)
                    v.scalar_tensor_tensor(x2[:, s, :], res[:, s, :], k['gate'][:, 6:7], x2[:, s, :], ALU.mult,
                                           ALU.add).then_inc(m.sem('combined'), 1)
        m.clear_all()



STORES3 = ('x_out', 'h_out', 'route_out')


def start3_sync(sync, h, a, k, W, L, scratch):
    yield
    for lane in h.lanes:
        b = h.batch(lane)
        if h.before is not None:
            for name in STORES3:
                sync.wait_ge(*h.before.landed(name, lane))
        sync.dma_start(L['x'][:, lane, :], scratch['x3'][bass.ds(b * T, T), :]).then_inc(h.sem(f'x_in{lane}'), 16)
        sync.dma_start(L['mid'][0:T, lane, 0:S_CTX].bitcast(I32),
                       a['mask_BxS2_ik1'][bass.ds(b, 1), :].broadcast_to([T, S_CTX])
                       ).then_inc(h.sem(f'mask_in{lane}'), 16)


def start3_tensor(pe, h, a, k, W, L, scratch):
    yield
    if h.before is not None:
        for lane in h.lanes:
            pe.wait_ge(*h.before.landed('ctx_in', lane))
            pe.wait_ge(*h.before.at('route_copied', 0, lane))
    turn_context(pe, h, k, L)
    yield
    for lane in h.lanes:
        pe.wait_ge(*h.at('ctx_copied', 0, lane))
    turn_rows(pe, h, k, L, 0, pick(L, 'xh'), after(h, 'norm_out', 0))


def start3_scalar(s, h, a, k, W, L, scratch):
    yield
    copy_context(s, h, L)
    yield
    copy_t(s, h, L, 0, pick(L, 'hT'), after(h, 'turned', 0), 'turned_copied')


def start3_gpsimd(gp, h, a, k, W, L, scratch):
    yield
    for lane in h.lanes:
        gp.wait_ge(*h.landed('mask_in', lane))
        gp.tensor_scalar(L['mask'][:, lane, :], L['mid'][0:T, lane, 0:S_CTX].bitcast(I32), 0.0,
                         MINUS_BIG, ALU.is_equal, ALU.mult).then_inc(h.sem('mask_ready'), 1)
    yield
    norm_rstd(gp, h, L, 0, k['minus_half'][0:T, 0:1])


def start3_vector(v, h, a, k, W, L, scratch):
    yield
    norm_stats(v, h, L, 0, pick(L, 'x'), lambda lane: h.landed('x_in', lane))
    yield
    norm_apply(v, h, L, 0, pick(L, 'x'), pick(L, 'xh'))


def keys3_tensor(pe, h, a, k, W, L, scratch):
    yield
    if h.before is not None:
        for lane in h.lanes:
            pe.wait_ge(*h.before.at('turned_copied', 0, lane))
    for lane in h.lanes:
        for o in range(KD):
            for c in range(KD):
                mm = pe.matmul(L['ps'][lane][:, o * T:(o + 1) * T], W['WqT3'][:, c, o * P:(o + 1) * P],
                               L['hT'][:, lane, c * T:(c + 1) * T], start=(c == 0), stop=(c == KD - 1))
        mm.then_inc(h.sem('q3_raw'), 1)
    yield
    for lane in h.lanes:
        pe.wait_ge(*h.at('q3', 0, lane))
        for o in range(KD):
            for c in range(KD):
                pe.matmul(L['ps'][lane][:, BANK + o * T:BANK + (o + 1) * T],
                          W['Wk3'][:, c, o * P:(o + 1) * P], L['qT'][:, lane, c * T:(c + 1) * T],
                          start=(c == 0), stop=(c == KD - 1))
        for c in range(KD):
            mm = pe.matmul(L['ps'][lane][0:T, BANK + KD * T:BANK + KD * T + 1],
                           L['qT'][:, lane, c * T:(c + 1) * T], W['bk3'][:, c:c + 1],
                           start=(c == 0), stop=(c == KD - 1))
        mm.then_inc(h.sem('key_q3'), 1)
    yield
    attention_scores(pe, h, L, 0, pick(L, 'hT'), after(h, 'key_q3_copied'))


def keys3_scalar(s, h, a, k, W, L, scratch):
    yield
    copy_t(s, h, L, 0, pick(L, 'qT'), after(h, 'q3_raw'), 'q3', scale=W['qscale'], bias=W['bq3s'])
    yield
    for lane in h.lanes:
        s.wait_ge(*h.at('key_q3', 0, lane))
        s.activation(L['hT'][:, lane, :], L['ps'][lane][:, BANK:BANK + KD * T], ACT.Copy)
        s.activation(L['row'][:, lane, :], L['ps'][lane][0:T, BANK + KD * T:BANK + KD * T + 1],
                     ACT.Copy).then_inc(h.sem('key_q3_copied'), 1)


def probs3_vector(v, h, a, k, W, L, scratch):
    yield
    for lane in h.lanes:
        if h.before is not None:
            v.wait_ge(*h.before.at('scores', 0, lane))
            v.wait_ge(*h.before.at('key_q3_copied', 0, lane))
            if h.before.before is not None:
                v.wait_ge(*h.before.before.at('mask_ready', 0, lane))
        v.scalar_tensor_tensor(L['wide'][0:T, lane, 0:S_CTX], L['ps'][lane][0:T, BANK:BANK + S_CTX],
                               L['row'][:, lane, 0:1], L['mask'][:, lane, :], ALU.add,
                               ALU.add).then_inc(h.sem('logits'), 1)
    for lane in h.lanes:
        v.wait_ge(*h.at('logits', 0, lane))
        v.tensor_reduce(L['nmax'][:, lane, 0:1], L['wide'][0:T, lane, 0:S_CTX], AX.X, ALU.max,
                        negate=True).then_inc(h.sem('row_max'), 1)
    yield
    attention_norm(v, h, L, 0)


def probs3_tensor(pe, h, a, k, W, L, scratch):
    yield
    turn_probs(pe, h, k, L, 0, after(h, 'probs_normed', 0))
    yield
    attend_t(pe, h, L, 0)


def probs3_scalar(s, h, a, k, W, L, scratch):
    yield
    attention_exp(s, h, L, 0)
    yield
    copy_probs(s, h, L, 0)
    yield
    copy_t(s, h, L, 1, pick(L, 'qT'), after(h, 'attended', 0), 'attended_copied')


def out3_sync(sync, h, a, k, W, L, scratch):
    yield
    for lane in h.lanes:
        if h.before is not None:
            sync.wait_ge(*h.before.at('attended', 0, lane))
        sync.dma_start(L['ctx'][:, lane, :, :],
                       a['ctx_1024'][bass.ds((h.batch(lane) + LANES) % B, 1), :, :]
                       .rearrange("o (c p) d -> p (o c) d", p=SC)).then_inc(h.sem(f'ctx_in{lane}'), 16)
    for ready, name, place, offset, tile in (('x_updated', 'x_out', 'x4', 0, 'x'),
                                             ('norm_out', 'h_out', 'moe_y3', E * CAP, 'u'),
                                             ('route_copied', 'route_out', 'route3', 0, 'logit')):
        yield
        for lane in h.lanes:
            sync.wait_ge(*h.at(ready, 0, lane))
            sync.dma_start(scratch[place][bass.ds(h.batch(lane) * T + offset, T), :], L[tile][:, lane, :]
                           ).then_inc(h.sem(f'{name}{lane}'), 16)


def out3_tensor(pe, h, a, k, W, L, scratch):
    yield
    for lane in h.lanes:
        if h.before is not None:
            pe.wait_ge(*h.before.at('attended_copied', 0, lane))
        rows_out(pe, L, lane, W['WvT3'], L['qT'][:, lane, :], KD, 0, D, W['bv3'][:, :], k['ones16']
                 ).then_inc(h.sem('v3'), 1)
    yield
    turn_rows(pe, h, k, L, 0, pick(L, 'u'), after(h, 'norm_out', 0))
    yield
    for lane in h.lanes:
        pe.wait_ge(*h.at('turned_copied', 0, lane))
        rows_out(pe, L, lane, W['Wr'], L['hT'][:, lane, :], KD, 1, E).then_inc(h.sem('route'), 1)


def out3_scalar(s, h, a, k, W, L, scratch):
    yield
    copy_t(s, h, L, 0, pick(L, 'hT'), after(h, 'turned', 0), 'turned_copied')


def out3_gpsimd(gp, h, a, k, W, L, scratch):
    yield
    norm_rstd(gp, h, L, 0, k['minus_half'][0:T, 0:1])


def out3_vector(v, h, a, k, W, L, scratch):
    yield
    for lane in h.lanes:
        v.wait_ge(*h.at('v3', 0, lane))
        v.scalar_tensor_tensor(L['x'][:, lane, :], L['ps'][lane][0:T, 0:D], k['gate'][0:T, 3:4],
                               L['x'][:, lane, :], ALU.mult, ALU.add).then_inc(h.sem('x_updated'), 1)
    yield
    norm_stats(v, h, L, 0, pick(L, 'x'), after(h, 'x_updated', 0))
    yield
    norm_apply(v, h, L, 0, pick(L, 'x'), pick(L, 'u'))
    yield
    for lane in h.lanes:
        v.wait_ge(*h.at('route', 0, lane))
        v.tensor_copy(L['logit'][:, lane, :], L['ps'][lane][0:T, BANK:BANK + E]
                      ).then_inc(h.sem('route_copied'), 1)


FOURTH_PROGRAMS = {
    'start3': {'sync': start3_sync, 'tensor': start3_tensor, 'scalar': start3_scalar,
               'gpsimd': start3_gpsimd, 'vector': start3_vector},
    'keys3': {'tensor': keys3_tensor, 'scalar': keys3_scalar},
    'probs3': {'tensor': probs3_tensor, 'scalar': probs3_scalar, 'vector': probs3_vector},
    'out3': {'sync': out3_sync, 'tensor': out3_tensor, 'scalar': out3_scalar, 'gpsimd': out3_gpsimd,
             'vector': out3_vector},
}
FOURTH_PERIOD = 834
FOURTH_TIMES = {
    'start3': {
        'sync': (0,),
        'tensor': (277, 849),
        'scalar': (363, 888),
        'gpsimd': (473, 577),
        'vector': (512, 750),
    },
    'keys3': {
        'tensor': (191, 387, 723),
        'scalar': (296, 536),
    },
    'probs3': {
        'tensor': (358, 551),
        'scalar': (209, 436, 700),
        'vector': (93, 274),
    },
    'out3': {
        'sync': (225, 256, 525, 763),
        'tensor': (93, 532, 680),
        'scalar': (571,),
        'gpsimd': (403,),
        'vector': (210, 339, 479, 743),
    },
}
FOURTH_CHAIN = Chain(FOURTH_PROGRAMS, {}, FOURTH_TIMES, FOURTH_PERIOD, STORES3 + ('ctx_in',))


def phase_four(nc, a, k, scratch):
    with ExitStack() as stack:
        m = Machine(nc, stack, 'four')
        W = {}
        for name, cols in [('WqT3', D), ('Wk3', D), ('WvT3', D), ('Wr', E)]:
            W[name] = m.sb(name, [P, KD, cols])
        for name in ('bq3', 'bq3s', 'bk3', 'qscale'):
            W[name] = m.sb(name, [P, KD])
        W['bv3'] = m.sb('bv3', [3, D], BF16)
        bv3_row, bv3_parts = m.sb('bv3_row', [1, D]), m.sb('bv3_parts', [1, 3, D], BF16)
        L = lane_buffers(m, [('x', T, [D]), ('xh', T, [D]), ('u', T, [D]), ('hT', P, [KD * T]),
                             ('qT', P, [KD * T]), ('ctx', SC, [NSC, D]), ('ctxT', P, [KD, S_CTX]),
                             ('mask', T, [S_CTX]), ('wide', P, [2 * 384]), ('mid', P, [384]),
                             ('stats', T, [12]), ('mv', T, [2]), ('var', T, [1]), ('rstd', T, [1]),
                             ('nmax', T, [1]), ('sum', T, [1]), ('rsum', T, [1]), ('factor', T, [1]),
                             ('row', T, [1]), ('logit', T, [E])])

        with nc.Block() as block:
            @block.sync
            def _(sync):
                load_context(sync, m, L, a['ctx_1024'], 0, 'out3_ctx_in')
                for name, src in (('WqT3', 'WqT3'), ('Wk3', 'L3_xattn_Wk'), ('WvT3', 'WvT3'), ('Wr', 'L3_ffn_Wr')):
                    sync.dma_start(W[name][:, :, :], a[src].rearrange("(c p) n -> p c n", p=P)
                                   ).then_inc(m.sem('w_in'), 16)
                with nc.allow_non_contiguous_dma(reason="a few hundred bias values, once"):
                    for name, src in (('bq3', 'L3_xattn_bq'), ('bk3', 'L3_xattn_bk')):
                        sync.dma_start(W[name][:, :], a[src].rearrange("(c p) -> p c", p=P)
                                       ).then_inc(m.sem('w_in'), 16)
                sync.dma_start(bv3_row[:, :], a['L3_xattn_bv'].partition_broadcast(1)).then_inc(m.sem('w_in'), 16)
                sync.wait_ge(m.sem('w_in'), 16 * 7)
                sync.wait_ge(m.sem('split'), 1)
                for j in range(3):
                    sync.dma_start(W['bv3'][j:j + 1, :], bv3_parts[:, j, :]).then_inc(m.sem('parts_placed'), 16)
                sync.wait_ge(m.sem('parts_placed'), 48)
                for lane in range(LANES):
                    sync.wait_ge(m.sem(f'out3_ctx_in{lane}'), 16)

            @block.vector
            def _(v):
                v.memset(W['qscale'][:, :], D ** -0.5)
                v.wait_ge(m.sem('w_in'), 16 * 7)
                v.tensor_scalar(W['bq3s'][:, :], W['bq3'][:, :], D ** -0.5, None, ALU.mult)
                split_three(v, m, 0, bv3_row[:, :], [bv3_parts[:, j, :] for j in range(3)])
        m.clear_all()

        run_chain(nc, m, FOURTH_CHAIN, 2 * LANES, a, k, W, L, scratch)



def phase_route_three(nc, a, k, scratch, K3):
    def finish(v, m, R):
        step = [0]

        def done(ins):
            step[0] += 1
            ins.then_inc(m.sem('steps'), 1)
            v.wait_ge(m.sem('steps'), step[0])
        done(v.tensor_tensor(R['slot'][:, :, :], R['ranks'][0:T, 0:B * E].rearrange("p (b e) -> p b e", e=E),
                             R['before'][:, :, :].rearrange("p e b -> p b e"), ALU.add))
        slots_of(v, m, R, k, 0, 1)
        done(v.tensor_scalar(R['slot0'][:, :], R['slot0'][:, :], -1.0, None, ALU.add))
        done(v.tensor_scalar(R['kept'][:, :], R['slot0'][:, :], float(CAP), None, ALU.is_lt))
        done(v.tensor_scalar(R['slot1'][:, :], R['prio_max'][:, :], -float(CAP), float(E * CAP), ALU.mult, ALU.add))
        done(v.tensor_tensor(R['slot0'][:, :], R['slot0'][:, :], R['slot1'][:, :], ALU.add))
        done(v.tensor_scalar(R['own'][:, :], R['iota'][:, 0:B], float(T), float(E * CAP), ALU.mult, ALU.add))
        done(v.tensor_scalar(R['own'][:, :], R['own'][:, :], R['part'][:, 0:1], None, ALU.add))
        done(v.tensor_tensor(R['slot0'][:, :], R['slot0'][:, :], R['own'][:, :], ALU.subtract))
        done(v.tensor_tensor(R['slot0'][:, :], R['slot0'][:, :], R['kept'][:, :], ALU.mult))
        done(v.tensor_tensor(R['slot0'][:, :], R['slot0'][:, :], R['own'][:, :], ALU.add))
        v.tensor_copy(K3['slot'][:, 0, :], R['slot0'][:, :])
        done(v.tensor_tensor(R['pm0'][:, :], R['pm0'][:, :], R['kept'][:, :], ALU.mult))
        done(v.tensor_scalar(R['kept'][:, :], R['kept'][:, :], -1.0, 1.0, ALU.mult, ALU.add))
        done(v.tensor_tensor(R['pm0'][:, :], R['pm0'][:, :], R['kept'][:, :], ALU.add))
        v.tensor_scalar(K3['factor'][:, :], R['pm0'][:, :], k['gate'][0:T, 7:8], None, ALU.mult)

    extra = lambda m, R: R.update(kept=m.sb('route_kept', [T, B]), own=m.sb('route_own', [T, B]))
    route_block(nc, a, k, scratch, 'route3', 1, finish, extra)


TILES = CAP // T
PARTS = ((0, 3), (3, 5))
assert TILES * T == CAP and TILES == 5


def phase_experts_three(nc, a, k, scratch):
    with ExitStack() as stack:
        m = Machine(nc, stack, 'experts3')
        w1 = [m.sb(f'w1_{i}', [P, KD, F1]) for i in range(2)]
        w2 = [m.sb(f'w2_{i}', [P, KF, D]) for i in range(2)]
        rows = m.sb('rows3', [T, 2, TILES, D])
        xT = m.sb('xT3', [P, 2, KD, CAP])
        hT = m.sb('hT3', [P, 2, KF, CAP])
        y = m.sb('y3', [T, 2, TILES, D])
        x_ps = [m.ps(f'x3_ps{i}', [P, BANK]) for i in range(2)]
        h_ps = [m.ps(f'h3_ps{i}', [P, BANK]) for i in range(4)]
        o_ps = [m.ps(f'o3_ps{i}', [P, BANK]) for i in range(2)]

        def load_rows(sync, i, e):
            sync.dma_start(rows[:, i, :, :], scratch['moe_x3'][bass.ds(e * CAP, CAP), :]
                           .rearrange("(j t) d -> t j d", t=T)).then_inc(m.sem(f'rows_in{i}'), 16)

        def load_w1(sync, i, e):
            sync.dma_start(w1[i][:, :, :], a['L3_ffn_W1'][bass.ds(e, 1), :, :]
                           .rearrange("o (c p) n -> p (o c) n", p=P)).then_inc(m.sem(f'w1_in{i}'), 16)

        def load_w2(sync, i, e):
            sync.dma_start(w2[i][:, :, :], a['L3_ffn_W2'][bass.ds(e, 1), :, :]
                           .rearrange("o (c p) n -> p (o c) n", p=P)).then_inc(m.sem(f'w2_in{i}'), 16)

        loaded = [f'{name}{i}' for name in ('rows_in', 'w1_in', 'w2_in') for i in range(2)]
        with nc.Block() as block:
            @block.sync
            def _(sync):
                for i in range(2):
                    for load in (load_rows, load_w1, load_w2):
                        load(sync, i, i)
                for name in loaded:
                    sync.wait_ge(m.sem(name), 16)
        m.clear_all()

        def pair(g, more):
            with nc.Block() as block:
                @block.sync
                def _(sync):
                    for i in range(2):
                        if more:
                            sync.wait_ge(m.sem('x_turned'), 2 * KD * (i + 1))
                            load_rows(sync, i, g * 2 + i + 2)
                            sync.wait_ge(m.sem('hidden'), 2 * KF * (i + 1))
                            load_w1(sync, i, g * 2 + i + 2)
                            sync.wait_ge(m.sem('out_done'), TILES * (i + 1))
                            load_w2(sync, i, g * 2 + i + 2)
                        sync.wait_ge(m.sem('y_copied'), TILES * (i + 1))
                        sync.dma_start(scratch['moe_y3'][bass.ds((g * 2 + i) * CAP, CAP), :]
                                       .rearrange("(j t) d -> t j d", t=T), y[:, i, :, :]).then_inc(m.sem(f'y_out{i}'), 16)
                    for name in (loaded if more else []) + ['y_out0', 'y_out1']:
                        sync.wait_ge(m.sem(name), 16)

                @block.tensor
                def _(pe):
                    def turn(i):
                        for q, (t0, t1) in enumerate(PARTS):
                            for c in range(KD):
                                use = (i * 2 + q) * KD + c
                                if use >= 2:
                                    pe.wait_ge(m.sem('x_copied'), use - 1)
                                for t in range(t0, t1):
                                    tr = pe.transpose(x_ps[use % 2][:, (t - t0) * T:(t - t0 + 1) * T],
                                                      rows[:, i, t, c * P:(c + 1) * P], k['ident'][0:T, 0:T])
                                tr.then_inc(m.sem('x_turned'), 1)

                    def hidden(i):
                        for q, (t0, t1) in enumerate(PARTS):
                            pe.wait_ge(m.sem('x_copied'), (i * 2 + q + 1) * KD)
                            for f in range(KF):
                                use = (i * 2 + q) * KF + f
                                if use >= 4:
                                    pe.wait_ge(m.sem('h_copied'), use - 3)
                                for c in range(KD):
                                    mm = pe.matmul(h_ps[use % 4][:, 0:(t1 - t0) * T], w1[i][:, c, f * P:(f + 1) * P],
                                                   xT[:, i, c, t0 * T:t1 * T], start=(c == 0), stop=(c == KD - 1))
                                mm.then_inc(m.sem('hidden'), 1)

                    def output(i):
                        for t in range(TILES):
                            use = i * TILES + t
                            pe.wait_ge(m.sem('h_copied'), (i * 2 + (1 if t < PARTS[0][1] else 2)) * KF)
                            if use >= 2:
                                pe.wait_ge(m.sem('y_copied'), use - 1)
                            for f in range(KF):
                                mm = pe.matmul(o_ps[use % 2][0:T, 0:D], hT[:, i, f, t * T:(t + 1) * T],
                                               w2[i][:, f, :], start=(f == 0), stop=(f == KF - 1))
                            mm.then_inc(m.sem('out_done'), 1)

                    turn(0)
                    hidden(0)
                    turn(1)
                    output(0)
                    hidden(1)
                    output(1)

                @block.scalar
                def _(s):
                    for i in range(2):
                        for q, (t0, t1) in enumerate(PARTS):
                            for f in range(KF):
                                use = (i * 2 + q) * KF + f
                                s.wait_ge(m.sem('hidden'), use + 1)
                                s.activation(hT[:, i, f, t0 * T:t1 * T], h_ps[use % 4][:, 0:(t1 - t0) * T], ACT.Relu
                                             ).then_inc(m.sem('h_copied'), 1)

                @block.vector
                def _(v):
                    def copy_x(i):
                        for q, (t0, t1) in enumerate(PARTS):
                            for c in range(KD):
                                use = (i * 2 + q) * KD + c
                                v.wait_ge(m.sem('x_turned'), use + 1)
                                v.tensor_copy(xT[:, i, c, t0 * T:t1 * T], x_ps[use % 2][:, 0:(t1 - t0) * T]
                                              ).then_inc(m.sem('x_copied'), 1)

                    copy_x(0)
                    copy_x(1)
                    for use in range(2 * TILES):
                        v.wait_ge(m.sem('out_done'), use + 1)
                        v.tensor_copy(y[:, use // TILES, use % TILES, :], o_ps[use % 2][0:T, 0:D]
                                      ).then_inc(m.sem('y_copied'), 1)
            m.clear_all()

        with nc.Fori(0, E // 2 - 1) as g:
            pair(g, True)
        pair(E // 2 - 1, False)


def phase_gather(nc, k, scratch, K3, out):
    with ExitStack() as stack:
        m = Machine(nc, stack, 'gather')
        gathered = Machine(nc, stack, 'gathered')
        x = m.sb('last_x', [T, AT_ONCE, D])
        y = m.sb('last_y', [T, AT_ONCE, D])
        index = m.sb('last_index', [T, AT_ONCE], U32)
        factor = m.sb('last_factor', [T, AT_ONCE])
        with nc.Fori(0, B // AT_ONCE) as g:
            with nc.Block() as block:
                @block.sync
                def _(sync):
                    for i in range(AT_ONCE):
                        sync.dma_start(x[:, i, :], scratch['x4'][bass.ds((g * AT_ONCE + i) * T, T), :]
                                       ).then_inc(m.sem(f'x_in{i}'), 16)
                    for i in range(AT_ONCE):
                        sync.wait_ge(m.sem('final'), i + 1)
                        sync.dma_start(out[bass.ds(g * AT_ONCE + i, 1), :, :].rearrange("o t d -> (o t) d"),
                                       x[:, i, :]).then_inc(m.sem('stored'), 16)
                    sync.wait_ge(m.sem('stored'), 16 * AT_ONCE)

                @block.vector
                def _(v):
                    v.tensor_copy(factor[:, :], K3['factor'][:, bass.ds(g * AT_ONCE, AT_ONCE)])
                    v.tensor_copy(index[:, :], K3['slot'][:, 0, bass.ds(g * AT_ONCE, AT_ONCE)]).then_inc(m.sem('indexed'), 1)
                    v.wait_ge(m.sem('indexed'), 1)
                    for i in range(AT_ONCE):
                        v.wait_ge(m.sem(f'x_in{i}'), 16)
                        v.wait_ge(gathered.sem(f'batch{i}'), (g + 1) * 16)
                        v.scalar_tensor_tensor(x[:, i, :], y[:, i, :], factor[:, i:i + 1], x[:, i, :],
                                               ALU.mult, ALU.add).then_inc(m.sem('final'), 1)

                @block.gpsimd
                def _(gp):
                    gp.wait_ge(m.sem('indexed'), 1)
                    for i in range(AT_ONCE):
                        gp.indirect_dma_start(y[:, i, :], None, scratch['moe_y3'],
                                              bass.IndirectOffsetOnAxis(ap=index[:, i:i + 1], axis=0)
                                              ).then_inc(gathered.sem(f'batch{i}'), 16)
            m.clear_all()


def later_phases(nc, a, k, scratch, out):
    with ExitStack() as stack:
        m = Machine(nc, stack, 'keep2')
        K2 = {'slot': m.sb('slot2', [T, 2, B]), 'weight': m.sb('weight2', [T, 2, B]),
              'expert': m.sb('expert2', [1, NBLK], I32), 'row': m.sb('row2', [1, NBLK], I32),
              'one_hot': m.sb('one_hot2', [3 * E, NBLK])}
        X = {'acc': m.sb('moe_acc', [P, TOKENS // BLK, D])}
        with ExitStack() as inner:
            w = Machine(nc, inner, 'weights2')
            X.update(w_fc=w.sb('w_fc', [P, E, KD, F1]), w_out=w.sb('w_out', [P, E, KF, D]),
                     fc_in=w.sem('fc_in'), out_in=w.sem('out_in'))
            phase_route_two(nc, a, k, scratch, K2, lambda sync, s: load_experts_two(sync, s, a, X))
            phase_scatter(nc, k, scratch, scratch['moe_in'], scratch['moe_x2'], K2['slot'], K2['weight'], 2)
            phase_experts_two(nc, a, k, scratch, K2, X)
            w.clear_all()
        phase_combine_two(nc, k, scratch, X['acc'])
    phase_four(nc, a, k, scratch)
    with ExitStack() as stack:
        m = Machine(nc, stack, 'keep3')
        K3 = {'slot': m.sb('slot3', [T, 1, B]), 'factor': m.sb('factor3', [T, B])}
        phase_route_three(nc, a, k, scratch, K3)
        phase_scatter(nc, k, scratch, scratch['moe_y3'][E * CAP:, :], scratch['moe_x3'], K3['slot'], None, 1)
        phase_experts_three(nc, a, k, scratch)
        phase_gather(nc, k, scratch, K3, out)



def build(nc, a, out):
    scratch = {}
    for name, shape in (('turned', [B, D, T]), ('x2', [TOKENS, D]), ('res2', [TOKENS, D]),
                        ('moe_in', [TOKENS, D]), ('route2', [TOKENS, E]),
                        ('moe_x2', [NBLK * BLK, D + 1]), ('x3', [TOKENS, D]), ('x4', [TOKENS, D]),
                        ('route3', [TOKENS, E]), ('moe_x3', [E * CAP + TOKENS, D]),
                        ('moe_y3', [E * CAP + TOKENS, D])):
        scratch[name] = nc.dram_tensor('scratch_' + name, shape, F32).ap()
    with ExitStack() as stack:
        m = Machine(nc, stack, 'all')
        k = {'ident': m.sb('ident', [P, P]), 'tri': m.sb('tri', [P, P]), 'ones': m.sb('ones', [P, P]),
             'ident16': m.sb('ident16', [P, P], BF16), 'ones16': m.sb('ones16', [3, P], BF16),
             'minus_half': m.sb('minus_half', [P, LANES]), 'gate': m.sb('gate', [P, 8]),
             'g_xattn': a['g_xattn'], 'g_ffn': a['g_ffn']}
        pool = Machine(nc, stack, 'pool')
        k['pool_dma'] = {name: pool.sem(name) for name in ['scattered1', 'scattered2']}
        k['zeros'], k['zeroed'] = m.sb('zeros', [P, D + 1]), pool.sem('zeroed')
        make_constants(nc, m, k)
        phase_one(nc, a, k, scratch)
        later_phases(nc, a, k, scratch, out)


_TURNED = {'w_gateT': 'L0_ffn_w_gate', 'w_upT': 'L0_ffn_w_up', 'w_downT': 'L0_ffn_w_down',
           'WkT1': 'L1_xattn_Wk', 'w1T': 'L1_ffn_w1', 'w2T': 'L1_ffn_w2', 'WT2': 'L2_xattn_W',
           'WqT3': 'L3_xattn_Wq', 'WvT3': 'L3_xattn_Wv'}


def kernel(**inputs):
    import numpy as np
    import concourse.bacc as bacc
    from concourse import mybir as mb
    from concourse.bass_utils import run_bass_kernel_spmd as run
    nc = bacc.Bacc("TRN2", target_bir_lowering=False, num_devices=1)
    host = {name: v for name, v in inputs.items() if name not in _TURNED.values()}
    for name, src in _TURNED.items():
        host[name] = np.asarray(inputs[src]).T
    arrays, args = {}, {}
    for name, v in host.items():
        v = np.ascontiguousarray(v)
        arrays[f"in_{name}_dram"] = v
        args[name] = nc.dram_tensor(f"in_{name}_dram", v.shape, mb.dt.from_np(v.dtype),
                                    kind="ExternalInput").ap()
    out = nc.dram_tensor("out_0_dram", (B, T, D), mb.dt.from_np(np.dtype('float32')),
                         kind="ExternalOutput").ap()
    build(nc, args, out)
    r = run(nc, [arrays], core_ids=[0])
    return r.results[0]["out_0_dram"]
```
